# Optimizing a Trainium2 kernel written in Bass

```python
import numpy as np
import jax
import jax.numpy as jnp

def _softmax(x, axis=-1):
    return jax.nn.softmax(x, axis=axis)

def _gelu(x):
    return jax.nn.gelu(x, approximate=True)

def _silu(x):
    return jax.nn.silu(x)

def _sigmoid(x):
    return jax.nn.sigmoid(x)

def _layernorm(x, axis=-1, eps=1e-05):
    m = jnp.mean(x, axis=axis, keepdims=True)
    v = jnp.var(x, axis=axis, keepdims=True)
    return (x - m) / jnp.sqrt(v + eps)

def _scatter_add(tgt, idx, src, axis=0):
    return tgt.at[idx].add(src)

def _segment_sum(src, seg, n):
    return jax.ops.segment_sum(src, seg, n)
kernel_name = 'mk_flamingo_gated_d2_seqx_r8_74b1d4'

def setup_inputs(seed: int=0):
    np.random.seed(seed)
    _w = jnp.asarray

    def _rec_inputs():
        import jax
        import jax.numpy as jnp
        _rk = jax.random.key(seed)
        x = -0.000125 + 0.9999 * jax.random.normal(jax.random.fold_in(_rk, 1), (4, 256, 256), jnp.float32)
        _lenS = 256 - jax.random.randint(jax.random.fold_in(_rk, 7), (4,), 0, max(1, 256 // 4) + 1, jnp.int32)
        _lenS2 = 256 - jax.random.randint(jax.random.fold_in(_rk, 8), (4,), 0, max(1, 256 // 4) + 1, jnp.int32)
        itok_BxS_13_99985 = jax.random.randint(jax.random.fold_in(_rk, 11), (4, 256), 13, 99986, jnp.int32)
        _ctx_2048P = jax.random.normal(jax.random.fold_in(_rk, 12), (4, 16, 256), jnp.float32)
        _ctx_2048c = jax.random.dirichlet(jax.random.fold_in(_rk, 512), 0.3 * jnp.ones((16,), jnp.float32), (4, 256))
        _ctx_2048t = jnp.einsum('bsk,bkd->bsd', _ctx_2048c, _ctx_2048P)
        _ctx_2048t = _ctx_2048t * jax.lax.rsqrt(jnp.mean(jnp.square(_ctx_2048t)) + 1e-12) * 0.953939
        ctx_2048 = 6.82029e-06 + 0.0200006 * (_ctx_2048t + 0.3 * jax.random.normal(jax.random.fold_in(_rk, 612), (4, 256, 256), jnp.float32))
        _g = jax.random.normal(jax.random.fold_in(_rk, 9001), (2, 2), jnp.float32)
        _g = jnp.sign(_g) * jnp.maximum(jnp.abs(_g), 1.0) + (_g == 0) * 1.0
        g_xattn = _g[0]
        g_ffn = _g[1]
        return (x, itok_BxS_13_99985, ctx_2048, g_xattn, g_ffn)
    x, itok_BxS_13_99985, ctx_2048, g_xattn, g_ffn = _rec_inputs()

    def _L0_xattn_setup():
        import jax, jax.numpy as jnp
        import numpy as np
        B, S, D = (4, 512, 256)
        E = 4
        F = 1024 // E
        VOCAB = 12500
        key = jax.random.key(seed)
        k1, k2, k3, k4, k5 = jax.random.split(key, 5)
        hidden_states = jax.random.normal(k1, (B, S, D), dtype=jnp.float32)
        token_ids = jax.random.randint(k2, (B, S), 0, VOCAB, dtype=jnp.int64)
        Wg = jax.random.normal(k3, (E, F, D), dtype=jnp.float32) * 0.02
        Wu = jax.random.normal(k4, (E, F, D), dtype=jnp.float32) * 0.02
        Wd = jax.random.normal(k5, (E, D, F), dtype=jnp.float32) * 0.02
        return {'hidden_states': hidden_states, 'token_ids': token_ids, 'Wg': Wg, 'Wu': Wu, 'Wd': Wd}
    _L0_xattn_all = _L0_xattn_setup()
    _L0_xattn_in = {k: v for k, v in _L0_xattn_all.items() if k in ()}
    del _L0_xattn_all

    def _L0_ffn_setup():
        import jax, jax.numpy as jnp
        import numpy as np
        ACT_BITS = 8
        EPS = 1e-05

        def act_quant(x, bits=ACT_BITS):
            qb = float(2 ** (bits - 1))
            scale = qb / jnp.clip(jnp.max(jnp.abs(x), axis=-1, keepdims=True), EPS)
            xq = jnp.clip(jnp.round(x * scale), -qb, qb - 1) / scale
            return x + jax.lax.stop_gradient(xq - x)

        def weight_quant(w):
            scale = 1.0 / jnp.clip(jnp.mean(jnp.abs(w)), EPS)
            wq = jnp.clip(jnp.round(w * scale), -1.0, 1.0) / scale
            return w + jax.lax.stop_gradient(wq - w)

        def fwht(x):
            shape = x.shape
            n = shape[-1]
            x = x.reshape(-1, n)
            h = 1
            while h < n:
                x = x.reshape(-1, n // (2 * h), 2, h)
                a, b = (x[..., 0, :], x[..., 1, :])
                x = jnp.stack([a + b, a - b], axis=-2).reshape(-1, n)
                h *= 2
            return (x * (1.0 / np.sqrt(n)).astype(np.float32)).reshape(shape)

        def bitlinear(x, w):
            return jnp.einsum('bsh,oh->bso', act_quant(x), weight_quant(w))

        def h_bitlinear(x, w):
            return jnp.einsum('bsh,oh->bso', act_quant(fwht(x)), weight_quant(w))
        key = jax.random.key(seed)
        k1, k2, k3, k4 = jax.random.split(key, 4)
        H, I = (256, 1024)
        B, S = (4, 256)
        std_in = 1.0 / np.sqrt(H)
        std_mid = 1.0 / np.sqrt(I)
        return {'x': jax.random.normal(k1, (B, S, H), dtype=jnp.float32), 'w_gate': jax.random.normal(k2, (I, H), dtype=jnp.float32) * std_in, 'w_up': jax.random.normal(k3, (I, H), dtype=jnp.float32) * std_in, 'w_down': jax.random.normal(k4, (H, I), dtype=jnp.float32) * std_mid}
    _L0_ffn_all = _L0_ffn_setup()
    _L0_ffn_in = {k: v for k, v in _L0_ffn_all.items() if k in ('w_gate', 'w_up', 'w_down')}
    del _L0_ffn_all

    def _L1_xattn_setup():
        import jax, jax.numpy as jnp
        import numpy as np
        B, S, D = (8, 128, 256)
        H, HD = (16, 128)
        key = jax.random.key(seed)
        ks = jax.random.split(key, 6)
        fan_in = 1.0 / np.sqrt(D)
        return {'inputs_q': jax.random.normal(ks[0], (B, S, D), jnp.float32), 'inputs_kv': jax.random.normal(ks[1], (B, S, D), jnp.float32), 'Wq': jax.random.normal(ks[2], (D, H * HD), jnp.float32) * fan_in, 'Wk': jax.random.normal(ks[3], (D, H * HD), jnp.float32) * fan_in, 'Wv': jax.random.normal(ks[4], (D, H * HD), jnp.float32) * fan_in, 'Wo': jax.random.normal(ks[5], (H * HD, D), jnp.float32) * (1.0 / np.sqrt(H * HD))}
    _L1_xattn_all = _L1_xattn_setup()
    _L1_xattn_in = {k: v for k, v in _L1_xattn_all.items() if k in ('Wq', 'Wk', 'Wv', 'Wo')}
    del _L1_xattn_all

    def _L1_ffn_setup():
        import jax, jax.numpy as jnp
        import numpy as np
        H, LAT, INTER, E, G, TOPK_G, TOP_K = (256, 128, 128, 32, 4, 2, 8)
        SHARED_INTER = 512
        ROUTED_SCALE = 2.5
        B, S = (2, 128)

        def relu2(x):
            return jnp.square(jax.nn.relu(x))
        key = jax.random.key(seed)
        ks = jax.random.split(key, 9)
        w = 0.02
        return {'hidden_states': jax.random.normal(ks[0], (B, S, H), jnp.float32), 'gate_w': jax.random.normal(ks[1], (E, H), jnp.float32) * w, 'gate_bias': jax.random.normal(ks[2], (E,), jnp.float32) * w, 'fc1_w': jax.random.normal(ks[3], (LAT, H), jnp.float32) * w, 'fc2_w': jax.random.normal(ks[4], (H, LAT), jnp.float32) * w, 'w1': jax.random.normal(ks[5], (E, INTER, LAT), jnp.float32) * w, 'w2': jax.random.normal(ks[6], (E, LAT, INTER), jnp.float32) * w, 'shared_up_w': jax.random.normal(ks[7], (SHARED_INTER, H), jnp.float32) * w, 'shared_down_w': jax.random.normal(ks[8], (H, SHARED_INTER), jnp.float32) * w}
    _L1_ffn_all = _L1_ffn_setup()
    _L1_ffn_in = {k: v for k, v in _L1_ffn_all.items() if k in ('gate_w', 'gate_bias', 'fc1_w', 'fc2_w', 'w1', 'w2', 'shared_up_w', 'shared_down_w')}
    del _L1_ffn_all
    return {'x': x, 'itok_BxS_13_99985': itok_BxS_13_99985, 'ctx_2048': ctx_2048, 'g_xattn': g_xattn, 'g_ffn': g_ffn, 'L0_ffn_w_gate': _L0_ffn_in['w_gate'], 'L0_ffn_w_up': _L0_ffn_in['w_up'], 'L0_ffn_w_down': _L0_ffn_in['w_down'], 'L1_xattn_Wq': _L1_xattn_in['Wq'], 'L1_xattn_Wk': _L1_xattn_in['Wk'], 'L1_xattn_Wv': _L1_xattn_in['Wv'], 'L1_xattn_Wo': _L1_xattn_in['Wo'], 'L1_ffn_gate_w': _L1_ffn_in['gate_w'], 'L1_ffn_gate_bias': _L1_ffn_in['gate_bias'], 'L1_ffn_fc1_w': _L1_ffn_in['fc1_w'], 'L1_ffn_fc2_w': _L1_ffn_in['fc2_w'], 'L1_ffn_w1': _L1_ffn_in['w1'], 'L1_ffn_w2': _L1_ffn_in['w2'], 'L1_ffn_shared_up_w': _L1_ffn_in['shared_up_w'], 'L1_ffn_shared_down_w': _L1_ffn_in['shared_down_w']}

def reference(x, itok_BxS_13_99985, ctx_2048, g_xattn, g_ffn, L0_ffn_w_gate, L0_ffn_w_up, L0_ffn_w_down, L1_xattn_Wq, L1_xattn_Wk, L1_xattn_Wv, L1_xattn_Wo, L1_ffn_gate_w, L1_ffn_gate_bias, L1_ffn_fc1_w, L1_ffn_fc2_w, L1_ffn_w1, L1_ffn_w2, L1_ffn_shared_up_w, L1_ffn_shared_down_w):
    import jax
    import jax.numpy as jnp

    def _L0_xattn_ref(hidden_states, token_ids, Wg, Wu, Wd):
        import jax, jax.numpy as jnp
        import numpy as np
        B, S, D = (4, 512, 256)
        E = 4
        F = 1024 // E
        VOCAB = 12500
        tokens_per_expert = VOCAB // E
        tid = jnp.clip(token_ids, 0, VOCAB - 1)
        expert_ids = jnp.minimum(tid // tokens_per_expert, E - 1)
        out = jnp.zeros_like(hidden_states)
        for e in range(E):
            g = jax.nn.silu(jnp.einsum('bsd,fd->bsf', hidden_states, Wg[e]))
            u = jnp.einsum('bsd,fd->bsf', hidden_states, Wu[e])
            y = jnp.einsum('bsf,df->bsd', g * u, Wd[e])
            out = jnp.where((expert_ids == e)[..., None], y, out)
        return out

    def _L0_ffn_ref(x, w_gate, w_up, w_down):
        import jax, jax.numpy as jnp
        import numpy as np
        ACT_BITS = 8
        EPS = 1e-05

        def act_quant(x, bits=ACT_BITS):
            qb = float(2 ** (bits - 1))
            scale = qb / jnp.clip(jnp.max(jnp.abs(x), axis=-1, keepdims=True), EPS)
            xq = jnp.clip(jnp.round(x * scale), -qb, qb - 1) / scale
            return x + jax.lax.stop_gradient(xq - x)

        def weight_quant(w):
            scale = 1.0 / jnp.clip(jnp.mean(jnp.abs(w)), EPS)
            wq = jnp.clip(jnp.round(w * scale), -1.0, 1.0) / scale
            return w + jax.lax.stop_gradient(wq - w)

        def fwht(x):
            shape = x.shape
            n = shape[-1]
            x = x.reshape(-1, n)
            h = 1
            while h < n:
                x = x.reshape(-1, n // (2 * h), 2, h)
                a, b = (x[..., 0, :], x[..., 1, :])
                x = jnp.stack([a + b, a - b], axis=-2).reshape(-1, n)
                h *= 2
            return (x * (1.0 / np.sqrt(n)).astype(np.float32)).reshape(shape)

        def bitlinear(x, w):
            return jnp.einsum('bsh,oh->bso', act_quant(x), weight_quant(w))

        def h_bitlinear(x, w):
            return jnp.einsum('bsh,oh->bso', act_quant(fwht(x)), weight_quant(w))
        gate = bitlinear(x, w_gate)
        up = bitlinear(x, w_up)
        intermediate = jax.nn.silu(gate) * up
        return h_bitlinear(intermediate, w_down)

    def _L1_xattn_ref(inputs_q, inputs_kv, Wq, Wk, Wv, Wo):
        import jax, jax.numpy as jnp
        import numpy as np
        B, S, D = (8, 128, 256)
        H, HD = (16, 128)
        b, sq, _ = inputs_q.shape
        skv = inputs_kv.shape[1]
        q = (inputs_q @ Wq).reshape(b, sq, H, HD) * (1.0 / np.sqrt(HD))
        k = (inputs_kv @ Wk).reshape(b, skv, H, HD)
        v = (inputs_kv @ Wv).reshape(b, skv, H, HD)
        scores = jnp.einsum('bqhd,bkhd->bhqk', q, k)
        attn = jax.nn.softmax(scores, axis=-1)
        ctx = jnp.einsum('bhqk,bkhd->bqhd', attn, v).reshape(b, sq, H * HD)
        return ctx @ Wo

    def _L1_ffn_ref(hidden_states, gate_w, gate_bias, fc1_w, fc2_w, w1, w2, shared_up_w, shared_down_w):
        import jax, jax.numpy as jnp
        import numpy as np
        H, LAT, INTER, E, G, TOPK_G, TOP_K = (256, 128, 128, 32, 4, 2, 8)
        SHARED_INTER = 512
        ROUTED_SCALE = 2.5
        B, S = (2, 128)

        def relu2(x):
            return jnp.square(jax.nn.relu(x))
        orig_shape = hidden_states.shape
        x = hidden_states.reshape(-1, H)
        T = x.shape[0]
        logits = jnp.einsum('th,eh->te', x.astype(jnp.float32), gate_w)
        scores = jax.nn.sigmoid(logits)
        sb = scores + gate_bias
        grp = sb.reshape(T, G, E // G)
        group_scores = jax.lax.top_k(grp, 2)[0].sum(-1)
        _, gidx = jax.lax.top_k(group_scores, TOPK_G)
        gmask = jax.nn.one_hot(gidx, G, dtype=sb.dtype).sum(1)
        masked = jnp.where(gmask[:, :, None] > 0, grp, -jnp.inf).reshape(T, E)
        _, topi = jax.lax.top_k(masked, TOP_K)
        wsel = jnp.take_along_axis(scores, topi, axis=1)
        wsel = wsel / wsel.sum(-1, keepdims=True) * ROUTED_SCALE
        cw = jnp.zeros((T, E), jnp.float32).at[jnp.arange(T)[:, None], topi].add(wsel)
        x_lat = x @ fc1_w.T
        h = relu2(jnp.einsum('tl,eil->eti', x_lat, w1))
        h = h * cw.T[:, :, None]
        y_lat = jnp.einsum('eti,eli->tl', h, w2)
        routed = y_lat @ fc2_w.T
        shared = relu2(x @ shared_up_w.T) @ shared_down_w.T
        return (shared + routed).reshape(orig_shape)
    x = x + jnp.tanh(g_xattn[0]) * _L0_xattn_ref(_layernorm(x, axis=-1), itok_BxS_13_99985, ctx_2048, ctx_2048, ctx_2048)
    x = x + jnp.tanh(g_ffn[0]) * _L0_ffn_ref(_layernorm(x, axis=-1), L0_ffn_w_gate, L0_ffn_w_up, L0_ffn_w_down)
    x = x + jnp.tanh(g_xattn[1]) * _L1_xattn_ref(_layernorm(x, axis=-1), ctx_2048, L1_xattn_Wq, L1_xattn_Wk, L1_xattn_Wv, L1_xattn_Wo)
    x = x + jnp.tanh(g_ffn[1]) * _L1_ffn_ref(_layernorm(x, axis=-1), L1_ffn_gate_w, L1_ffn_gate_bias, L1_ffn_fc1_w, L1_ffn_fc2_w, L1_ffn_w1, L1_ffn_w2, L1_ffn_shared_up_w, L1_ffn_shared_down_w)
    return x

_drawn_inputs = setup_inputs


def setup_inputs(seed=0):
    import zlib

    import numpy as np

    out = dict(_drawn_inputs(seed))
    spreads = {'g_ffn': (-1.0, 0.6)}
    factors = {'L1_xattn_Wq': 8.0,
     'L1_xattn_Wk': 8.0,
     'L1_xattn_Wv': 5.703,
     'L1_xattn_Wo': 5.786,
     'L1_ffn_gate_w': 8.0,
     'L1_ffn_gate_bias': 8.0,
     'L1_ffn_fc1_w': 8.0,
     'L1_ffn_fc2_w': 8.0,
     'L1_ffn_w1': 8.0,
     'L1_ffn_w2': 8.0,
     'L1_ffn_shared_up_w': 8.0,
     'L1_ffn_shared_down_w': 8.0}
    for name, (base, spread) in spreads.items():
        noise = np.random.default_rng([zlib.crc32(name.encode()), seed]).standard_normal(out[name].shape)
        drawn = base * np.exp(spread * noise) if base else spread * noise
        out[name] = jnp.asarray(drawn.astype(out[name].dtype))
    for name, factor in factors.items():
        out[name] = (out[name] * factor).astype(out[name].dtype)
    return out
```

```python
import concourse.bass as bass
from concourse import mybir
from contextlib import ExitStack


def flamingo_two_layer_kernel(nc, x, ids, ctx_t, g_xattn, g_ffn, w_gate_t, w_up_t, w_down_t,
                              w_qkv, w_o, gate_w_t, gate_bias, fc1_t, fc2_t, w1_t, w2_t,
                              shared_up_t, shared_down_t, consts, cw_scratch, out, batches):
    F32, F32R, BF16, I32 = mybir.dt.float32, mybir.dt.float32r, mybir.dt.bfloat16, mybir.dt.int32
    ALU, ACT, AX = mybir.AluOpType, mybir.ActivationFunctionType, mybir.AxisListType

    P = 128
    T, D = x.shape
    NB = batches
    S = T // NB
    NT = T // P
    DC = D // P
    NG = 2
    GN = NT // NG
    GT = T // NG
    INTER = w_gate_t.shape[1]
    IC = INTER // P
    NH = w_qkv.shape[0]
    E = gate_w_t.shape[1]
    NGRP, TOPG, TOPK = 4, 2, 8
    EG = E // NGRP
    SI = shared_up_t.shape[1]
    SC = SI // P
    LN_EPS, Q_EPS = 1e-5, 1e-5
    ROUTED_SCALE = 2.5
    TOK_PER_EXPERT = 12500 // NB
    ROUND = 12582912.0
    RSQRT_GUESS = float(0x5F3759DF - 2**31)
    QK_SCALE = float(P) ** -0.5
    W_COUNT = float(INTER * D)

    ctx = ExitStack()
    with ctx:
        def sb(name, shape, dt=F32, where=None):
            return (where or ctx).enter_context(nc.sbuf_tensor(name, shape, dt))

        def sem(name):
            return ctx.enter_context(nc.semaphore(name))

        xr = sb("xr", [P, NT, D])
        h = sb("h", [P, NT, D])
        hT_hi = sb("hT_hi", [P, DC, T], F32R)
        hT_lo = sb("hT_lo", [P, DC, T], F32R)
        cT_hi = sb("cT_hi", [P, DC, NB * S], F32R)
        cT_lo = sb("cT_lo", [P, DC, NB * S], F32R)
        cst = sb("cst", [P, 2, P])
        ident, had = cst[:, 0, :], cst[:, 1, :]
        ones = sb("ones", [P, P])
        zeros = sb("zeros", [P, 512], F32R)
        gl = sb("gl", [P, 4])
        tg = sb("tg", [P, 4])
        st = sb("st", [P, NT, 6])
        mv = sb("mv", [P, NT, 2])
        ln_v = sb("ln_v", [P, NT])
        ln_y = sb("ln_y", [P, NT])
        ln_t = sb("ln_t", [P, NT])
        ln_i = sb("ln_i", [P, NT], I32)
        wqkv_raw = [sb(f"wqkv_raw{i}", [P, 3, DC, P]) for i in range(2)]
        wqkv_hi = [sb(f"wqkv_hi{i}", [P, 3, DC, P], F32R) for i in range(2)]
        wqkv_lo = [sb(f"wqkv_lo{i}", [P, 3, DC, P], F32R) for i in range(2)]
        wo_raw = [sb(f"wo_raw{i}", [P, D]) for i in range(2)]
        wo_hi = [sb(f"wo_hi{i}", [P, D], F32R) for i in range(2)]
        wo_lo = [sb(f"wo_lo{i}", [P, D], F32R) for i in range(2)]
        fc1_raw = sb("fc1_raw", [P, DC, P])
        fc1_hi = sb("fc1_hi", [P, DC, P], F32R)
        fc1_lo = sb("fc1_lo", [P, DC, P], F32R)
        fc2 = sb("fc2", [P, D])
        gw_raw = sb("gw_raw", [P, DC, E])
        gw_hi = sb("gw_hi", [P, DC, E], F32R)
        gw_lo = sb("gw_lo", [P, DC, E], F32R)
        gbias = sb("gbias", [P, E])

        region = ExitStack()
        cT_raw = sb("cT_raw", [P, DC, NB * S], F32, region)
        wq8 = [sb(f"wq8_{i}", [P, 2 * INTER], BF16, region) for i in range(3)]
        ids_row = sb("ids_row", [P, T], I32, region)
        ids_col = sb("ids_col", [P, NT], I32, region)
        ge_row = sb("ge_row", [P, NB - 1, T], I32, region)
        ge_col = sb("ge_col", [P, NB - 1, NT], F32, region)
        tgm = sb("tgm", [P, NB, NT], F32, region)
        wraw = [sb(f"wraw{i}", [P, 2 * INTER], F32, region) for i in range(3)]
        inner_a = sb("inner_a", [P, IC, GT], F32, region)
        wsum = sb("wsum", [P, 3], F32, region)
        wmean = sb("wmean", [P, 3], F32, region)
        wscale = sb("wscale", [P, 3], F32, region)
        fdown = sb("fdown", [P, 1], F32, region)
        am = sb("am", [P, NT], F32, region)
        am_r = sb("am_r", [P, NT], F32, region)
        am_c = sb("am_c", [P, NT], F32, region)
        c_up = sb("c_up", [P, NT], F32, region)
        qtok = sb("qtok", [P, GN, D], F32, region)
        diag = sb("diag", [P, GN, P], F32, region)
        qT = sb("qT", [P, DC, GT], BF16, region)
        sB = sb("sB", [P, GT], F32, region)
        gate_s = sb("gate_s", [P, 2, GT], F32, region)
        gate_silu = sb("gate_silu", [P, 2, GT], F32, region)
        am2 = sb("am2", [P, 2, 4], F32, region)
        part = ExitStack()
        a_sel = sb("a_sel", [P, NG, DC, GT], F32, part)
        z_hi = sb("z_hi", [P, NG, DC, GT], F32R, part)
        z_lo = sb("z_lo", [P, NG, DC, GT], F32R, part)
        a_silu = sb("a_silu", [P, DC, GT], F32, part)
        part.close()
        part = ExitStack()
        inner_b = sb("inner_b", [P, IC, GT], F32, part)
        q2 = sb("q2", [P, 2, INTER], F32, part)
        q2T = sb("q2T", [P, 2, IC, P], BF16, part)
        part.close()
        region.close()

        region = ExitStack()
        qT_hi = [sb(f"qT_hi{i}", [P, T], F32R, region) for i in range(2)]
        qT_lo = [sb(f"qT_lo{i}", [P, T], F32R, region) for i in range(2)]
        kT_hi = [sb(f"kT_hi{i}", [P, T], F32R, region) for i in range(2)]
        kT_lo = [sb(f"kT_lo{i}", [P, T], F32R, region) for i in range(2)]
        v_hi = [sb(f"v_hi{i}", [P, NT, P], F32R, region) for i in range(2)]
        v_lo = [sb(f"v_lo{i}", [P, NT, P], F32R, region) for i in range(2)]
        probs = sb("probs", [P, NB, 2, S], F32, region)
        pT_hi = sb("pT_hi", [P, NB, 2, S], F32R, region)
        pT_lo = sb("pT_lo", [P, NB, 2, S], F32R, region)
        oT_hi = sb("oT_hi", [P, T], F32R, region)
        oT_lo = sb("oT_lo", [P, T], F32R, region)
        nmax = sb("nmax", [P, NB, 2], F32, region)
        esum = sb("esum", [P, NB, 2], F32, region)
        rsum = sb("rsum", [P, NB, 2], F32, region)
        region.close()

        region = ExitStack()
        su_raw = sb("su_raw", [P, DC, SI], F32, region)
        su_hi = sb("su_hi", [P, DC, SI], F32R, region)
        su_lo = sb("su_lo", [P, DC, SI], F32R, region)
        sd = sb("sd", [P, SC, D], F32, region)
        s_relu = sb("s_relu", [P, 2, GT], F32, region)
        s_act = sb("s_act", [P, SC, T], F32, region)
        xl_hi = sb("xl_hi", [P, T], F32R, region)
        xl_lo = sb("xl_lo", [P, T], F32R, region)
        sc = sb("sc", [P, NT, E], F32, region)
        sbias = sb("sbias", [P, NT, E], F32, region)
        gtop = sb("gtop", [P, NT * NGRP, 8], F32, region)
        gscore = sb("gscore", [P, NT, NGRP], F32, region)
        before = sb("before", [P, NGRP, NGRP], F32, region)
        cmp = sb("cmp", [P, NT, NGRP, NGRP], F32, region)
        eqs = sb("eqs", [P, NT, NGRP, NGRP], F32, region)
        grank = sb("grank", [P, NT, NGRP], F32, region)
        gmask = sb("gmask", [P, NT, NGRP], I32, region)
        gmask8 = sb("gmask8", [P, NT, E], I32, region)
        masked = sb("masked", [P, NT, E], F32, region)
        top8 = sb("top8", [P, NT, 8], F32, region)
        left = sb("left", [P, NT, E], F32, region)
        sel = sb("sel", [P, NT, E], F32, region)
        wsel = sb("wsel", [P, NT, E], F32, region)
        wden = sb("wden", [P, NT], F32, region)
        cw = sb("cw", [P, NT, E], F32, region)
        cwT = sb("cwT", [P, NG * P], F32, region)
        cw_row = [sb(f"cw_row{i}", [P, T], F32, region) for i in range(4)]
        w1_raw = [sb(f"w1_raw{i}", [P, 2, P], F32, region) for i in range(2)]
        w1_hi = [sb(f"w1_hi{i}", [P, 2, P], F32R, region) for i in range(2)]
        w1_lo = [sb(f"w1_lo{i}", [P, 2, P], F32R, region) for i in range(2)]
        w2 = [sb(f"w2_{i}", [P, 2, P], F32, region) for i in range(2)]
        e_relu = [sb(f"e_relu{i}", [P, T], F32, region) for i in range(2)]
        e_wa = [sb(f"e_wa{i}", [P, T], F32, region) for i in range(2)]
        e_z = [sb(f"e_z{i}", [P, T], F32, region) for i in range(2)]
        yl = sb("yl", [P, T], F32, region)
        region.close()

        ps = ctx.enter_context(nc.psum_tensor("ps", [P, 8, 512], F32))

        ld_const, ld_ids, ld_ctx, ld_gates = sem("ld_const"), sem("ld_ids"), sem("ld_ctx"), sem("ld_gates")
        ld_x = [sem(f"ld_x{g}") for g in range(NG)]
        ld_w = [sem(f"ld_w{i}") for i in range(3)]
        ld_small = sem("ld_small")
        ld_qkv = [sem(f"ld_qkv{i}") for i in range(2)]
        ld_wo = [sem(f"ld_wo{i}") for i in range(2)]
        ld_shared = sem("ld_shared")
        ld_w1 = [sem(f"ld_w1_{i}") for i in range(2)]
        ld_w2 = [sem(f"ld_w2_{i}") for i in range(2)]
        ld_cw = [sem(f"ld_cw{i}") for i in range(4)]
        cw_stored, out_stored = sem("cw_stored"), sem("out_stored")
        dve_step, pool_step = sem("dve_step"), sem("pool_step")
        set_up, h_ready, hT_filled, hT_hi_done, hT_done = (
            sem("set_up"), sem("h_ready"), sem("hT_filled"), sem("hT_hi_done"), sem("hT_done"))
        tanh_done, masks_ready = sem("tanh_done"), sem("masks_ready")
        ctx_hi_done, ctx_done = sem("ctx_hi_done"), sem("ctx_done")
        a_filled, a_first_copied, a_taken = sem("a_filled"), sem("a_first_copied"), sem("a_taken")
        a_silu_done, z_ready, z_hi_done, z_done = sem("a_silu_done"), sem("z_ready"), sem("z_hi_done"), sem("z_done")
        y0_filled, y0_taken = sem("y0_filled"), sem("y0_taken")
        wsum_done, wtot_filled, wscale_done, w_ternary = (
            sem("wsum_done"), sem("wtot_filled"), sem("wscale_done"), sem("w_ternary"))
        q1_ready, q1T_filled, q1T_done = sem("q1_ready"), sem("q1T_filled"), sem("q1T_done")
        diag_ready, sB_filled, sB_done = sem("diag_ready"), sem("sB_filled"), sem("sB_done")
        gu_filled, gs_done, silu_done, gu_taken = sem("gu_filled"), sem("gs_done"), sem("silu_done"), sem("gu_taken")
        fly_sum, fly_diff = sem("fly_sum"), sem("fly_diff")
        had_filled, s2_ready, q2_done, q2_clipped = sem("had_filled"), sem("s2_ready"), sem("q2_done"), sem("q2_clipped")
        q2T_filled, q2T_done, y1_filled, y1_taken = sem("q2T_filled"), sem("q2T_done"), sem("y1_filled"), sem("y1_taken")
        small_split = sem("small_split")
        qkv_split, wo_split = sem("qkv_split"), sem("wo_split")
        unit_filled, hi_done, lo_done = sem("unit_filled"), sem("hi_done"), sem("lo_done")
        max_done, exp_done, rsum_done, probs_done = sem("max_done"), sem("exp_done"), sem("rsum_done"), sem("probs_done")
        y2_cleared, y2_part, y2_filled, y2_taken = sem("y2_cleared"), sem("y2_part"), sem("y2_filled"), sem("y2_taken")
        su_hi_done, su_split = sem("su_hi_done"), sem("su_split")
        logit_filled, sc_done = sem("logit_filled"), sem("sc_done")
        xl_filled, xl_hi_done, xl_done = sem("xl_filled"), sem("xl_hi_done"), sem("xl_done")
        su_filled, su_relu, su_taken = sem("su_filled"), sem("su_relu"), sem("su_taken")
        y3_filled, y3_taken = sem("y3_filled"), sem("y3_taken")
        cw_ready, cwT_filled, cwT_done = sem("cw_ready"), sem("cwT_filled"), sem("cwT_done")
        w1_split = sem("w1_split")
        up_filled, relu_done, wa_done, e_z_done, down_done = (
            sem("up_filled"), sem("relu_done"), sem("wa_done"), sem("e_z_done"), sem("down_done"))
        yl_done, y4_filled, y4_taken = sem("yl_done"), sem("y4_filled"), sem("y4_taken")

        block = ctx.enter_context(nc.Block())

        STEP = ["S0", "Q0", "S1", "Q1", "S2", "K0", "S3", "T0",
                "K1", "T1", "V0", "T2", "V1", "T3", "O0", "O1"]
        FIRST = ["K0", "K1", "V0", "V1", "Q0", "Q1"]
        LAST = [u for u in STEP if u[0] not in "QKV"]
        SPLIT = [u for u in STEP if u[0] != "S"]
        SPLIT_LAST = [u for u in LAST if u[0] != "S"]
        BANK = {u: p % 4 for p, u in enumerate(STEP)}
        FIRST_BANK = {u: p % 4 for p, u in enumerate(FIRST)}

        def filled(i, u, units=STEP):
            return len(FIRST) + len(STEP) * i + units.index(u) + 1

        def split(i, u, units=SPLIT):
            return len(FIRST) + len(SPLIT) * i + units.index(u) + 1

        Y3_BANK = [0, 1, 3, 4]

        @block.sync
        def _(sp):
            sp.dma_start(xr[:, 0:GN, :], x[0:GT, :].rearrange("(n p) d -> p n d", p=P)).then_inc(ld_x[0], 16)
            sp.dma_start(cst[:, :, :], consts).then_inc(ld_const, 16)
            sp.dma_start(cT_raw[:, :, :], ctx_t.rearrange("(c p) n -> p c n", p=P)).then_inc(ld_ctx, 16)
            sp.dma_start(xr[:, GN:NT, :], x[GT:T, :].rearrange("(n p) d -> p n d", p=P)).then_inc(ld_x[1], 16)
            sp.dma_start(ids_row[:, :], ids.rearrange("(a t) -> a t", a=1).broadcast_to([P, T])).then_inc(ld_ids, 16)
            sp.dma_start(ids_col[:, :], ids.rearrange("(n p) -> p n", p=P),
                         allow_slow_non_contiguous=True).then_inc(ld_ids, 16)
            sp.dma_start(gl[:, 0:2], g_xattn.rearrange("(a t) -> a t", a=1).broadcast_to([P, 2])).then_inc(ld_gates, 16)
            sp.dma_start(gl[:, 2:4], g_ffn.rearrange("(a t) -> a t", a=1).broadcast_to([P, 2])).then_inc(ld_gates, 16)
            for i, (w, c) in enumerate(((w_gate_t, DC), (w_up_t, DC), (w_down_t, IC))):
                sp.dma_start(wraw[i][:, :].rearrange("p (c n) -> p c n", c=c),
                             w.rearrange("(c p) n -> p c n", p=P)).then_inc(ld_w[i], 16)
            for i in range(2):
                sp.dma_start(wqkv_raw[i][:, :, :, :], w_qkv[i]).then_inc(ld_qkv[i], 16)
                sp.dma_start(wo_raw[i][:, :], w_o[i]).then_inc(ld_wo[i], 16)
            sp.dma_start(fc1_raw[:, :, :], fc1_t.rearrange("(c p) n -> p c n", p=P)).then_inc(ld_small, 16)
            sp.dma_start(gw_raw[:, :, :], gate_w_t.rearrange("(c p) n -> p c n", p=P)).then_inc(ld_small, 16)
            sp.dma_start(fc2[:, :], fc2_t).then_inc(ld_small, 16)
            sp.dma_start(gbias[:, :], gate_bias.rearrange("(a t) -> a t", a=1).broadcast_to([P, E])).then_inc(ld_small, 16)
            with sp.Fori(0, NH // 2 - 1) as i:
                for b in range(2):
                    sp.wait_ge(qkv_split, i * 2 + b + 1)
                    sp.dma_start(wqkv_raw[b][:, :, :, :], w_qkv[i * 2 + (b + 2)]).then_inc(ld_qkv[b], 16)
                    sp.wait_ge(wo_split, i * 2 + b + 1)
                    sp.dma_start(wo_raw[b][:, :], w_o[i * 2 + (b + 2)]).then_inc(ld_wo[b], 16)
            sp.wait_ge(y2_filled, 4)
            sp.dma_start(su_raw[:, :, :], shared_up_t.rearrange("(c p) n -> p c n", p=P)).then_inc(ld_shared, 16)
            sp.dma_start(sd[:, :, :], shared_down_t.rearrange("(c p) n -> p c n", p=P)).then_inc(ld_shared, 16)
            for i in range(2):
                sp.dma_start(w1_raw[i][:, :, :], w1_t[2 * i:2 * i + 2].rearrange("e p n -> p e n")).then_inc(ld_w1[i], 16)
                sp.dma_start(w2[i][:, :, :], w2_t[2 * i:2 * i + 2].rearrange("e p n -> p e n")).then_inc(ld_w2[i], 16)
            sp.wait_ge(cwT_done, 1)
            for n in range(NT):
                sp.dma_start(cw_scratch[:, n * P:(n + 1) * P],
                             cwT[(n % GN) * E:(n % GN + 1) * E, (n // GN) * P:(n // GN + 1) * P]).then_inc(cw_stored, 16)
            sp.wait_ge(cw_stored, 16 * NT)
            for j in range(4):
                sp.dma_start(cw_row[j][:, :], cw_scratch[j:j + 1, :].broadcast_to([P, T])).then_inc(ld_cw[j], 16)
            with sp.Fori(0, E // 4 - 1) as i:
                for j in range(4):
                    sp.wait_ge(wa_done, i * 4 + j + 1)
                    sp.dma_start(cw_row[j][:, :], cw_scratch[bass.ds(i * 4 + (j + 4), 1), :].broadcast_to([P, T])).then_inc(ld_cw[j], 16)
                    if j % 2:
                        b = j // 2
                        sp.wait_ge(w1_split, i * 2 + b + 1)
                        sp.dma_start(w1_raw[b][:, :, :], w1_t[bass.ds(i * 4 + (2 * b + 4), 2)].rearrange("e p n -> p e n")).then_inc(ld_w1[b], 16)
                        sp.wait_ge(down_done, i * 4 + j + 1)
                        sp.dma_start(w2[b][:, :, :], w2_t[bass.ds(i * 4 + (2 * b + 4), 2)].rearrange("e p n -> p e n")).then_inc(ld_w2[b], 16)
            for g in range(NG):
                sp.wait_ge(y4_taken, GN * (g + 1))
                sp.dma_start(out[g * GT:(g + 1) * GT, :].rearrange("(n p) d -> p n d", p=P),
                             xr[:, g * GN:(g + 1) * GN, :]).then_inc(out_stored, 16)
            sp.wait_ge(out_stored, 16 * NG)

        @block.gpsimd
        def _(pool):
            steps = [0]

            def own(ins):
                steps[0] += 1
                ins.then_inc(pool_step, 1)
                pool.wait_ge(pool_step, steps[0])

            nc.gpsimd.memset(ones[:, :], 1.0).then_inc(set_up, 1)
            nc.gpsimd.memset(zeros[:, :].bitcast(F32), 0.0).then_inc(set_up, 1)

            def high(dst, src):
                return nc.gpsimd.tensor_tensor(dst, src, zeros[:, 0:1].bitcast(F32).to_broadcast([P, src.shape[1]]), ALU.add)

            for i in range(3):
                pool.wait_ge(wscale_done, 1)
                own(nc.gpsimd.tensor_scalar(wraw[i][:, :], wraw[i][:, :], wscale[:, i:i + 1], ROUND, ALU.mult, ALU.add))
                own(nc.gpsimd.tensor_scalar(wraw[i][:, :], wraw[i][:, :], ROUND + 1.0, ROUND - 1.0, ALU.min, ALU.max))
                nc.gpsimd.tensor_scalar(wq8[i][:, :], wraw[i][:, :], -ROUND, 1.0, ALU.add, ALU.mult).then_inc(w_ternary, 1)

            for b in range(2):
                pool.wait_ge(ld_qkv[b], 16)
                own(nc.gpsimd.tensor_copy(wqkv_hi[b][:, :, :, :], wqkv_raw[b][:, :, :, :]))
                nc.gpsimd.tensor_tensor(wqkv_lo[b][:, :, :, :], wqkv_raw[b][:, :, :, :],
                                        wqkv_hi[b][:, :, :, :].bitcast(F32), ALU.subtract).then_inc(qkv_split, 1)
            pool.wait_ge(ld_wo[0], 16)
            own(nc.gpsimd.tensor_copy(wo_hi[0][:, :], wo_raw[0][:, :]))
            nc.gpsimd.tensor_tensor(wo_lo[0][:, :], wo_raw[0][:, :], wo_hi[0][:, :].bitcast(F32), ALU.subtract).then_inc(wo_split, 1)
            pool.wait_ge(ld_small, 64)
            nc.gpsimd.tensor_copy(gw_hi[:, :, :], gw_raw[:, :, :])
            own(nc.gpsimd.tensor_copy(fc1_hi[:, :, :], fc1_raw[:, :, :]))
            nc.gpsimd.tensor_tensor(gw_lo[:, :, :], gw_raw[:, :, :], gw_hi[:, :, :].bitcast(F32), ALU.subtract)
            nc.gpsimd.tensor_tensor(fc1_lo[:, :, :], fc1_raw[:, :, :], fc1_hi[:, :, :].bitcast(F32), ALU.subtract).then_inc(small_split, 1)

            def fly_diffs(g):
                for lvl, (src, dst) in enumerate(((inner_a, inner_b), (inner_b, inner_a), (inner_a, inner_b))):
                    hh = IC // 2 >> lvl
                    s = src[:, :, :].rearrange("p (a two c) t -> p a two c t", two=2, c=hh)
                    d = dst[:, :, :].rearrange("p (a two c) t -> p a two c t", two=2, c=hh)
                    if lvl == 0:
                        pool.wait_ge(gu_taken, IC * (g + 1))
                        if g:
                            pool.wait_ge(had_filled, GN * g)
                    else:
                        pool.wait_ge(fly_sum, 3 * g + lvl)
                        pool.wait_ge(fly_diff, 3 * g + lvl)
                    nc.gpsimd.tensor_tensor(d[:, :, 1], s[:, :, 0], s[:, :, 1], ALU.subtract).then_inc(fly_diff, 1)

            def clip_q2(g):
                for j in range(GN):
                    n = g * GN + j
                    pool.wait_ge(q2_done, n + 1)
                    nc.gpsimd.tensor_scalar(q2[:, j % 2, :], q2[:, j % 2, :], ROUND + 127.0, ROUND - 128.0,
                                            ALU.min, ALU.max).then_inc(q2_clipped, 1)

            fly_diffs(0)
            clip_q2(0)
            fly_diffs(1)
            clip_q2(1)

            def attend(i):
                for b in range(NB):
                    pool.wait_ge(rsum_done, i * NB + b + 1)
                    nc.gpsimd.tensor_tensor(probs[:, b, :, :], probs[:, b, :, :],
                                            rsum[:, b, :].unsqueeze(2).to_broadcast([P, 2, S]), ALU.mult).then_inc(probs_done, 1)

            def split_weights(par, half, qkv, count):
                if qkv:
                    pool.wait_ge(ld_qkv[par], half * 16 + 32)
                    high(wqkv_hi[par][:, :, :, :].rearrange("p w c n -> p (w c n)"), wqkv_raw[par][:, :, :, :].rearrange("p w c n -> p (w c n)")).then_inc(pool_step, 1)
                q = 1 - par
                pool.wait_ge(ld_wo[q], half * 16 + 16 if par == 0 else half * 16 + 32)
                high(wo_hi[q][:, :], wo_raw[q][:, :]).then_inc(pool_step, 1)
                pool.wait_ge(pool_step, count)
                if qkv:
                    nc.gpsimd.tensor_tensor(wqkv_lo[par][:, :, :, :], wqkv_raw[par][:, :, :, :],
                                            wqkv_hi[par][:, :, :, :].bitcast(F32), ALU.subtract).then_inc(qkv_split, 1)
                nc.gpsimd.tensor_tensor(wo_lo[q][:, :], wo_raw[q][:, :], wo_hi[q][:, :].bitcast(F32),
                                        ALU.subtract).then_inc(wo_split, 1)

            base = steps[0]
            with pool.Fori(0, NH // 2 - 1) as i:
                for par in range(2):
                    attend(i * 2 + par)
                    split_weights(par, i, True, i * 4 + (base + 2 * par + 2))
            steps[0] = base + 4 * (NH // 2 - 1)
            attend(NH - 2)
            steps[0] += 1
            split_weights(0, NH // 2 - 1, False, steps[0])
            attend(NH - 1)

            pool.wait_ge(y2_filled, 4)
            nc.gpsimd.memset(before[:, :, :], 0.0).then_inc(set_up, 1)
            pool.wait_ge(set_up, 3)
            for a in range(1, NGRP):
                last = nc.gpsimd.memset(before[:, a, 0:a], 1.0)
            last.then_inc(set_up, 1)
            pool.wait_ge(ld_shared, 32)
            own(nc.gpsimd.tensor_copy(su_hi[:, :, :], su_raw[:, :, :]))
            nc.gpsimd.tensor_tensor(su_lo[:, :, :], su_raw[:, :, :], su_hi[:, :, :].bitcast(F32), ALU.subtract).then_inc(su_split, 1)

            def split_w1(b, landed, count):
                pool.wait_ge(ld_w1[b], landed)
                high(w1_hi[b][:, :, :].rearrange("p e n -> p (e n)"), w1_raw[b][:, :, :].rearrange("p e n -> p (e n)")).then_inc(pool_step, 1)
                pool.wait_ge(pool_step, count)
                nc.gpsimd.tensor_tensor(w1_lo[b][:, :, :], w1_raw[b][:, :, :], w1_hi[b][:, :, :].bitcast(F32),
                                        ALU.subtract).then_inc(w1_split, 1)

            base = steps[0]
            for b in range(2):
                split_w1(b, 16, base + b + 1)
            with pool.Fori(0, E // 4 - 1) as i:
                for b in range(2):
                    pool.wait_ge(up_filled, i * 4 + 2 * b + 2)
                    split_w1(b, i * 16 + 32, i * 2 + (base + b + 3))

        @block.scalar
        def _(act):
            act.wait_ge(ld_gates, 32)
            nc.scalar.activation(tg[:, :], gl[:, :], ACT.Tanh).then_inc(tanh_done, 1)

            def norm_hi(k, g, bank):
                act.wait_ge(hT_filled, k * NG + g + 1)
                nc.scalar.activation(hT_hi[:, :, g * GT:(g + 1) * GT], ps[:, bank:bank + 2, :], ACT.Copy).then_inc(hT_hi_done, 1)

            act.wait_ge(ld_ctx, 16)
            nc.scalar.activation(cT_hi[:, :, :], cT_raw[:, :, :], ACT.Copy).then_inc(ctx_hi_done, 1)
            for g in range(NG):
                norm_hi(0, g, 0)
            for g in range(NG):
                act.wait_ge(a_filled, NB * g + 1)
                nc.scalar.activation(a_sel[:, g, :, :], ps[:, 2:4, :], ACT.Copy).then_inc(a_first_copied, 1)
                act.wait_ge(a_taken, (NB - 1) * (g + 1))
                nc.scalar.activation(a_silu[:, :, :], a_sel[:, g, :, :], ACT.Silu).then_inc(a_silu_done, 1)
                act.wait_ge(z_ready, g + 1)
                nc.scalar.activation(z_hi[:, g, :, :], a_sel[:, g, :, :], ACT.Copy).then_inc(z_hi_done, 1)

            def gate_silus(g):
                act.wait_ge(sB_filled, g + 1)
                act.wait_ge(wscale_done, 1)
                nc.scalar.activation(sB[:, :], ps[:, 4, :], ACT.Copy, scale=wmean[:, 0:1]).then_inc(sB_done, 1)
                for c in range(IC):
                    act.wait_ge(gs_done, IC * g + c + 1)
                    if IC * g + c >= 2:
                        act.wait_ge(gu_taken, IC * g + c - 1)
                    nc.scalar.activation(gate_silu[:, c % 2, :], gate_s[:, c % 2, :], ACT.Silu).then_inc(silu_done, 1)

            def quant_steps(g):
                for j in range(GN + 1):
                    if j < GN:
                        n = g * GN + j
                        act.wait_ge(s2_ready, n + 1)
                        if n >= 2:
                            act.wait_ge(q2T_filled, n - 1)
                        b = 6 * (j % 2)
                        nc.scalar.activation(q2[:, j % 2, :], ps[:, b:b + 2, :], ACT.Copy,
                                             scale=am2[:, j % 2, 2:3], bias=ROUND).then_inc(q2_done, 1)
                    if j:
                        n = g * GN + j - 1
                        act.wait_ge(q2T_filled, n + 1)
                        if n >= 2:
                            act.wait_ge(y1_filled, n - 1)
                        b = 2 + 2 * ((j - 1) % 2)
                        nc.scalar.activation(q2T[:, (j - 1) % 2, :, :], ps[:, b:b + 2, :], ACT.Copy, bias=-ROUND).then_inc(q2T_done, 1)

            gate_silus(0)
            gate_silus(1)
            quant_steps(0)
            norm_hi(1, 0, 2)
            quant_steps(1)
            norm_hi(1, 1, 2)

            def unit_dst(kind, half, par):
                if kind == "Q":
                    return qT_hi[par][:, half * GT:(half + 1) * GT], QK_SCALE
                if kind == "K":
                    return kT_hi[par][:, half * GT:(half + 1) * GT], 1.0
                if kind == "V":
                    return v_hi[par][:, half * GN:(half + 1) * GN, :], 1.0
                if kind == "T":
                    return pT_hi[:, half, :, :], 1.0
                return oT_hi[:, half * GT:(half + 1) * GT], 1.0

            def high_part(u, bank, par, at):
                act.wait_ge(unit_filled, at)
                dst, scale = unit_dst(u[0], int(u[1]), par)
                nc.scalar.activation(dst, ps[:, bank, :], ACT.Copy, scale=scale).then_inc(hi_done, 1)

            def attend(i, par, units=STEP):
                for u in units:
                    if u[0] == "S":
                        b = int(u[1])
                        act.wait_ge(max_done, i * NB + b + 1)
                        for t in range(2):
                            last = nc.scalar.activation(probs[:, b, t, :], ps[:, BANK[u], t * S:(t + 1) * S], ACT.Exp,
                                                        bias=nmax[:, b, t:t + 1], accum_out=esum[:, b, t:t + 1])
                        last.then_inc(exp_done, 1)
                    else:
                        p = 1 - par if u[0] in "QKV" else par
                        high_part(u, BANK[u], p, filled(i, u, units))

            for n, u in enumerate(FIRST):
                high_part(u, FIRST_BANK[u], 0, n + 1)
            with act.Fori(0, NH // 2 - 1) as i:
                for par in range(2):
                    attend(i * 2 + par, par)
            attend(NH - 2, 0)
            attend(NH - 1, 1, LAST)

            for g in range(NG):
                norm_hi(2, g, 0)
                act.wait_ge(logit_filled, g + 1)
                nc.scalar.activation(sc[:, g * GN:(g + 1) * GN, :],
                                     ps[:, 2, g * GN * E:(g + 1) * GN * E].rearrange("p (n e) -> p n e", e=E),
                                     ACT.Sigmoid).then_inc(sc_done, 1)
                act.wait_ge(xl_filled, g + 1)
                nc.scalar.activation(xl_hi[:, g * GT:(g + 1) * GT], ps[:, 3, :], ACT.Copy).then_inc(xl_hi_done, 1)
            for n in range(NG * SC):
                act.wait_ge(su_filled, n + 1)
                nc.scalar.activation(s_relu[:, n % 2, :], ps[:, 4 + n % SC, :], ACT.Relu).then_inc(su_relu, 1)
                act.wait_ge(su_relu, n + 1)
                nc.scalar.activation(s_act[:, n % SC, n // SC * GT:(n // SC + 1) * GT], s_relu[:, n % 2, :], ACT.Square)\
                    .then_inc(su_taken, 1)

            act.wait_ge(cwT_filled, 1)
            nc.scalar.activation(cwT[:, :], ps[:, 2, 0:NG * P], ACT.Copy).then_inc(cwT_done, 1)

            def expert(e, j, first):
                act.wait_ge(up_filled, e + (j + 1))
                if not (first and j < 2):
                    act.wait_ge(e_z_done, e + (j - 1))
                nc.scalar.activation(e_relu[j % 2][:, :], ps[:, 4 + 2 * (j % 2):6 + 2 * (j % 2), :], ACT.Relu).then_inc(relu_done, 1)

            for j in range(4):
                expert(0, j, True)
            with act.Fori(1, E // 4) as i:
                for j in range(4):
                    expert(i * 4, j, False)
            act.wait_ge(down_done, E)
            nc.scalar.activation(yl[:, :], ps[:, 0:2, :], ACT.Copy).then_inc(yl_done, 1)

        @block.vector
        def _(dve):
            steps = [0]
            V = nc.vector

            def own(ins):
                steps[0] += 1
                ins.then_inc(dve_step, 1)
                dve.wait_ge(dve_step, steps[0])

            def norm(g):
                t0, t1 = g * GN, (g + 1) * GN
                for n in range(t0, t1):
                    last = V.bn_stats(st[:, n, :], xr[:, n, :])
                own(last)
                for n in range(t0, t1):
                    last = V.bn_aggr(mv[:, n, :], st[:, n, :])
                own(last)
                v, y, t = ln_v[:, t0:t1], ln_y[:, t0:t1], ln_t[:, t0:t1]
                own(V.tensor_scalar(v, mv[:, t0:t1, 1], LN_EPS, None, ALU.add))
                own(V.tensor_scalar(ln_i[:, t0:t1], v.bitcast(I32), 1, None, ALU.logical_shift_right))
                own(V.tensor_scalar(y.bitcast(I32), ln_i[:, t0:t1], -1.0, RSQRT_GUESS, ALU.mult, ALU.add))
                for _ in range(3):
                    own(V.scalar_tensor_tensor(t, y, 0.5, y, ALU.mult, ALU.mult))
                    own(V.tensor_tensor(t, t, v, ALU.mult))
                    own(V.scalar_tensor_tensor(y, t, 1.5, y, ALU.subtract, ALU.mult))
                for n in range(t0, t1):
                    last = V.tensor_scalar(h[:, n, :], xr[:, n, :], mv[:, n, 0:1], ln_y[:, n:n + 1], ALU.subtract, ALU.mult)
                return last

            def norm_lo(k, g, bank):
                dve.wait_ge(hT_hi_done, k * NG + g + 1)
                s = slice(g * GT, (g + 1) * GT)
                V.tensor_tensor(hT_lo[:, :, s], ps[:, bank:bank + 2, :], hT_hi[:, :, s].bitcast(F32), ALU.subtract).then_inc(hT_done, 1)

            for g in range(NG):
                dve.wait_ge(ld_x[g], 16)
                norm(g).then_inc(h_ready, 1)
            dve.wait_ge(ctx_hi_done, 1)
            V.tensor_tensor(cT_lo[:, :, :], cT_raw[:, :, :], cT_hi[:, :, :].bitcast(F32), ALU.subtract).then_inc(ctx_done, 1)
            norm_lo(0, 0, 0)

            dve.wait_ge(ld_ids, 32)
            for e in range(1, NB):
                V.tensor_scalar(ge_row[:, e - 1, :], ids_row[:, :], float(e * TOK_PER_EXPERT), None, ALU.is_ge)
                last = V.tensor_scalar(ge_col[:, e - 1, :], ids_col[:, :], float(e * TOK_PER_EXPERT), None, ALU.is_ge)
            own(last)
            norm_lo(0, 1, 0)
            V.tensor_scalar(tgm[:, 0, :], ge_col[:, 0, :], -1.0, 1.0, ALU.mult, ALU.add)
            for e in range(1, NB - 1):
                V.tensor_tensor(tgm[:, e, :], ge_col[:, e - 1, :], ge_col[:, e, :], ALU.subtract)
            own(V.tensor_copy(tgm[:, NB - 1, :], ge_col[:, NB - 2, :]))
            dve.wait_ge(tanh_done, 1)
            own(V.tensor_scalar(tgm[:, :, :], tgm[:, :, :], tg[:, 0:1], None, ALU.mult))

            for g in range(NG):
                s = slice(g * GT, (g + 1) * GT)
                for e in range(1, NB):
                    dve.wait_ge(a_filled, NB * g + e + 1)
                    if e == 1:
                        dve.wait_ge(a_first_copied, g + 1)
                    b = 2 + 2 * (e % 2)
                    for c in range(DC):
                        last = V.copy_predicated(a_sel[:, g, c, :], ge_row[:, e - 1, s], ps[:, b + c, :])
                    last.then_inc(a_taken, 1)
                    dve.wait_ge(a_taken, (NB - 1) * g + e)
                dve.wait_ge(a_silu_done, g + 1)
                V.tensor_tensor(a_sel[:, g, :, :], a_sel[:, g, :, :], a_silu[:, :, :], ALU.mult).then_inc(z_ready, 1)
                dve.wait_ge(z_hi_done, g + 1)
                V.tensor_tensor(z_lo[:, g, :, :], a_sel[:, g, :, :], z_hi[:, g, :, :].bitcast(F32), ALU.subtract).then_inc(z_done, 1)
                if g == 0:
                    for i in range(3):
                        dve.wait_ge(ld_w[i], 16)
                        last = V.tensor_reduce(wsum[:, i:i + 1], wraw[i][:, :], AX.X, ALU.add, apply_absolute_value=True)
                    last.then_inc(wsum_done, 1)

            def add_experts(g):
                for n in range(g * GN, (g + 1) * GN):
                    dve.wait_ge(y0_filled, n + 1)
                    for e in range(NB):
                        b = (6 if n % 2 == 0 else 0) + e // 2
                        ins = V.scalar_tensor_tensor(xr[:, n, :], ps[:, b, (e % 2) * D:(e % 2 + 1) * D], tgm[:, e, n:n + 1],
                                                     xr[:, n, :], ALU.mult, ALU.add)
                        if e < NB - 1:
                            own(ins)
                    ins.then_inc(y0_taken, 1)
                dve.wait_ge(y0_taken, (g + 1) * GN)

            def quantise(g):
                s = slice(g * GN, (g + 1) * GN)
                own(V.tensor_reduce(am[:, s], h[:, s, :], AX.X, ALU.max, apply_absolute_value=True))
                own(V.tensor_scalar(am[:, s], am[:, s], Q_EPS, None, ALU.max))
                own(V.reciprocal(am_r[:, s], am[:, s]))
                own(V.tensor_scalar(am_r[:, s], am_r[:, s], 128.0, None, ALU.mult))
                if g:
                    dve.wait_ge(q1T_filled, g)
                for n in range(GN):
                    last = V.tensor_scalar(qtok[:, n, :], h[:, g * GN + n, :], am_r[:, g * GN + n:g * GN + n + 1], ROUND,
                                           ALU.mult, ALU.add)
                own(last)
                V.tensor_scalar(qtok[:, :, :], qtok[:, :, :], ROUND + 127.0, ROUND - 128.0, ALU.min, ALU.max).then_inc(q1_ready, 1)
                own(V.tensor_scalar(am_c[:, s], am[:, s], 1.0 / 128.0, None, ALU.mult))
                if g:
                    dve.wait_ge(sB_filled, g)
                V.tensor_scalar(c_up[:, s], am_c[:, s], wmean[:, 1:2], None, ALU.mult)
                for n in range(GN):
                    last = V.tensor_scalar(diag[:, n, :], ident, am_c[:, g * GN + n:g * GN + n + 1], None, ALU.mult)
                last.then_inc(diag_ready, 1)

            def gate_up(g):
                dve.wait_ge(q1T_filled, g + 1)
                V.tensor_scalar(qT[:, :, :], ps[:, 2:4, :], -ROUND, None, ALU.add).then_inc(q1T_done, 1)
                dve.wait_ge(sB_done, g + 1)
                if g:
                    dve.wait_ge(fly_diff, 3 * g)
                for c in range(IC + 1):
                    if c < IC:
                        n = IC * g + c
                        dve.wait_ge(gu_filled, n + 1)
                        V.tensor_tensor(gate_s[:, c % 2, :], ps[:, 2 + 2 * (c % 2), :], sB[:, :], ALU.mult).then_inc(gs_done, 1)
                    if c:
                        n = IC * g + c - 1
                        dve.wait_ge(silu_done, n + 1)
                        V.tensor_tensor(inner_a[:, c - 1, :], gate_silu[:, (c - 1) % 2, :], ps[:, 3 + 2 * ((c - 1) % 2), :],
                                        ALU.mult).then_inc(gu_taken, 1)

            def fly_sums(g):
                for lvl, (src, dst) in enumerate(((inner_a, inner_b), (inner_b, inner_a), (inner_a, inner_b))):
                    hh = IC // 2 >> lvl
                    s = src[:, :, :].rearrange("p (a two c) t -> p a two c t", two=2, c=hh)
                    d = dst[:, :, :].rearrange("p (a two c) t -> p a two c t", two=2, c=hh)
                    if lvl == 0:
                        dve.wait_ge(gu_taken, IC * (g + 1))
                        if g:
                            dve.wait_ge(had_filled, GN * g)
                    else:
                        dve.wait_ge(fly_sum, 3 * g + lvl)
                        dve.wait_ge(fly_diff, 3 * g + lvl)
                    V.tensor_tensor(d[:, :, 0], s[:, :, 0], s[:, :, 1], ALU.add).then_inc(fly_sum, 1)

            def down(g):
                for j in range(GN + 1):
                    if j < GN:
                        n = g * GN + j
                        b, a = 6 * (n % 2), am2[:, n % 2, :]
                        dve.wait_ge(had_filled, n + 1)
                        own(V.tensor_reduce(a[:, 0:1], ps[:, b:b + 2, :], AX.XY, ALU.max, apply_absolute_value=True))
                        own(V.tensor_scalar(a[:, 1:2], a[:, 0:1], c_up[:, n:n + 1], Q_EPS, ALU.mult, ALU.max))
                        own(V.reciprocal(a[:, 0:1], a[:, 1:2]))
                        V.tensor_scalar(a[:, 3:4], a[:, 1:2], fdown[:, 0:1], None, ALU.mult)
                        own(V.tensor_scalar(a[:, 0:1], a[:, 0:1], 128.0, None, ALU.mult))
                        V.tensor_scalar(a[:, 2:3], a[:, 0:1], c_up[:, n:n + 1], None, ALU.mult).then_inc(s2_ready, 1)
                    if j:
                        n = g * GN + j - 1
                        b, a = 6 * (n % 2), am2[:, n % 2, :]
                        dve.wait_ge(y1_filled, n + 1)
                        V.scalar_tensor_tensor(xr[:, n, :], ps[:, b, 0:D], a[:, 3:4], xr[:, n, :], ALU.mult, ALU.add)\
                            .then_inc(y1_taken, 1)
                dve.wait_ge(y1_taken, (g + 1) * GN)

            add_experts(0)
            dve.wait_ge(wtot_filled, 1)
            own(V.tensor_scalar(wmean[:, :], ps[:, 2, 0:3], 1.0 / W_COUNT, Q_EPS, ALU.mult, ALU.max))
            V.tensor_scalar(fdown[:, :], wmean[:, 2:3], tg[:, 2:3], 1.0 / 128.0, ALU.mult, ALU.mult)
            V.reciprocal(wscale[:, :], wmean[:, :]).then_inc(wscale_done, 1)
            own(norm(0))
            quantise(0)
            add_experts(1)
            gate_up(0)
            own(norm(1))
            quantise(1)
            fly_sums(0)
            gate_up(1)
            down(0)
            fly_sums(1)
            norm(0).then_inc(h_ready, 1)
            norm_lo(1, 0, 2)
            down(1)
            norm(1).then_inc(h_ready, 1)
            norm_lo(1, 1, 2)

            def low_part(u, bank, par, at):
                dve.wait_ge(hi_done, at)
                kind, half = u[0], int(u[1])
                s, n = slice(half * GT, (half + 1) * GT), slice(half * GN, (half + 1) * GN)
                src = ps[:, bank, :]
                if kind == "Q":
                    ins = V.scalar_tensor_tensor(qT_lo[par][:, s], src, QK_SCALE, qT_hi[par][:, s].bitcast(F32),
                                                 ALU.mult, ALU.subtract)
                elif kind == "K":
                    ins = V.tensor_tensor(kT_lo[par][:, s], src, kT_hi[par][:, s].bitcast(F32), ALU.subtract)
                elif kind == "V":
                    ins = V.tensor_tensor(v_lo[par][:, n, :].rearrange("p n d -> p (n d)"), src,
                                          v_hi[par][:, n, :].rearrange("p n d -> p (n d)").bitcast(F32), ALU.subtract)
                elif kind == "T":
                    ins = V.tensor_tensor(pT_lo[:, half, :, :].rearrange("p c q -> p (c q)"), src,
                                          pT_hi[:, half, :, :].rearrange("p c q -> p (c q)").bitcast(F32), ALU.subtract)
                else:
                    ins = V.tensor_tensor(oT_lo[:, s], src, oT_hi[:, s].bitcast(F32), ALU.subtract)
                ins.then_inc(lo_done, 1)

            def attend(i, par, units=STEP, splits=SPLIT):
                for p, u in enumerate(units):
                    if u[0] == "S":
                        b = int(u[1])
                        dve.wait_ge(unit_filled, filled(i, u, units))
                        V.tensor_reduce(nmax[:, b, :], ps[:, BANK[u], :].rearrange("p (t k) -> p t k", t=2), AX.X, ALU.max,
                                        negate=True).then_inc(max_done, 1)
                        if b:
                            inverse_sum(i, b - 1)
                    else:
                        low_part(u, BANK[u], 1 - par if u[0] in "QKV" else par, split(i, u, splits))
                    if u == "T0":
                        inverse_sum(i, NB - 1)

            def inverse_sum(i, b):
                dve.wait_ge(exp_done, i * NB + b + 1)
                V.reciprocal(rsum[:, b, :], esum[:, b, :]).then_inc(rsum_done, 1)

            for n, u in enumerate(FIRST):
                low_part(u, FIRST_BANK[u], 0, n + 1)
            with dve.Fori(0, NH // 2 - 1) as i:
                for par in range(2):
                    attend(i * 2 + par, par)
            attend(NH - 2, 0)
            attend(NH - 1, 1, LAST, SPLIT_LAST)

            for g in range(NG):
                for n in range(g * GN, (g + 1) * GN):
                    dve.wait_ge(y2_filled, n // 2 + 1)
                    last = V.scalar_tensor_tensor(xr[:, n, :], ps[:, 4 + n // 2, (n % 2) * D:(n % 2 + 1) * D], tg[:, 1:2],
                                                  xr[:, n, :], ALU.mult, ALU.add).then_inc(y2_taken, 1)
                dve.wait_ge(y2_taken, (g + 1) * GN)
                norm(g).then_inc(h_ready, 1)
            for g in range(NG):
                norm_lo(2, g, 0)
                dve.wait_ge(xl_hi_done, g + 1)
                V.tensor_tensor(xl_lo[:, g * GT:(g + 1) * GT], ps[:, 3, :], xl_hi[:, g * GT:(g + 1) * GT].bitcast(F32),
                                ALU.subtract).then_inc(xl_done, 1)

            dve.wait_ge(sc_done, NG)
            dve.wait_ge(ld_small, 64)
            own(V.tensor_tensor(sbias[:, :, :], sc[:, :, :],
                                gbias[:, :].unsqueeze(1).to_broadcast([P, NT, E]), ALU.add))
            for n in range(NT):
                for q in range(NGRP):
                    last = V.max(gtop[:, n * NGRP + q, :], sbias[:, n, q * EG:(q + 1) * EG])
            own(last)
            own(V.tensor_tensor(gscore[:, :, :].rearrange("p n q -> p (n q)"), gtop[:, :, 0], gtop[:, :, 1], ALU.add))
            other = gscore[:, :, :].unsqueeze(2).to_broadcast([P, NT, NGRP, NGRP])
            own_score = gscore[:, :, :].unsqueeze(3).to_broadcast([P, NT, NGRP, NGRP])
            dve.wait_ge(set_up, 4)
            V.tensor_tensor(cmp[:, :, :, :], other, own_score, ALU.is_gt)
            own(V.tensor_tensor(eqs[:, :, :, :], other, own_score, ALU.is_equal))
            own(V.tensor_tensor(eqs[:, :, :, :], eqs[:, :, :, :],
                                before[:, :, :].unsqueeze(1).to_broadcast([P, NT, NGRP, NGRP]), ALU.mult))
            own(V.tensor_tensor(cmp[:, :, :, :], cmp[:, :, :, :], eqs[:, :, :, :], ALU.add))
            own(V.tensor_reduce(grank[:, :, :], cmp[:, :, :, :], AX.X, ALU.add))
            V.memset(masked[:, :, :], -3.0e38)
            own(V.tensor_scalar(gmask[:, :, :], grank[:, :, :], float(TOPG), None, ALU.is_lt))
            own(V.tensor_copy(gmask8[:, :, :].rearrange("p n (q k) -> p (n q) k", k=EG),
                              gmask[:, :, :].rearrange("p n q -> p (n q)").unsqueeze(2).to_broadcast([P, NT * NGRP, EG])))
            own(V.copy_predicated(masked[:, :, :], gmask8[:, :, :], sbias[:, :, :]))
            for n in range(NT):
                last = V.max(top8[:, n, :], masked[:, n, :])
            own(last)
            for n in range(NT):
                last = V.match_replace(left[:, n, :], top8[:, n, :], masked[:, n, :], -3.4e38)
            own(last)
            own(V.tensor_tensor(sel[:, :, :], masked[:, :, :], left[:, :, :], ALU.not_equal))
            own(V.tensor_tensor(wsel[:, :, :], sel[:, :, :], sc[:, :, :], ALU.mult))
            own(V.tensor_reduce(wden[:, :], wsel[:, :, :], AX.X, ALU.add))
            own(V.reciprocal(wden[:, :], wden[:, :]))
            own(V.tensor_scalar(wden[:, :], wden[:, :], ROUTED_SCALE, None, ALU.mult))
            V.tensor_tensor(cw[:, :, :], wsel[:, :, :], wden[:, :].unsqueeze(2).to_broadcast([P, NT, E]), ALU.mult)\
                .then_inc(cw_ready, 1)

            for n in range(NT):
                dve.wait_ge(y3_filled, n // 2 + 1)
                V.scalar_tensor_tensor(xr[:, n, :], ps[:, Y3_BANK[n // 2], (n % 2) * D:(n % 2 + 1) * D], tg[:, 3:4], xr[:, n, :],
                                       ALU.mult, ALU.add).then_inc(y3_taken, 1)

            def expert(e, j, landed, first):
                up = ps[:, 4 + 2 * (j % 2):6 + 2 * (j % 2), :].rearrange("p b t -> p (b t)")
                dve.wait_ge(relu_done, e + (j + 1))
                dve.wait_ge(ld_cw[j], landed)
                V.scalar_tensor_tensor(e_wa[j % 2][:, :], up, 0.0, cw_row[j][:, :], ALU.max, ALU.mult).then_inc(wa_done, 1)
                dve.wait_ge(wa_done, e + (j + 1))
                if not (first and j < 2):
                    dve.wait_ge(down_done, e + (j - 1))
                V.tensor_tensor(e_z[j % 2][:, :], e_wa[j % 2][:, :], e_relu[j % 2][:, :], ALU.mult).then_inc(e_z_done, 1)

            for j in range(4):
                expert(0, j, 16, True)
            with dve.Fori(1, E // 4) as i:
                for j in range(4):
                    expert(i * 4, j, i * 16 + 16, False)
            dve.wait_ge(y3_taken, NT)
            for n in range(NT):
                dve.wait_ge(y4_filled, n // 2 + 1)
                V.scalar_tensor_tensor(xr[:, n, :], ps[:, 4 + n // 2, (n % 2) * D:(n % 2 + 1) * D], tg[:, 3:4], xr[:, n, :],
                                       ALU.mult, ALU.add).then_inc(y4_taken, 1)

        @block.tensor
        def _(pe):
            mm = nc.tensor.matmul

            def product(dst, lhs, rhs, first=True, last=True, check=True):
                (l_hi, l_lo), (r_hi, r_lo) = lhs, rhs
                kw = {} if check else {"skip_group_check": True}
                mm(dst, l_lo, r_hi, start=first, stop=False, **kw)
                mm(dst, l_hi, r_lo, start=False, stop=False, **kw)
                return mm(dst, l_hi, r_hi, start=False, stop=last, **kw)

            def both(hi, lo, *at):
                return hi[at], lo[at]

            A = slice(None)

            def transpose_norm(k, g, bank):
                pe.wait_ge(h_ready, k * NG + g + 1)
                for c in range(DC):
                    for j in range(GN):
                        last = nc.tensor.transpose(ps[:, bank + c, j * P:(j + 1) * P], h[:, g * GN + j, c * P:(c + 1) * P], ident)
                last.then_inc(hT_filled, 1)

            pe.wait_ge(ld_const, 16)
            transpose_norm(0, 0, 0)
            pe.wait_ge(hT_done, 1)
            transpose_norm(0, 1, 0)
            pe.wait_ge(ctx_done, 1)
            for g in range(NG):
                pe.wait_ge(hT_done, g + 1)
                for e in range(NB):
                    if e >= 2 or g:
                        before_e = (e - 2) % NB
                        before_g = g if e >= 2 else g - 1
                        if before_e == 0:
                            pe.wait_ge(a_first_copied, before_g + 1)
                        else:
                            pe.wait_ge(a_taken, (NB - 1) * before_g + before_e)
                    for f in range(DC):
                        for c in range(DC):
                            last = product(ps[:, 2 + 2 * (e % 2) + f, :],
                                           both(cT_hi, cT_lo, A, c, slice(e * S + f * P, e * S + (f + 1) * P)),
                                           both(hT_hi, hT_lo, A, c, slice(g * GT, (g + 1) * GT)), c == 0, c == DC - 1)
                    last.then_inc(a_filled, 1)
            for g in range(NG):
                pe.wait_ge(z_done, g + 1)
                for n in range(g * GN, (g + 1) * GN):
                    if n >= 2:
                        pe.wait_ge(y0_taken, n - 1)
                    for b in range(2):
                        for c in range(DC):
                            last = product(ps[:, (6 if n % 2 == 0 else 0) + b, :],
                                           both(z_hi, z_lo, A, g, c, slice((n - g * GN) * P, (n - g * GN + 1) * P)),
                                           both(cT_hi, cT_lo, A, c, slice(b * 2 * S, (b + 1) * 2 * S)), c == 0, c == DC - 1)
                    last.then_inc(y0_filled, 1)
                if g == 0:
                    pe.wait_ge(set_up, 2)
                    pe.wait_ge(wsum_done, 1)
                    pe.wait_ge(a_taken, (NB - 1) * NG)
                    mm(ps[:, 2, 0:3], ones[:, :], wsum[:, :], start=True, stop=True).then_inc(wtot_filled, 1)

            w_gate = wq8[0][:, :].rearrange("p (c n) -> p c n", c=DC)
            w_up = wq8[1][:, :].rearrange("p (c n) -> p c n", c=DC)
            w_down = wq8[2][:, :].rearrange("p (c n) -> p c n", c=IC)

            def gate_up(g):
                pe.wait_ge(q1_ready, g + 1)
                if g:
                    pe.wait_ge(gu_taken, IC * g)
                for c in range(DC):
                    for j in range(GN):
                        last = nc.tensor.transpose(ps[:, 2 + c, j * P:(j + 1) * P], qtok[:, j, c * P:(c + 1) * P], ident)
                last.then_inc(q1T_filled, 1)
                pe.wait_ge(diag_ready, g + 1)
                for j in range(GN):
                    last = mm(ps[:, 4, j * P:(j + 1) * P], ones[:, :], diag[:, j, :], start=True, stop=True)
                last.then_inc(sB_filled, 1)
                pe.wait_ge(q1T_done, g + 1)
                pe.wait_ge(sB_done, g + 1)
                pe.wait_ge(w_ternary, 2)
                for c in range(IC):
                    if c >= 2:
                        pe.wait_ge(gu_taken, IC * g + c - 1)
                    for k, w in enumerate((w_gate, w_up)):
                        for d in range(DC):
                            last = mm(ps[:, 2 + 2 * (c % 2) + k, :], w[:, d, c * P:(c + 1) * P], qT[:, d, :],
                                      start=(d == 0), stop=(d == DC - 1))
                    last.then_inc(gu_filled, 1)

            def hadamard(n):
                if n >= 2:
                    pe.wait_ge(y1_taken, n - 1)
                b, j = 6 * (n % 2), n % GN
                for c in range(IC):
                    last = mm(ps[:, b + c // 4, (c % 4) * P:(c % 4 + 1) * P], inner_b[:, c, j * P:(j + 1) * P], had,
                              start=True, stop=True)
                last.then_inc(had_filled, 1)

            def down(n):
                pe.wait_ge(q2_clipped, n + 1)
                if n >= 2:
                    pe.wait_ge(q2T_done, n - 1)
                b = 2 + 2 * (n % 2)
                for c in range(IC):
                    last = nc.tensor.transpose(ps[:, b + c // 4, (c % 4) * P:(c % 4 + 1) * P],
                                               q2[:, n % 2, c * P:(c + 1) * P], ident)
                last.then_inc(q2T_filled, 1)
                pe.wait_ge(q2T_done, n + 1)
                for c in range(IC):
                    last = mm(ps[:, 6 * (n % 2), 0:D], q2T[:, n % 2, c, :], w_down[:, c, :], start=(c == 0), stop=(c == IC - 1))
                last.then_inc(y1_filled, 1)

            gate_up(0)
            gate_up(1)
            pe.wait_ge(y0_taken, NT)
            pe.wait_ge(w_ternary, 3)
            for g in range(NG):
                pe.wait_ge(fly_sum, 3 * (g + 1))
                pe.wait_ge(fly_diff, 3 * (g + 1))
                if g == 0:
                    pe.wait_ge(gu_taken, IC * NG)
                else:
                    pe.wait_ge(hT_done, NG + 1)
                t0 = g * GN
                hadamard(t0)
                hadamard(t0 + 1)
                for j in range(GN):
                    down(t0 + j)
                    if j + 2 < GN:
                        hadamard(t0 + j + 2)
                transpose_norm(1, g, 2)

            def unit(u, bank, par):
                kind, half = u[0], int(u[1])
                dst = ps[:, bank, :]
                s = slice(half * GT, (half + 1) * GT)
                if kind in "QK":
                    w = "QK".index(kind)
                    src = (hT_hi, hT_lo) if kind == "Q" else (cT_hi, cT_lo)
                    for c in range(DC):
                        last = product(dst, both(wqkv_hi[par], wqkv_lo[par], A, w, c, A), both(*src, A, c, s), c == 0, c == DC - 1)
                elif kind == "V":
                    for n in range(GN):
                        t = half * GN + n
                        for c in range(DC):
                            last = product(dst[:, n * P:(n + 1) * P], both(cT_hi, cT_lo, A, c, slice(t * P, (t + 1) * P)),
                                           both(wqkv_hi[par], wqkv_lo[par], A, 2, c, A), c == 0, c == DC - 1)
                elif kind == "S":
                    for t in range(2):
                        q0 = half * S + t * P
                        last = product(dst[:, t * S:(t + 1) * S], both(qT_hi[par], qT_lo[par], A, slice(q0, q0 + P)),
                                       both(kT_hi[par], kT_lo[par], A, slice(half * S, (half + 1) * S)))
                elif kind == "T":
                    for k in range(2):
                        for t in range(2):
                            last = nc.tensor.transpose(dst[:, k * S + t * P:k * S + (t + 1) * P],
                                                       probs[:, half, t, k * P:(k + 1) * P], ident)
                else:
                    for b in (2 * half, 2 * half + 1):
                        for k in range(2):
                            last = product(dst[:, (b % 2) * S:(b % 2 + 1) * S], both(v_hi[par], v_lo[par], A, 2 * b + k, A),
                                           both(pT_hi, pT_lo, A, b, k, A), k == 0, k == 1)
                last.then_inc(unit_filled, 1)

            def attend(i, par, units=STEP, splits=SPLIT):
                pe.wait_ge(lo_done, i * len(SPLIT) + len(FIRST))
                for p, u in enumerate(units):
                    before_u = [v for v in units[:p] if BANK[v] == BANK[u]]
                    if before_u and before_u[-1][0] == "S":
                        pe.wait_ge(exp_done, i * NB + int(before_u[-1][1]) + 1)
                    elif before_u:
                        pe.wait_ge(lo_done, split(i, before_u[-1], splits))
                    if u == "Q0":
                        pe.wait_ge(qkv_split, i + 2)
                    if u[0] == "T":
                        pe.wait_ge(probs_done, i * NB + int(u[1]) + 1)
                    if u[0] == "O":
                        pe.wait_ge(lo_done, split(i, "T" + str(2 * int(u[1]) + 1), splits))
                    unit(u, BANK[u], 1 - par if u[0] in "QKV" else par)
                pe.wait_ge(wo_split, i + 1)
                final = units is LAST
                for n in range(NT):
                    if n % GN == 0:
                        pe.wait_ge(lo_done, split(i, "O" + str(n // GN), splits))
                    last = product(ps[:, 4 + n // 2, (n % 2) * D:(n % 2 + 1) * D],
                                   both(oT_hi, oT_lo, A, slice(n * P, (n + 1) * P)), (wo_hi[par][:, :], wo_lo[par][:, :]),
                                   False, final and n % 2 == 1, check=False)
                    if final and n % 2:
                        last.then_inc(y2_filled, 1)

            pe.wait_ge(y1_taken, NT)
            pe.wait_ge(q2T_done, NT)
            for b in range(4):
                mm(ps[:, 4 + b, :], zeros[:, 0:P], zeros[:, :], start=True, stop=False, skip_group_check=True)
            pe.wait_ge(qkv_split, 1)
            for n, u in enumerate(FIRST):
                if n == 2:
                    pe.wait_ge(hT_done, 2 * NG)
                if n >= 4:
                    pe.wait_ge(lo_done, n - 3)
                unit(u, FIRST_BANK[u], 0)
            with pe.Fori(0, NH // 2 - 1) as i:
                for par in range(2):
                    attend(i * 2 + par, par)
            attend(NH - 2, 0)
            attend(NH - 1, 1, LAST, SPLIT_LAST)

            pe.wait_ge(lo_done, len(FIRST) + len(SPLIT) * (NH - 1) + len(SPLIT_LAST))
            pe.wait_ge(small_split, 1)
            for g in range(NG):
                s = slice(g * GT, (g + 1) * GT)
                if g:
                    pe.wait_ge(hT_done, 2 * NG + g)
                transpose_norm(2, g, 0)
                pe.wait_ge(hT_done, 2 * NG + g + 1)
                for n in range(g * GN, (g + 1) * GN):
                    for c in range(DC):
                        last = product(ps[:, 2, n * E:(n + 1) * E], both(hT_hi, hT_lo, A, c, slice(n * P, (n + 1) * P)),
                                       both(gw_hi, gw_lo, A, c, A), c == 0, c == DC - 1)
                last.then_inc(logit_filled, 1)
                if g:
                    pe.wait_ge(xl_done, g)
                for c in range(DC):
                    last = product(ps[:, 3, :], both(fc1_hi, fc1_lo, A, c, A), both(hT_hi, hT_lo, A, c, s), c == 0, c == DC - 1)
                last.then_inc(xl_filled, 1)
            pe.wait_ge(su_split, 1)
            pe.wait_ge(y2_taken, NT)
            for n in range(NG * SC):
                g, m = n // SC, n % SC
                if g:
                    pe.wait_ge(su_taken, n - SC + 1)
                for c in range(DC):
                    last = product(ps[:, 4 + m, :], both(su_hi, su_lo, A, c, slice(m * P, (m + 1) * P)),
                                   both(hT_hi, hT_lo, A, c, slice(g * GT, (g + 1) * GT)), c == 0, c == DC - 1)
                last.then_inc(su_filled, 1)
            pe.wait_ge(xl_done, NG)
            for n in range(NT):
                if n % GN == 0:
                    pe.wait_ge(su_taken, SC * (n // GN + 1))
                if n == 6:
                    pe.wait_ge(su_taken, SC * NG)
                for c in range(SC):
                    last = mm(ps[:, Y3_BANK[n // 2], (n % 2) * D:(n % 2 + 1) * D], s_act[:, c, n * P:(n + 1) * P], sd[:, c, :],
                              start=(c == 0), stop=(c == SC - 1))
                if n % 2:
                    last.then_inc(y3_filled, 1)

            pe.wait_ge(cw_ready, 1)
            pe.wait_ge(sc_done, NG)
            for q in range(NG):
                last = nc.tensor.transpose(ps[:, 2, q * P:(q + 1) * P],
                                           cw[:, q * GN:(q + 1) * GN, :].rearrange("p n e -> p (n e)"), ident)
            last.then_inc(cwT_filled, 1)

            def up(e, j, split_count, free):
                pe.wait_ge(w1_split, split_count)
                if free:
                    pe.wait_ge(wa_done, e + (j - 1))
                    pe.wait_ge(relu_done, e + (j - 1))
                w = both(w1_hi[j // 2 % 2], w1_lo[j // 2 % 2], A, j % 2, A)
                for t in range(2):
                    last = product(ps[:, 4 + 2 * (j % 2) + t, :], w, both(xl_hi, xl_lo, A, slice(t * 512, (t + 1) * 512)))
                last.then_inc(up_filled, 1)

            def experts(e, i, final):
                for j in range(4):
                    if not (final and j >= 2):
                        up(e, j + 2, i * 2 + ((j + 2) // 2 + 1), True)
                    pe.wait_ge(e_z_done, e + (j + 1))
                    pe.wait_ge(ld_w2[j // 2], i * 16 + 16)
                    for t in range(2):
                        last = mm(ps[:, t, :], w2[j // 2][:, j % 2, :], e_z[j % 2][:, t * 512:(t + 1) * 512],
                                  start=False, stop=final and j == 3, skip_group_check=True)
                    last.then_inc(down_done, 1)

            pe.wait_ge(y3_taken, NT)
            for b in range(2):
                mm(ps[:, b, :], zeros[:, 0:P], zeros[:, :], start=True, stop=False, skip_group_check=True)
            up(0, 0, 1, False)
            up(0, 1, 1, False)
            with pe.Fori(0, E // 4 - 1) as i:
                experts(i * 4, i, False)
            experts(E - 4, E // 4 - 1, True)
            pe.wait_ge(yl_done, 1)
            for n in range(NT):
                last = mm(ps[:, 4 + n // 2, (n % 2) * D:(n % 2 + 1) * D], yl[:, n * P:(n + 1) * P], fc2[:, :], start=True, stop=True)
                if n % 2:
                    last.then_inc(y4_filled, 1)


def kernel(**inputs):
    import numpy as np
    import concourse.bacc as bacc
    from concourse.bass_utils import run_bass_kernel_spmd

    a = {k: np.asarray(v) for k, v in inputs.items()}
    B, S, D = a["x"].shape
    T, P = B * S, 128
    heads = a["L1_xattn_Wq"].shape[1] // P

    def head_columns(w):
        return w.reshape(D // P, P, heads, P).transpose(2, 1, 0, 3)

    had = np.ones((1, 1), np.float32)
    while had.shape[0] < P:
        had = np.block([[had, had], [had, -had]])
    inner = a["L0_ffn_w_gate"].shape[0]
    arrays = {
        "x": a["x"].reshape(T, D),
        "ids": a["itok_BxS_13_99985"].reshape(T),
        "ctx_t": a["ctx_2048"].transpose(2, 0, 1).reshape(D, T),
        "g_xattn": a["g_xattn"],
        "g_ffn": a["g_ffn"],
        "w_gate_t": a["L0_ffn_w_gate"].T,
        "w_up_t": a["L0_ffn_w_up"].T,
        "w_down_t": a["L0_ffn_w_down"].T,
        "w_qkv": np.stack([head_columns(a["L1_xattn_" + n]) for n in ("Wq", "Wk", "Wv")], axis=2),
        "w_o": a["L1_xattn_Wo"].reshape(heads, P, D),
        "gate_w_t": a["L1_ffn_gate_w"].T,
        "gate_bias": a["L1_ffn_gate_bias"],
        "fc1_t": a["L1_ffn_fc1_w"].T,
        "fc2_t": a["L1_ffn_fc2_w"].T,
        "w1_t": a["L1_ffn_w1"].transpose(0, 2, 1),
        "w2_t": a["L1_ffn_w2"].transpose(0, 2, 1),
        "shared_up_t": a["L1_ffn_shared_up_w"].T,
        "shared_down_t": a["L1_ffn_shared_down_w"].T,
        "consts": np.stack([np.eye(P, dtype=np.float32), had * np.float32(1.0 / np.sqrt(inner))], axis=1),
    }
    arrays = {f"in_{k}": np.ascontiguousarray(v) for k, v in arrays.items()}
    nc = bacc.Bacc("TRN2", target_bir_lowering=False, num_devices=1)
    args = [nc.dram_tensor(k, v.shape, mybir.dt.from_np(v.dtype), kind="ExternalInput").ap() for k, v in arrays.items()]
    experts = a["L1_ffn_gate_w"].shape[0]
    scratch = nc.dram_tensor("cw_scratch", (experts, T), mybir.dt.float32, kind="Internal").ap()
    out = nc.dram_tensor("out", (T, D), mybir.dt.float32, kind="ExternalOutput").ap()
    flamingo_two_layer_kernel(nc, *args, scratch, out, B)
    r = run_bass_kernel_spmd(nc, [arrays], core_ids=[0])
    return r.results[0]["out"].reshape(B, S, D)
```

```python
import concourse.bass as bass
from concourse import mybir
from contextlib import ExitStack


def flamingo_two_layer_kernel(nc, x, ids, ctx_t, g_xattn, g_ffn, w_gate_t, w_up_t, w_down_t,
                              w_qk, w_v, w_o, gate_w_t, gate_bias, fc1_t, fc2_t, w1_t, w2_t,
                              shared_up_t, shared_down_t, consts, cw_scratch, out, batches):
    F32, F32R, BF16, I32 = mybir.dt.float32, mybir.dt.float32r, mybir.dt.bfloat16, mybir.dt.int32
    ALU, ACT, AX = mybir.AluOpType, mybir.ActivationFunctionType, mybir.AxisListType

    P = 128
    T, D = x.shape
    NB = batches
    S = T // NB
    NT = T // P
    DC = D // P
    NG = 2
    GN = NT // NG
    GT = T // NG
    INTER = w_gate_t.shape[1]
    IC = INTER // P
    NH = w_qk.shape[0]
    E = gate_w_t.shape[1]
    NGRP, TOPG, TOPK = 4, 2, 8
    EG = E // NGRP
    SI = shared_up_t.shape[1]
    SC = SI // P
    LN_EPS, Q_EPS = 1e-5, 1e-5
    ROUTED_SCALE = 2.5
    TOK_PER_EXPERT = 12500 // NB
    ROUND = 12582912.0
    RSQRT_GUESS = float(0x5F3759DF - 2**31)
    QK_SCALE = float(P) ** -0.5
    W_COUNT = float(INTER * D)

    ctx = ExitStack()
    with ctx:
        def sb(name, shape, dt=F32, where=None):
            return (where or ctx).enter_context(nc.sbuf_tensor(name, shape, dt))

        def sem(name):
            return ctx.enter_context(nc.semaphore(name))

        xr = sb("xr", [P, NT, D])
        h = sb("h", [P, NT, D])
        hT_hi = sb("hT_hi", [P, DC, T], F32R)
        hT_lo = sb("hT_lo", [P, DC, T], F32R)
        cT_hi = sb("cT_hi", [P, DC, NB * S], F32R)
        cT_lo = sb("cT_lo", [P, DC, NB * S], F32R)
        cst = sb("cst", [P, 5, P])
        ident = cst[:, 0, :]
        ones = sb("ones", [P, P])
        zeros = sb("zeros", [P, 512], F32R)
        gl = sb("gl", [P, 4])
        tg = sb("tg", [P, 4])
        st = sb("st", [P, NT, 6])
        mv = sb("mv", [P, NT, 2])
        ln_v = sb("ln_v", [P, NT])
        ln_y = sb("ln_y", [P, NT])
        ln_t = sb("ln_t", [P, NT])
        ln_i = sb("ln_i", [P, NT], I32)
        wqk_raw = [sb(f"wqk_raw{i}", [P, 2, DC, P]) for i in range(2)]
        wqk_hi = [sb(f"wqk_hi{i}", [P, 2, DC, P], F32R) for i in range(2)]
        wqk_lo = [sb(f"wqk_lo{i}", [P, 2, DC, P], F32R) for i in range(2)]
        wv_raw = [sb(f"wv_raw{i}", [P, DC, 2 * P]) for i in range(2)]
        wv_hi = sb("wv_hi", [P, DC, 2 * P], F32R)
        wv_lo = sb("wv_lo", [P, DC, 2 * P], F32R)
        wo_raw = [sb(f"wo_raw{i}", [P, D]) for i in range(2)]
        wo_hi = [sb(f"wo_hi{i}", [P, D], F32R) for i in range(2)]
        wo_lo = [sb(f"wo_lo{i}", [P, D], F32R) for i in range(2)]
        fc1_raw = sb("fc1_raw", [P, DC, P])
        fc1_hi = sb("fc1_hi", [P, DC, P], F32R)
        fc1_lo = sb("fc1_lo", [P, DC, P], F32R)
        fc2 = sb("fc2", [P, D])
        gw_raw = sb("gw_raw", [P, DC, E])
        gw_hi = sb("gw_hi", [P, DC, E], F32R)
        gw_lo = sb("gw_lo", [P, DC, E], F32R)
        gbias = sb("gbias", [P, E])

        region = ExitStack()
        cT_raw = sb("cT_raw", [P, DC, NB * S], F32, region)
        ids_row = sb("ids_row", [P, T], I32, region)
        ge_row = sb("ge_row", [P, NB - 1, T], I32, region)
        wraw = [sb(f"wraw{i}", [P, 2 * INTER], F32, region) for i in range(3)]
        wq8 = [sb(f"wq8_{i}", [P, 2 * INTER], BF16, region) for i in range(3)]
        ids_col = sb("ids_col", [P, NT], I32, region)
        ge_col = sb("ge_col", [P, NB - 1, NT], F32, region)
        tgm = sb("tgm", [P, NB, NT], F32, region)
        had = sb("had", [P, 2, 2 * P], F32R, region)
        wsum = sb("wsum", [P, 3], F32, region)
        wmean = sb("wmean", [P, 3], F32, region)
        wscale = sb("wscale", [P, 3], F32, region)
        fdown = sb("fdown", [P, 1], F32, region)
        am = sb("am", [P, NT], F32, region)
        am_r = sb("am_r", [P, NT], F32, region)
        am_c = sb("am_c", [P, NT], F32, region)
        c_gate = sb("c_gate", [P, NT], F32, region)
        c_up = sb("c_up", [P, NT], F32, region)
        qtok = sb("qtok", [P, GN, D], F32, region)
        qT = sb("qT", [P, NG, DC, GT], BF16, region)
        am2 = sb("am2", [P, 2, 4], F32, region)
        part = ExitStack()
        a_sel = sb("a_sel", [P, NG, DC, GT], F32, part)
        z_hi = sb("z_hi", [P, NG, DC, GT], F32R, part)
        z_lo = sb("z_lo", [P, NG, DC, GT], F32R, part)
        a_silu = sb("a_silu", [P, DC, GT], F32, part)
        part.close()
        part = ExitStack()
        inner = sb("inner", [P, 2, INTER], F32, part)
        fly = sb("fly", [P, INTER], F32, part)
        fT_hi = sb("fT_hi", [P, IC, P], F32R, part)
        fT_lo = sb("fT_lo", [P, IC, P], F32R, part)
        q2 = sb("q2", [P, INTER], F32, part)
        q2T = sb("q2T", [P, IC, P], BF16, part)
        part.close()
        region.close()

        region = ExitStack()
        kT_hi = [sb(f"kT_hi{i}", [P, T], F32R, region) for i in range(2)]
        kT_lo = [sb(f"kT_lo{i}", [P, T], F32R, region) for i in range(2)]
        v_hi, v_lo = [None, None], [None, None]
        v_hi[0] = sb("v_hi0", [P, NT, 2, P], F32R, region)
        v_lo[0] = sb("v_lo0", [P, NT, 2, P], F32R, region)
        qT_hi = [sb(f"qT_hi{i}", [P, T], F32R, region) for i in range(2)]
        qT_lo = [sb(f"qT_lo{i}", [P, T], F32R, region) for i in range(2)]
        v_hi[1] = sb("v_hi1", [P, NT, 2, P], F32R, region)
        v_lo[1] = sb("v_lo1", [P, NT, 2, P], F32R, region)
        probs = sb("probs", [P, NB, 2, S], F32, region)
        pT_hi = sb("pT_hi", [P, NB, 2, S], F32R, region)
        pT_lo = sb("pT_lo", [P, NB, 2, S], F32R, region)
        oT_hi = sb("oT_hi", [P, T], F32R, region)
        oT_lo = sb("oT_lo", [P, T], F32R, region)
        nmax = sb("nmax", [P, NB, 2], F32, region)
        esum = sb("esum", [P, NB, 2], F32, region)
        rsum = sb("rsum", [P, NB, 2], F32, region)
        region.close()

        region = ExitStack()
        su_raw = sb("su_raw", [P, DC, SI], F32, region)
        su_hi = sb("su_hi", [P, DC, SI], F32R, region)
        su_lo = sb("su_lo", [P, DC, SI], F32R, region)
        sd = sb("sd", [P, SC, D], F32, region)
        s_relu = sb("s_relu", [P, 2, GT], F32, region)
        s_act = sb("s_act", [P, SC, T], F32, region)
        xl_hi = sb("xl_hi", [P, T], F32R, region)
        xl_lo = sb("xl_lo", [P, T], F32R, region)
        sc = sb("sc", [P, NT, E], F32, region)
        sbias = sb("sbias", [P, NT, E], F32, region)
        gtop = sb("gtop", [P, NT * NGRP, 8], F32, region)
        gscore = sb("gscore", [P, NT, NGRP], F32, region)
        before = sb("before", [P, NGRP, NGRP], F32, region)
        cmp = sb("cmp", [P, NT, NGRP, NGRP], F32, region)
        eqs = sb("eqs", [P, NT, NGRP, NGRP], F32, region)
        grank = sb("grank", [P, NT, NGRP], F32, region)
        gmask = sb("gmask", [P, NT, NGRP], I32, region)
        gmask8 = sb("gmask8", [P, NT, E], I32, region)
        masked = sb("masked", [P, NT, E], F32, region)
        top8 = sb("top8", [P, NT, 8], F32, region)
        left = sb("left", [P, NT, E], F32, region)
        sel = sb("sel", [P, NT, E], F32, region)
        wsel = sb("wsel", [P, NT, E], F32, region)
        wden = sb("wden", [P, NT], F32, region)
        cw = sb("cw", [P, NT, E], F32, region)
        cwT = sb("cwT", [P, NG * P], F32, region)
        cw_row = [sb(f"cw_row{i}", [P, T], F32, region) for i in range(4)]
        w1_raw = [sb(f"w1_raw{i}", [P, 2, P], F32, region) for i in range(2)]
        w1_hi = [sb(f"w1_hi{i}", [P, 2, P], F32R, region) for i in range(2)]
        w1_lo = [sb(f"w1_lo{i}", [P, 2, P], F32R, region) for i in range(2)]
        w2 = [sb(f"w2_{i}", [P, 2, P], F32, region) for i in range(2)]
        e_relu = [sb(f"e_relu{i}", [P, T], F32, region) for i in range(2)]
        e_wa = [sb(f"e_wa{i}", [P, T], F32, region) for i in range(2)]
        e_z = [sb(f"e_z{i}", [P, T], F32, region) for i in range(2)]
        yl = sb("yl", [P, T], F32, region)
        region.close()

        ps = ctx.enter_context(nc.psum_tensor("ps", [P, 8, 512], F32))

        ld_const, ld_ids, ld_ctx, ld_gates = sem("ld_const"), sem("ld_ids"), sem("ld_ctx"), sem("ld_gates")
        ld_x = [sem(f"ld_x{g}") for g in range(NG)]
        ld_w = [sem(f"ld_w{i}") for i in range(3)]
        ld_small = sem("ld_small")
        ld_qk = [sem(f"ld_qk{i}") for i in range(2)]
        ld_wv = [sem(f"ld_wv{i}") for i in range(2)]
        ld_wo = [sem(f"ld_wo{i}") for i in range(2)]
        ld_shared = sem("ld_shared")
        ld_w1 = [sem(f"ld_w1_{i}") for i in range(2)]
        ld_w2 = [sem(f"ld_w2_{i}") for i in range(2)]
        ld_cw = [sem(f"ld_cw{i}") for i in range(4)]
        cw_stored, out_stored = sem("cw_stored"), sem("out_stored")
        dve_step, pool_step = sem("dve_step"), sem("pool_step")
        set_up, h_ready, hT_filled, hT_hi_done, hT_done = (
            sem("set_up"), sem("h_ready"), sem("hT_filled"), sem("hT_hi_done"), sem("hT_done"))
        tanh_done, masks_ready = sem("tanh_done"), sem("masks_ready")
        ctx_hi_done, ctx_done = sem("ctx_hi_done"), sem("ctx_done")
        a_filled, a_first_copied, a_taken = sem("a_filled"), sem("a_first_copied"), sem("a_taken")
        a_silu_done, z_ready, z_hi_done, z_done = sem("a_silu_done"), sem("z_ready"), sem("z_hi_done"), sem("z_done")
        y0_filled, y0_taken = sem("y0_filled"), sem("y0_taken")
        wsum_done, wtot_filled, wscale_done, w_ternary = (
            sem("wsum_done"), sem("wtot_filled"), sem("wscale_done"), sem("w_ternary"))
        q1_ready, q1T_filled, q1T_done = sem("q1_ready"), sem("q1T_filled"), sem("q1T_done")
        had_copied = sem("had_copied")
        gate_filled, up0_filled, silu_done, inner_done = sem("gate_filled"), sem("up0_filled"), sem("silu_done"), sem("inner_done")
        fly_step, fly_done = sem("fly_step"), sem("fly_done")
        scales_ready = sem("scales_ready")
        fT_filled, fT_hi_done, fT_done = sem("fT_filled"), sem("fT_hi_done"), sem("fT_done")
        had_filled, s2_ready, q2_done, q2_clipped = sem("had_filled"), sem("s2_ready"), sem("q2_done"), sem("q2_clipped")
        q2T_filled, q2T_done, y1_filled, y1_taken = sem("q2T_filled"), sem("q2T_done"), sem("y1_filled"), sem("y1_taken")
        small_split = sem("small_split")
        qk_split, wv_split, wo_split = sem("qk_split"), sem("wv_split"), sem("wo_split")
        unit_filled, hi_done, lo_done = sem("unit_filled"), sem("hi_done"), sem("lo_done")
        max_done, exp_done, rsum_done, probs_done = sem("max_done"), sem("exp_done"), sem("rsum_done"), sem("probs_done")
        y2_filled, y2_taken = sem("y2_filled"), sem("y2_taken")
        su_hi_done, su_split = sem("su_hi_done"), sem("su_split")
        logit_filled, sc_done = sem("logit_filled"), sem("sc_done")
        xl_filled, xl_hi_done, xl_done = sem("xl_filled"), sem("xl_hi_done"), sem("xl_done")
        su_filled, su_relu, su_taken = sem("su_filled"), sem("su_relu"), sem("su_taken")
        y3_filled, y3_taken = sem("y3_filled"), sem("y3_taken")
        cw_ready, cwT_filled, cwT_done = sem("cw_ready"), sem("cwT_filled"), sem("cwT_done")
        w1_split = sem("w1_split")
        up_filled, relu_done, wa_done, e_z_done, down_done = (
            sem("up_filled"), sem("relu_done"), sem("wa_done"), sem("e_z_done"), sem("down_done"))
        yl_done, y4_filled, y4_taken = sem("yl_done"), sem("y4_filled"), sem("y4_taken")

        block = ctx.enter_context(nc.Block())

        STEP = ["S0", "S1", "Y0", "S2", "K0", "S3", "K1", "T0", "Y1", "T1", "V0", "T2",
                "Q0", "Q1", "T3", "O0", "V1", "O1"]
        RING = [u for u in STEP if u[0] != "Y"]
        BANK = {u: p % 4 for p, u in enumerate(RING)}
        FIRST = ["K0", "K1", "V0", "V1", "V2", "V3", "Q0", "Q1"]
        LOOPED = NH // 4 * 4 - 4
        SPLITS = sum(u[0] != "S" for u in RING)

        def ring_of(i):
            if i == NH - 1:
                return [u for u in RING if u[0] not in "QKV"]
            return [u for u in RING if u[0] != "V"] if i == NH - 2 else RING

        def filled(i, u, at=None):
            if at == NH - 1:
                return len(FIRST) + len(RING) * (NH - 2) + len(ring_of(NH - 2)) + ring_of(at).index(u) + 1
            return i * len(RING) + (len(FIRST) + ring_of(at).index(u) + 1)

        def split(i, u, at=None):
            units = [v for v in ring_of(at) if v[0] != "S"]
            if at == NH - 1:
                return len(FIRST) + SPLITS * (NH - 2) + sum(v[0] != "S" for v in ring_of(NH - 2)) + units.index(u) + 1
            return i * SPLITS + (len(FIRST) + units.index(u) + 1)

        def place(u, j):
            if u[0] == "V":
                return "V" + str(2 * (j % 2) + int(u[1])), 1 - j // 2
            return u, 1 - j % 2 if u[0] in "QK" else j % 2

        def split_before(i, u, at=None):
            if at == 0:
                return len(FIRST)
            if at == NH - 1:
                return split(NH - 2, u, NH - 2)
            return i * SPLITS + (split(0, u) - SPLITS)

        XL_BANK = [3, 0]
        Y3_BANK = [0, 1, 3, 0]

        STAGES = [("G", 0), ("U", 0), ("C", 3), ("H", 2), ("F", 1), ("D", 3)]
        AFTER = {0: [("A", 0)], 1: [("A", 1)], 2: [("A", 2)], NT: [("N", 0)], NT + 1: [("A", 3)], NT + 2: [("N", 1), ("A", 4)]}
        FFN = [("Q", 0)]
        for i in range(NT + 3):
            if i == GN - 1:
                FFN.append(("Q", 1))
            FFN += [(u, i - behind) for u, behind in STAGES if 0 <= i - behind < NT]
            FFN += AFTER.get(i, [])
        PAIRS = [4, 2, 6, 0]
        pair_of, user_before = {}, {}
        on_pair = [u for u in FFN if u[0] != "D"]
        for k, u in enumerate(on_pair):
            pair_of[u] = PAIRS[k % 4]
            user_before[u] = on_pair[k - 4] if k >= 4 else None
        Y0_PAIR = [6, 0, 2, 6, 0, 2, 6, 0]
        FIRST_OF = [(0, 1), (2, 3), (4, 5), (6,), (7,)]
        first_bank = {m: pair_of["A", n] + m % 2 for n, ms in enumerate(FIRST_OF) for m in ms}

        @block.sync
        def _(sp):
            sp.dma_start(xr[:, 0:GN, :], x[0:GT, :].rearrange("(n p) d -> p n d", p=P)).then_inc(ld_x[0], 16)
            sp.dma_start(cst[:, :, :], consts).then_inc(ld_const, 16)
            sp.dma_start(cT_raw[:, :, :], ctx_t.rearrange("(c p) n -> p c n", p=P)).then_inc(ld_ctx, 16)
            sp.dma_start(xr[:, GN:NT, :], x[GT:T, :].rearrange("(n p) d -> p n d", p=P)).then_inc(ld_x[1], 16)
            sp.dma_start(ids_row[:, :], ids.rearrange("(a t) -> a t", a=1).broadcast_to([P, T])).then_inc(ld_ids, 16)
            sp.dma_start(ids_col[:, :], ids.rearrange("(n p) -> p n", p=P),
                         allow_slow_non_contiguous=True).then_inc(ld_ids, 16)
            sp.dma_start(gl[:, 0:2], g_xattn.rearrange("(a t) -> a t", a=1).broadcast_to([P, 2])).then_inc(ld_gates, 16)
            sp.dma_start(gl[:, 2:4], g_ffn.rearrange("(a t) -> a t", a=1).broadcast_to([P, 2])).then_inc(ld_gates, 16)
            for i, (w, c) in enumerate(((w_gate_t, DC), (w_up_t, DC), (w_down_t, IC))):
                sp.dma_start(wraw[i][:, :].rearrange("p (c n) -> p c n", c=c),
                             w.rearrange("(c p) n -> p c n", p=P)).then_inc(ld_w[i], 16)
            for i in range(2):
                sp.dma_start(wqk_raw[i][:, :, :, :], w_qk[i]).then_inc(ld_qk[i], 16)
                sp.dma_start(wv_raw[i][:, :, :], w_v[i]).then_inc(ld_wv[i], 16)
                sp.dma_start(wo_raw[i][:, :], w_o[i]).then_inc(ld_wo[i], 16)
            sp.dma_start(fc1_raw[:, :, :], fc1_t.rearrange("(c p) n -> p c n", p=P)).then_inc(ld_small, 16)
            sp.dma_start(gw_raw[:, :, :], gate_w_t.rearrange("(c p) n -> p c n", p=P)).then_inc(ld_small, 16)
            sp.dma_start(fc2[:, :], fc2_t).then_inc(ld_small, 16)
            sp.dma_start(gbias[:, :], gate_bias.rearrange("(a t) -> a t", a=1).broadcast_to([P, E])).then_inc(ld_small, 16)
            def reload(i, j, pair):
                b = j % 2
                sp.wait_ge(qk_split, i + 1)
                sp.dma_start(wqk_raw[b][:, :, :, :], w_qk[i + 2]).then_inc(ld_qk[b], 16)
                if pair is not None:
                    sp.wait_ge(wv_split, pair + 1)
                    sp.dma_start(wv_raw[j // 2][:, :, :], w_v[pair + 2]).then_inc(ld_wv[j // 2], 16)
                sp.wait_ge(wo_split, i + 1)
                sp.dma_start(wo_raw[b][:, :], w_o[i + 2]).then_inc(ld_wo[b], 16)

            with sp.Fori(0, LOOPED // 4) as i:
                for j in range(4):
                    reload(i * 4 + j, j, None if j % 2 else i * 2 + j // 2)
            for j in range(2):
                reload(LOOPED + j, j, None)
            sp.wait_ge(y2_filled, 4)
            sp.dma_start(su_raw[:, :, :], shared_up_t.rearrange("(c p) n -> p c n", p=P)).then_inc(ld_shared, 16)
            sp.dma_start(sd[:, :, :], shared_down_t.rearrange("(c p) n -> p c n", p=P)).then_inc(ld_shared, 16)
            for i in range(2):
                sp.dma_start(w1_raw[i][:, :, :], w1_t[2 * i:2 * i + 2].rearrange("e p n -> p e n")).then_inc(ld_w1[i], 16)
                sp.dma_start(w2[i][:, :, :], w2_t[2 * i:2 * i + 2].rearrange("e p n -> p e n")).then_inc(ld_w2[i], 16)
            sp.wait_ge(cwT_done, 1)
            for n in range(NT):
                sp.dma_start(cw_scratch[:, n * P:(n + 1) * P],
                             cwT[(n % GN) * E:(n % GN + 1) * E, (n // GN) * P:(n // GN + 1) * P]).then_inc(cw_stored, 16)
            sp.wait_ge(cw_stored, 16 * NT)
            for j in range(4):
                sp.dma_start(cw_row[j][:, :], cw_scratch[j:j + 1, :].broadcast_to([P, T])).then_inc(ld_cw[j], 16)
            with sp.Fori(0, E // 4 - 1) as i:
                for b in range(2):
                    sp.wait_ge(w1_split, i * 2 + b + 1)
                    sp.dma_start(w1_raw[b][:, :, :], w1_t[bass.ds(i * 4 + (2 * b + 4), 2)].rearrange("e p n -> p e n")).then_inc(ld_w1[b], 16)
                    for j in (2 * b, 2 * b + 1):
                        sp.wait_ge(wa_done, i * 4 + j + 1)
                        sp.dma_start(cw_row[j][:, :], cw_scratch[bass.ds(i * 4 + (j + 4), 1), :].broadcast_to([P, T])).then_inc(ld_cw[j], 16)
                    sp.wait_ge(down_done, i * 4 + 2 * b + 2)
                    sp.dma_start(w2[b][:, :, :], w2_t[bass.ds(i * 4 + (2 * b + 4), 2)].rearrange("e p n -> p e n")).then_inc(ld_w2[b], 16)
            for g in range(NG):
                sp.wait_ge(y4_taken, GN * (g + 1))
                sp.dma_start(out[g * GT:(g + 1) * GT, :].rearrange("(n p) d -> p n d", p=P),
                             xr[:, g * GN:(g + 1) * GN, :]).then_inc(out_stored, 16)
            sp.wait_ge(out_stored, 16 * NG)

        @block.gpsimd
        def _(pool):
            steps = [0]

            def own(ins):
                steps[0] += 1
                ins.then_inc(pool_step, 1)
                pool.wait_ge(pool_step, steps[0])

            nc.gpsimd.memset(ones[:, :], 1.0).then_inc(set_up, 1)
            nc.gpsimd.memset(zeros[:, :].bitcast(F32), 0.0).then_inc(set_up, 1)

            def high(dst, src):
                return nc.gpsimd.tensor_tensor(dst, src, zeros[:, 0:1].bitcast(F32).to_broadcast([P, src.shape[1]]), ALU.add)

            pool.wait_ge(ld_ids, 32)
            for e in range(1, NB):
                nc.gpsimd.tensor_scalar(ge_row[:, e - 1, :], ids_row[:, :], float(e * TOK_PER_EXPERT), None, ALU.is_ge)\
                    .then_inc(masks_ready, 1)

            def first_weights():
                for b in range(2):
                    pool.wait_ge(ld_qk[b], 16)
                    own(nc.gpsimd.tensor_copy(wqk_hi[b][:, :, :, :], wqk_raw[b][:, :, :, :]))
                    nc.gpsimd.tensor_tensor(wqk_lo[b][:, :, :, :], wqk_raw[b][:, :, :, :],
                                            wqk_hi[b][:, :, :, :].bitcast(F32), ALU.subtract).then_inc(qk_split, 1)
                pool.wait_ge(ld_wv[0], 16)
                own(nc.gpsimd.tensor_copy(wv_hi[:, :, :], wv_raw[0][:, :, :]))
                nc.gpsimd.tensor_tensor(wv_lo[:, :, :], wv_raw[0][:, :, :], wv_hi[:, :, :].bitcast(F32), ALU.subtract).then_inc(wv_split, 1)

            for i in range(3):
                if i == 2:
                    first_weights()
                pool.wait_ge(wscale_done, 1)
                own(nc.gpsimd.tensor_scalar(wraw[i][:, :], wraw[i][:, :], wscale[:, i:i + 1], ROUND, ALU.mult, ALU.add))
                own(nc.gpsimd.tensor_scalar(wraw[i][:, :], wraw[i][:, :], ROUND + 1.0, ROUND - 1.0, ALU.min, ALU.max))
                nc.gpsimd.tensor_scalar(wq8[i][:, :], wraw[i][:, :], -ROUND, 1.0, ALU.add, ALU.mult).then_inc(w_ternary, 1)

            pool.wait_ge(ld_small, 64)
            nc.gpsimd.tensor_copy(gw_hi[:, :, :], gw_raw[:, :, :])
            own(nc.gpsimd.tensor_copy(fc1_hi[:, :, :], fc1_raw[:, :, :]))
            nc.gpsimd.tensor_tensor(gw_lo[:, :, :], gw_raw[:, :, :], gw_hi[:, :, :].bitcast(F32), ALU.subtract)
            nc.gpsimd.tensor_tensor(fc1_lo[:, :, :], fc1_raw[:, :, :], fc1_hi[:, :, :].bitcast(F32), ALU.subtract).then_inc(small_split, 1)

            for n in range(NT):
                pool.wait_ge(inner_done, n + 1)
                if n:
                    pool.wait_ge(fly_done, n)
                half = INTER // 2
                src = inner[:, n % 2, :]
                nc.gpsimd.tensor_tensor(fly[:, 0:half], src[:, 0:half], src[:, half:INTER], ALU.add)
                nc.gpsimd.tensor_tensor(fly[:, half:INTER], src[:, 0:half], src[:, half:INTER], ALU.subtract).then_inc(fly_step, 1)
                pool.wait_ge(fly_step, n + 1)
                f = fly[:, :].rearrange("p (a two c) -> p a two c", a=2, two=2)
                d = src.rearrange("p (a two c) -> p a two c", a=2, two=2)
                nc.gpsimd.tensor_tensor(d[:, :, 0], f[:, :, 0], f[:, :, 1], ALU.add)
                nc.gpsimd.tensor_tensor(d[:, :, 1], f[:, :, 0], f[:, :, 1], ALU.subtract).then_inc(fly_done, 1)

            def attend(i):
                for b in range(NB):
                    pool.wait_ge(rsum_done, i * NB + b + 1)
                    nc.gpsimd.tensor_tensor(probs[:, b, :, :], probs[:, b, :, :],
                                            rsum[:, b, :].unsqueeze(2).to_broadcast([P, 2, S]), ALU.mult).then_inc(probs_done, 1)

            def split_weights(par, load, qk, count):
                if qk:
                    pool.wait_ge(ld_qk[par], load + 32)
                    high(wqk_hi[par][:, :, :, :].rearrange("p w c n -> p (w c n)"), wqk_raw[par][:, :, :, :].rearrange("p w c n -> p (w c n)")).then_inc(pool_step, 1)
                pool.wait_ge(ld_wo[par], load + 16)
                high(wo_hi[par][:, :], wo_raw[par][:, :]).then_inc(pool_step, 1)
                pool.wait_ge(pool_step, count)
                if qk:
                    nc.gpsimd.tensor_tensor(wqk_lo[par][:, :, :, :], wqk_raw[par][:, :, :, :],
                                            wqk_hi[par][:, :, :, :].bitcast(F32), ALU.subtract).then_inc(qk_split, 1)
                nc.gpsimd.tensor_tensor(wo_lo[par][:, :], wo_raw[par][:, :], wo_hi[par][:, :].bitcast(F32),
                                        ALU.subtract).then_inc(wo_split, 1)

            def split_values(b, load, read, count):
                pool.wait_ge(ld_wv[b], load)
                pool.wait_ge(unit_filled, read)
                high(wv_hi[:, :, :].rearrange("p c n -> p (c n)"), wv_raw[b][:, :, :].rearrange("p c n -> p (c n)")).then_inc(pool_step, 1)
                pool.wait_ge(pool_step, count)
                nc.gpsimd.tensor_tensor(wv_lo[:, :, :], wv_raw[b][:, :, :], wv_hi[:, :, :].bitcast(F32), ALU.subtract).then_inc(wv_split, 1)

            steps[0] += 1
            split_values(1, 16, len(FIRST), steps[0])
            base = steps[0]
            with pool.Fori(0, LOOPED // 4) as i:
                for j in range(4):
                    attend(i * 4 + j)
                    split_weights(j % 2, i * 32 + 16 * (j // 2), True, i * 10 + (base + 2 * j + 2 + j // 2))
                    if j % 2:
                        split_values(j // 2, i * 16 + 32, filled(i * 4 + j, "V1"), i * 10 + (base + 2 * j + 3 + j // 2))
            steps[0] = base + 10 * (LOOPED // 4)
            for j in range(4):
                attend(LOOPED + j)
                steps[0] += 2 if j < 2 else 1
                split_weights(j % 2, 8 * LOOPED + 16 * (j // 2), j < 2, steps[0])

            pool.wait_ge(y2_filled, 4)
            nc.gpsimd.memset(before[:, :, :], 0.0).then_inc(set_up, 1)
            pool.wait_ge(set_up, 3)
            for a in range(1, NGRP):
                last = nc.gpsimd.memset(before[:, a, 0:a], 1.0)
            last.then_inc(set_up, 1)
            pool.wait_ge(ld_shared, 32)
            own(nc.gpsimd.tensor_copy(su_hi[:, :, :], su_raw[:, :, :]))
            nc.gpsimd.tensor_tensor(su_lo[:, :, :], su_raw[:, :, :], su_hi[:, :, :].bitcast(F32), ALU.subtract).then_inc(su_split, 1)

            def split_w1(b, landed, count):
                pool.wait_ge(ld_w1[b], landed)
                high(w1_hi[b][:, :, :].rearrange("p e n -> p (e n)"), w1_raw[b][:, :, :].rearrange("p e n -> p (e n)")).then_inc(pool_step, 1)
                pool.wait_ge(pool_step, count)
                nc.gpsimd.tensor_tensor(w1_lo[b][:, :, :], w1_raw[b][:, :, :], w1_hi[b][:, :, :].bitcast(F32),
                                        ALU.subtract).then_inc(w1_split, 1)

            base = steps[0]
            for b in range(2):
                split_w1(b, 16, base + b + 1)
            with pool.Fori(0, E // 4 - 1) as i:
                for b in range(2):
                    pool.wait_ge(up_filled, i * 4 + 2 * b + 2)
                    split_w1(b, i * 16 + 32, i * 2 + (base + b + 3))

        @block.scalar
        def _(act):
            def norm_hi(k, g, bank):
                act.wait_ge(hT_filled, k * NG + g + 1)
                nc.scalar.activation(hT_hi[:, :, g * GT:(g + 1) * GT], ps[:, bank:bank + 2, :], ACT.Copy).then_inc(hT_hi_done, 1)

            act.wait_ge(ld_ctx, 16)
            nc.scalar.activation(cT_hi[:, :, :], cT_raw[:, :, :], ACT.Copy).then_inc(ctx_hi_done, 1)
            norm_hi(0, 0, 0)

            def sum_weight(i):
                act.wait_ge(ld_w[i], 16)
                return nc.scalar.activation(wq8[i][:, :], wraw[i][:, :], ACT.Abs, accum_out=wsum[:, i:i + 1])

            def first_expert(g):
                act.wait_ge(a_filled, NB * g + 1)
                nc.scalar.activation(a_sel[:, g, :, :], ps[:, 2:4, :], ACT.Copy).then_inc(a_first_copied, 1)

            sum_weight(0)
            sum_weight(1)
            first_expert(0)
            act.wait_ge(ld_gates, 32)
            nc.scalar.activation(tg[:, :], gl[:, :], ACT.Tanh).then_inc(tanh_done, 1)
            norm_hi(0, 1, 0)
            sum_weight(2).then_inc(wsum_done, 1)
            act.wait_ge(ld_const, 16)
            nc.scalar.activation(had[:, :, :].rearrange("p a n -> p (a n)"), cst[:, 1:5, :].rearrange("p a n -> p (a n)"), ACT.Copy)\
                .then_inc(had_copied, 1)
            for g in range(NG):
                if g:
                    first_expert(g)
                act.wait_ge(a_taken, (NB - 1) * (g + 1))
                nc.scalar.activation(a_silu[:, :, :], a_sel[:, g, :, :], ACT.Silu).then_inc(a_silu_done, 1)
                act.wait_ge(z_ready, g + 1)
                nc.scalar.activation(z_hi[:, g, :, :], a_sel[:, g, :, :], ACT.Copy).then_inc(z_hi_done, 1)

            def tokens_back(g):
                act.wait_ge(q1T_filled, g + 1)
                b = pair_of["Q", g]
                nc.scalar.activation(qT[:, g, :, :], ps[:, b:b + 2, :], ACT.Copy, bias=-ROUND).then_inc(q1T_done, 1)

            def unit_dst(kind, half, par):
                if kind == "Q":
                    return qT_hi[par][:, half * GT:(half + 1) * GT], QK_SCALE
                if kind == "K":
                    return kT_hi[par][:, half * GT:(half + 1) * GT], 1.0
                if kind == "V":
                    return v_hi[par][:, 2 * half:2 * half + 2, :, :].rearrange("p n a d -> p (n a d)"), 1.0
                if kind == "T":
                    return pT_hi[:, half, :, :], 1.0
                return oT_hi[:, half * GT:(half + 1) * GT], 1.0

            def high_part(u, bank, par, at):
                act.wait_ge(unit_filled, at)
                dst, scale = unit_dst(u[0], int(u[1]), par)
                nc.scalar.activation(dst, ps[:, bank, :], ACT.Copy, scale=scale).then_inc(hi_done, 1)

            def attend(i, j, at=None):
                for u in ring_of(at):
                    if u[0] == "S":
                        b = int(u[1])
                        act.wait_ge(max_done, i * NB + b + 1)
                        for t in range(2):
                            last = nc.scalar.activation(probs[:, b, t, :], ps[:, BANK[u], t * S:(t + 1) * S], ACT.Exp,
                                                        bias=nmax[:, b, t:t + 1], accum_out=esum[:, b, t:t + 1])
                        last.then_inc(exp_done, 1)
                    else:
                        name, slot = place(u, j)
                        high_part(name, BANK[u], slot, filled(i, u, at))

            tokens_back(0)
            for i in range(NT + 3):
                if i < NT:
                    act.wait_ge(gate_filled, i + 1)
                    b = pair_of["G", i]
                    nc.scalar.activation(inner[:, i % 2, :], ps[:, b:b + 2, :], ACT.Silu, scale=c_gate[:, i:i + 1])\
                        .then_inc(silu_done, 1)
                if i == GN - 1:
                    tokens_back(1)
                if 0 <= i - 3 < NT:
                    act.wait_ge(q2T_filled, i - 2)
                    b = pair_of["C", i - 3]
                    nc.scalar.activation(q2T[:, :, :], ps[:, b:b + 2, :], ACT.Copy, bias=-ROUND).then_inc(q2T_done, 1)
                if 0 <= i - 1 < NT:
                    act.wait_ge(fT_filled, i)
                    b = pair_of["F", i - 1]
                    nc.scalar.activation(fT_hi[:, :, :], ps[:, b:b + 2, :], ACT.Copy).then_inc(fT_hi_done, 1)
                if 0 <= i - 2 < NT:
                    act.wait_ge(s2_ready, i - 1)
                    b = pair_of["H", i - 2]
                    nc.scalar.activation(q2[:, :], ps[:, b:b + 2, :], ACT.Copy,
                                         scale=am2[:, i % 2, 2:3], bias=ROUND).then_inc(q2_done, 1)
                for u, n in AFTER.get(i, []):
                    if u == "N":
                        norm_hi(1, n, pair_of["N", n])
                    else:
                        for m in FIRST_OF[n]:
                            high_part(FIRST[m], first_bank[m], 0, m + 1)

            with act.Fori(0, LOOPED // 4) as i:
                for j in range(4):
                    attend(i * 4 + j, j)
            for j in range(4):
                attend(LOOPED + j, j, LOOPED + j)

            norm_hi(2, 0, 0)
            norm_hi(2, 1, 4)
            act.wait_ge(logit_filled, NG)
            nc.scalar.activation(sc[:, :, :], ps[:, 2, 0:NT * E].rearrange("p (n e) -> p n e", e=E), ACT.Sigmoid).then_inc(sc_done, 1)
            for g in range(NG):
                act.wait_ge(xl_filled, g + 1)
                nc.scalar.activation(xl_hi[:, g * GT:(g + 1) * GT], ps[:, XL_BANK[g], :], ACT.Copy).then_inc(xl_hi_done, 1)
            for n in range(NG * SC):
                act.wait_ge(su_filled, n + 1)
                nc.scalar.activation(s_relu[:, n % 2, :], ps[:, 4 + n % SC, :], ACT.Relu).then_inc(su_relu, 1)
                act.wait_ge(su_relu, n + 1)
                nc.scalar.activation(s_act[:, n % SC, n // SC * GT:(n // SC + 1) * GT], s_relu[:, n % 2, :], ACT.Square)\
                    .then_inc(su_taken, 1)

            act.wait_ge(cwT_filled, 1)
            nc.scalar.activation(cwT[:, :], ps[:, 2, 0:NG * P], ACT.Copy).then_inc(cwT_done, 1)

            def expert(e, j, first):
                act.wait_ge(up_filled, e + (j + 1))
                if not (first and j < 2):
                    act.wait_ge(e_z_done, e + (j - 1))
                nc.scalar.activation(e_relu[j % 2][:, :], ps[:, 4 + 2 * (j % 2):6 + 2 * (j % 2), :], ACT.Relu).then_inc(relu_done, 1)

            for j in range(4):
                expert(0, j, True)
            with act.Fori(1, E // 4) as i:
                for j in range(4):
                    expert(i * 4, j, False)
            act.wait_ge(down_done, E)
            nc.scalar.activation(yl[:, :], ps[:, 0:2, :], ACT.Copy).then_inc(yl_done, 1)

        @block.vector
        def _(dve):
            steps = [0]
            V = nc.vector

            def own(ins):
                steps[0] += 1
                ins.then_inc(dve_step, 1)
                dve.wait_ge(dve_step, steps[0])

            def stats(n):
                return V.bn_stats(st[:, n, :], xr[:, n, :])

            def factors(t0, t1):
                for n in range(t0, t1):
                    last = V.bn_aggr(mv[:, n, :], st[:, n, :])
                own(last)
                v, y, t = ln_v[:, t0:t1], ln_y[:, t0:t1], ln_t[:, t0:t1]
                own(V.tensor_scalar(v, mv[:, t0:t1, 1], LN_EPS, None, ALU.add))
                own(V.tensor_scalar(ln_i[:, t0:t1], v.bitcast(I32), 1, None, ALU.logical_shift_right))
                own(V.tensor_scalar(y.bitcast(I32), ln_i[:, t0:t1], -1.0, RSQRT_GUESS, ALU.mult, ALU.add))
                for _ in range(3):
                    own(V.scalar_tensor_tensor(t, y, 0.5, y, ALU.mult, ALU.mult))
                    own(V.tensor_tensor(t, t, v, ALU.mult))
                    own(V.scalar_tensor_tensor(y, t, 1.5, y, ALU.subtract, ALU.mult))

            def scaled(g):
                for n in range(g * GN, (g + 1) * GN):
                    last = V.tensor_scalar(h[:, n, :], xr[:, n, :], mv[:, n, 0:1], ln_y[:, n:n + 1], ALU.subtract, ALU.mult)
                return last

            def norm(g, counted=0):
                for n in range(g * GN + counted, (g + 1) * GN):
                    last = stats(n)
                own(last)
                factors(g * GN, (g + 1) * GN)
                return scaled(g)

            def norm_lo(k, g, bank):
                dve.wait_ge(hT_hi_done, k * NG + g + 1)
                s = slice(g * GT, (g + 1) * GT)
                V.tensor_tensor(hT_lo[:, :, s], ps[:, bank:bank + 2, :], hT_hi[:, :, s].bitcast(F32), ALU.subtract).then_inc(hT_done, 1)

            dve.wait_ge(ld_x[0], 16)
            norm(0).then_inc(h_ready, 1)
            dve.wait_ge(ctx_hi_done, 1)
            V.tensor_tensor(cT_lo[:, :, :], cT_raw[:, :, :], cT_hi[:, :, :].bitcast(F32), ALU.subtract).then_inc(ctx_done, 1)
            norm_lo(0, 0, 0)
            dve.wait_ge(ld_x[1], 16)
            norm(1).then_inc(h_ready, 1)

            dve.wait_ge(ld_ids, 32)
            for e in range(1, NB):
                last = V.tensor_scalar(ge_col[:, e - 1, :], ids_col[:, :], float(e * TOK_PER_EXPERT), None, ALU.is_ge)
            own(last)
            V.tensor_scalar(tgm[:, 0, :], ge_col[:, 0, :], -1.0, 1.0, ALU.mult, ALU.add)
            for e in range(1, NB - 1):
                V.tensor_tensor(tgm[:, e, :], ge_col[:, e - 1, :], ge_col[:, e, :], ALU.subtract)
            own(V.tensor_copy(tgm[:, NB - 1, :], ge_col[:, NB - 2, :]))

            def gates_and_means():
                dve.wait_ge(tanh_done, 1)
                own(V.tensor_scalar(tgm[:, :, :], tgm[:, :, :], tg[:, 0:1], None, ALU.mult))
                dve.wait_ge(wtot_filled, 1)
                own(V.tensor_scalar(wmean[:, :], ps[:, 7, 0:3], 1.0 / W_COUNT, Q_EPS, ALU.mult, ALU.max))
                V.tensor_scalar(fdown[:, :], wmean[:, 2:3], tg[:, 2:3], 1.0 / 128.0, ALU.mult, ALU.mult)
                V.reciprocal(wscale[:, :], wmean[:, :]).then_inc(wscale_done, 1)

            for g in range(NG):
                s = slice(g * GT, (g + 1) * GT)
                for e in range(1, NB):
                    dve.wait_ge(a_filled, NB * g + e + 1)
                    if e == 1:
                        dve.wait_ge(a_first_copied, g + 1)
                        dve.wait_ge(masks_ready, NB - 1)
                    b = 2 + 2 * (e % 2)
                    for c in range(DC):
                        last = V.copy_predicated(a_sel[:, g, c, :], ge_row[:, e - 1, s], ps[:, b + c, :])
                    last.then_inc(a_taken, 1)
                    if g == 0 and e == 1:
                        norm_lo(0, 1, 0)
                    if g == 0 and e == 3:
                        gates_and_means()
                    dve.wait_ge(a_taken, (NB - 1) * g + e)
                dve.wait_ge(a_silu_done, g + 1)
                V.tensor_tensor(a_sel[:, g, :, :], a_sel[:, g, :, :], a_silu[:, :, :], ALU.mult).then_inc(z_ready, 1)
                dve.wait_ge(z_hi_done, g + 1)
                V.tensor_tensor(z_lo[:, g, :, :], a_sel[:, g, :, :], z_hi[:, g, :, :].bitcast(F32), ALU.subtract).then_inc(z_done, 1)

            def add_experts(tiles, counted=None):
                before = {}
                for e in range(NB):
                    for n in tiles:
                        if e == 0:
                            dve.wait_ge(y0_filled, n + 1)
                        else:
                            dve.wait_ge(dve_step, before[n])
                        ins = V.scalar_tensor_tensor(xr[:, n, :], ps[:, Y0_PAIR[n] + e // 2, (e % 2) * D:(e % 2 + 1) * D],
                                                     tgm[:, e, n:n + 1], xr[:, n, :], ALU.mult, ALU.add)
                        if e < NB - 1:
                            steps[0] += 1
                            before[n] = steps[0]
                            ins.then_inc(dve_step, 1)
                        else:
                            ins.then_inc(y0_taken, 1)
                    if e == 0 and counted is not None:
                        dve.wait_ge(y0_taken, counted + 1)
                        stats(counted)

            def quantise(g):
                s = slice(g * GN, (g + 1) * GN)
                own(V.tensor_reduce(am[:, s], h[:, s, :], AX.X, ALU.max, apply_absolute_value=True))
                own(V.tensor_scalar(am[:, s], am[:, s], Q_EPS, None, ALU.max))
                own(V.reciprocal(am_r[:, s], am[:, s]))
                own(V.tensor_scalar(am_r[:, s], am_r[:, s], 128.0, None, ALU.mult))
                if g:
                    dve.wait_ge(q1T_filled, g)
                for n in range(GN):
                    last = V.tensor_scalar(qtok[:, n, :], h[:, g * GN + n, :], am_r[:, g * GN + n:g * GN + n + 1], ROUND,
                                           ALU.mult, ALU.add)
                own(last)
                V.tensor_scalar(qtok[:, :, :], qtok[:, :, :], ROUND + 127.0, ROUND - 128.0, ALU.min, ALU.max).then_inc(q1_ready, 1)
                own(V.tensor_scalar(am_c[:, s], am[:, s], 1.0 / 128.0, None, ALU.mult))
                V.tensor_scalar(c_up[:, s], am_c[:, s], wmean[:, 1:2], None, ALU.mult)
                V.tensor_scalar(c_gate[:, s], am_c[:, s], wmean[:, 0:1], None, ALU.mult).then_inc(scales_ready, 1)

            def low_part(u, bank, par, at):
                dve.wait_ge(hi_done, at)
                kind, half = u[0], int(u[1])
                s, n = slice(half * GT, (half + 1) * GT), slice(2 * half, 2 * half + 2)
                src = ps[:, bank, :]
                if kind == "Q":
                    ins = V.scalar_tensor_tensor(qT_lo[par][:, s], src, QK_SCALE, qT_hi[par][:, s].bitcast(F32),
                                                 ALU.mult, ALU.subtract)
                elif kind == "K":
                    ins = V.tensor_tensor(kT_lo[par][:, s], src, kT_hi[par][:, s].bitcast(F32), ALU.subtract)
                elif kind == "V":
                    ins = V.tensor_tensor(v_lo[par][:, n, :, :].rearrange("p n a d -> p (n a d)"), src,
                                          v_hi[par][:, n, :, :].rearrange("p n a d -> p (n a d)").bitcast(F32), ALU.subtract)
                elif kind == "T":
                    ins = V.tensor_tensor(pT_lo[:, half, :, :].rearrange("p c q -> p (c q)"), src,
                                          pT_hi[:, half, :, :].rearrange("p c q -> p (c q)").bitcast(F32), ALU.subtract)
                else:
                    ins = V.tensor_tensor(oT_lo[:, s], src, oT_hi[:, s].bitcast(F32), ALU.subtract)
                ins.then_inc(lo_done, 1)

            def attend(i, j, at=None):
                units = ring_of(at)
                for u in [v for v in units if v[0] == "S"] + [v for v in units if v[0] != "S"]:
                    if u[0] == "S":
                        b = int(u[1])
                        dve.wait_ge(unit_filled, filled(i, u, at))
                        V.tensor_reduce(nmax[:, b, :], ps[:, BANK[u], :].rearrange("p (t k) -> p t k", t=2), AX.X, ALU.max,
                                        negate=True).then_inc(max_done, 1)
                    else:
                        name, slot = place(u, j)
                        low_part(name, BANK[u], slot, split(i, u, at))
                    for b in {"S1": [0], "S2": [1, 2], "K0": [3], "T0": [] if "K0" in units else [3]}.get(u, []):
                        dve.wait_ge(exp_done, i * NB + b + 1)
                        V.reciprocal(rsum[:, b, :], esum[:, b, :]).then_inc(rsum_done, 1)

            for n in range(GN):
                add_experts([n], n - 1 if n else None)
            dve.wait_ge(y0_taken, GN)
            own(norm(0, GN - 1))
            quantise(0)
            add_experts([GN])
            add_experts([GN + 1, GN + 2], GN)
            add_experts([GN + 3], GN + 1)
            dve.wait_ge(y0_taken, NT)
            for i in range(NT + 3):
                if i < NT:
                    b = pair_of["U", i]
                    dve.wait_ge(silu_done, i + 1)
                    dve.wait_ge(up0_filled, i + 1)
                    V.tensor_tensor(inner[:, i % 2, :], inner[:, i % 2, :], ps[:, b:b + 2, :].rearrange("p a n -> p (a n)"),
                                    ALU.mult).then_inc(inner_done, 1)
                if i == 0:
                    own(norm(1, 2))
                if i == 1:
                    quantise(1)
                if 0 <= i - 2 < NT:
                    n = i - 2
                    b, a = pair_of["H", n], am2[:, n % 2, :]
                    dve.wait_ge(had_filled, n + 1)
                    own(V.tensor_reduce(a[:, 0:1], ps[:, b:b + 2, :], AX.XY, ALU.max, apply_absolute_value=True))
                    own(V.tensor_scalar(a[:, 1:2], a[:, 0:1], c_up[:, n:n + 1], Q_EPS, ALU.mult, ALU.max))
                    own(V.reciprocal(a[:, 0:1], a[:, 1:2]))
                    V.tensor_scalar(a[:, 2:3], a[:, 0:1], 128.0, c_up[:, n:n + 1], ALU.mult, ALU.mult).then_inc(s2_ready, 1)
                    V.tensor_scalar(a[:, 3:4], a[:, 1:2], fdown[:, 0:1], None, ALU.mult)
                if 0 <= i - 3 < NT:
                    n = i - 3
                    dve.wait_ge(y1_filled, n + 1)
                    dve.wait_ge(dve_step, steps[0])
                    V.scalar_tensor_tensor(xr[:, n, :], ps[:, pair_of["C", n], 0:D], am2[:, n % 2, 3:4], xr[:, n, :],
                                           ALU.mult, ALU.add).then_inc(y1_taken, 1)
                if 0 <= i - 1 < NT:
                    n = i - 1
                    b = pair_of["F", n]
                    dve.wait_ge(fT_hi_done, n + 1)
                    V.tensor_tensor(fT_lo[:, :, :].rearrange("p c t -> p (c t)"), ps[:, b:b + 2, :].rearrange("p a n -> p (a n)"),
                                    fT_hi[:, :, :].rearrange("p c t -> p (c t)").bitcast(F32), ALU.subtract).then_inc(fT_done, 1)
                if 0 <= i - 2 < NT:
                    dve.wait_ge(q2_done, i - 1)
                    V.tensor_scalar(q2[:, :], q2[:, :], ROUND + 127.0, ROUND - 128.0, ALU.min, ALU.max).then_inc(q2_clipped, 1)
                if 0 <= i - 3 < NT:
                    dve.wait_ge(y1_taken, i - 2)
                    last = stats(i - 3)
                if i == GN + 2:
                    own(last)
                    factors(0, GN)
                if i == GN + 3:
                    scaled(0).then_inc(h_ready, 1)
                if i == NT + 2:
                    own(last)
                    factors(GN, NT)
                    scaled(1).then_inc(h_ready, 1)
                for u, n in AFTER.get(i, []):
                    if u == "N":
                        norm_lo(1, n, pair_of["N", n])
                    else:
                        for m in FIRST_OF[n]:
                            low_part(FIRST[m], first_bank[m], 0, m + 1)

            with dve.Fori(0, LOOPED // 4) as i:
                for j in range(4):
                    attend(i * 4 + j, j)
            for j in range(4):
                attend(LOOPED + j, j, LOOPED + j)

            for n in range(NT):
                dve.wait_ge(y2_filled, n // 2 + 1)
                V.scalar_tensor_tensor(xr[:, n, :], ps[:, 4 + n // 2, (n % 2) * D:(n % 2 + 1) * D], tg[:, 1:2],
                                       xr[:, n, :], ALU.mult, ALU.add).then_inc(y2_taken, 1)
                if n:
                    dve.wait_ge(y2_taken, n)
                    stats(n - 1)
            dve.wait_ge(y2_taken, NT)
            own(stats(NT - 1))
            factors(0, NT)
            for g in range(NG):
                scaled(g).then_inc(h_ready, 1)
            norm_lo(2, 0, 0)
            norm_lo(2, 1, 4)

            dve.wait_ge(sc_done, 1)
            dve.wait_ge(ld_small, 64)
            own(V.tensor_tensor(sbias[:, :, :], sc[:, :, :],
                                gbias[:, :].unsqueeze(1).to_broadcast([P, NT, E]), ALU.add))
            for n in range(NT):
                for q in range(NGRP):
                    last = V.max(gtop[:, n * NGRP + q, :], sbias[:, n, q * EG:(q + 1) * EG])
            own(last)
            for g in range(NG):
                dve.wait_ge(xl_hi_done, g + 1)
                V.tensor_tensor(xl_lo[:, g * GT:(g + 1) * GT], ps[:, XL_BANK[g], :], xl_hi[:, g * GT:(g + 1) * GT].bitcast(F32),
                                ALU.subtract).then_inc(xl_done, 1)
            own(V.tensor_tensor(gscore[:, :, :].rearrange("p n q -> p (n q)"), gtop[:, :, 0], gtop[:, :, 1], ALU.add))
            other = gscore[:, :, :].unsqueeze(2).to_broadcast([P, NT, NGRP, NGRP])
            own_score = gscore[:, :, :].unsqueeze(3).to_broadcast([P, NT, NGRP, NGRP])
            dve.wait_ge(set_up, 4)
            V.tensor_tensor(cmp[:, :, :, :], other, own_score, ALU.is_gt)
            own(V.tensor_tensor(eqs[:, :, :, :], other, own_score, ALU.is_equal))
            own(V.tensor_tensor(eqs[:, :, :, :], eqs[:, :, :, :],
                                before[:, :, :].unsqueeze(1).to_broadcast([P, NT, NGRP, NGRP]), ALU.mult))
            own(V.tensor_tensor(cmp[:, :, :, :], cmp[:, :, :, :], eqs[:, :, :, :], ALU.add))
            own(V.tensor_reduce(grank[:, :, :], cmp[:, :, :, :], AX.X, ALU.add))
            V.memset(masked[:, :, :], -3.0e38)
            own(V.tensor_scalar(gmask[:, :, :], grank[:, :, :], float(TOPG), None, ALU.is_lt))
            own(V.tensor_copy(gmask8[:, :, :].rearrange("p n (q k) -> p (n q) k", k=EG),
                              gmask[:, :, :].rearrange("p n q -> p (n q)").unsqueeze(2).to_broadcast([P, NT * NGRP, EG])))
            own(V.copy_predicated(masked[:, :, :], gmask8[:, :, :], sbias[:, :, :]))
            for n in range(NT):
                last = V.max(top8[:, n, :], masked[:, n, :])
            own(last)
            for n in range(NT):
                last = V.match_replace(left[:, n, :], top8[:, n, :], masked[:, n, :], -3.4e38)
            own(last)
            own(V.tensor_tensor(sel[:, :, :], masked[:, :, :], left[:, :, :], ALU.not_equal))
            own(V.tensor_tensor(wsel[:, :, :], sel[:, :, :], sc[:, :, :], ALU.mult))
            own(V.tensor_reduce(wden[:, :], wsel[:, :, :], AX.X, ALU.add))
            own(V.reciprocal(wden[:, :], wden[:, :]))
            own(V.tensor_scalar(wden[:, :], wden[:, :], ROUTED_SCALE, None, ALU.mult))
            V.tensor_tensor(cw[:, :, :], wsel[:, :, :], wden[:, :].unsqueeze(2).to_broadcast([P, NT, E]), ALU.mult)\
                .then_inc(cw_ready, 1)

            for n in range(NT):
                dve.wait_ge(y3_filled, n // 2 + 1)
                V.scalar_tensor_tensor(xr[:, n, :], ps[:, Y3_BANK[n // 2], (n % 2) * D:(n % 2 + 1) * D], tg[:, 3:4], xr[:, n, :],
                                       ALU.mult, ALU.add).then_inc(y3_taken, 1)

            def expert(e, j, landed, first):
                up = ps[:, 4 + 2 * (j % 2):6 + 2 * (j % 2), :].rearrange("p b t -> p (b t)")
                dve.wait_ge(relu_done, e + (j + 1))
                dve.wait_ge(ld_cw[j], landed)
                V.scalar_tensor_tensor(e_wa[j % 2][:, :], up, 0.0, cw_row[j][:, :], ALU.max, ALU.mult).then_inc(wa_done, 1)
                dve.wait_ge(wa_done, e + (j + 1))
                if not (first and j < 2):
                    dve.wait_ge(down_done, e + (j - 1))
                V.tensor_tensor(e_z[j % 2][:, :], e_wa[j % 2][:, :], e_relu[j % 2][:, :], ALU.mult).then_inc(e_z_done, 1)

            for j in range(4):
                expert(0, j, 16, True)
            with dve.Fori(1, E // 4) as i:
                for j in range(4):
                    expert(i * 4, j, i * 16 + 16, False)
            dve.wait_ge(y3_taken, NT)
            for n in range(NT):
                dve.wait_ge(y4_filled, n // 2 + 1)
                V.scalar_tensor_tensor(xr[:, n, :], ps[:, 4 + n // 2, (n % 2) * D:(n % 2 + 1) * D], tg[:, 3:4], xr[:, n, :],
                                       ALU.mult, ALU.add).then_inc(y4_taken, 1)

        @block.tensor
        def _(pe):
            mm = nc.tensor.matmul

            def product(dst, lhs, rhs, first=True, last=True, check=True):
                (l_hi, l_lo), (r_hi, r_lo) = lhs, rhs
                kw = {} if check else {"skip_group_check": True}
                mm(dst, l_lo, r_hi, start=first, stop=False, **kw)
                mm(dst, l_hi, r_lo, start=False, stop=False, **kw)
                return mm(dst, l_hi, r_hi, start=False, stop=last, **kw)

            def both(hi, lo, *at):
                return hi[at], lo[at]

            A = slice(None)

            def transpose_norm(k, g, bank):
                pe.wait_ge(h_ready, k * NG + g + 1)
                for c in range(DC):
                    for j in range(GN):
                        last = nc.tensor.transpose(ps[:, bank + c, j * P:(j + 1) * P], h[:, g * GN + j, c * P:(c + 1) * P], ident)
                last.then_inc(hT_filled, 1)

            def unit(u, bank, par, j=0):
                kind, half = u[0], int(u[1])
                dst = ps[:, bank, :]
                s = slice(half * GT, (half + 1) * GT)
                if kind in "QK":
                    w = "QK".index(kind)
                    src = (hT_hi, hT_lo) if kind == "Q" else (cT_hi, cT_lo)
                    for c in range(DC):
                        last = product(dst, both(wqk_hi[par], wqk_lo[par], A, w, c, A), both(*src, A, c, s), c == 0, c == DC - 1)
                elif kind == "V":
                    for n in range(2):
                        t = half * 2 + n
                        for c in range(DC):
                            last = product(dst[:, n * 2 * P:(n + 1) * 2 * P], both(cT_hi, cT_lo, A, c, slice(t * P, (t + 1) * P)),
                                           both(wv_hi, wv_lo, A, c, A), c == 0, c == DC - 1)
                elif kind == "S":
                    for t in range(2):
                        q0 = half * S + t * P
                        last = product(dst[:, t * S:(t + 1) * S], both(qT_hi[par], qT_lo[par], A, slice(q0, q0 + P)),
                                       both(kT_hi[par], kT_lo[par], A, slice(half * S, (half + 1) * S)))
                elif kind == "T":
                    for k in range(2):
                        for t in range(2):
                            last = nc.tensor.transpose(dst[:, k * S + t * P:k * S + (t + 1) * P],
                                                       probs[:, half, t, k * P:(k + 1) * P], ident)
                else:
                    pair = j // 2
                    for b in (2 * half, 2 * half + 1):
                        for k in range(2):
                            last = product(dst[:, (b % 2) * S:(b % 2 + 1) * S], both(v_hi[pair], v_lo[pair], A, 2 * b + k, par, A),
                                           both(pT_hi, pT_lo, A, b, k, A), k == 0, k == 1)
                last.then_inc(unit_filled, 1)

            w_gate = wq8[0][:, :].rearrange("p (c n) -> p c n", c=DC)
            w_up = wq8[1][:, :].rearrange("p (c n) -> p c n", c=DC)
            w_down = wq8[2][:, :].rearrange("p (c n) -> p c n", c=IC)

            freed = {"Q": q1T_done, "G": silu_done, "U": inner_done, "C": y1_taken, "H": q2_done, "F": fT_done,
                     "A": lo_done, "N": hT_done}

            def fill(u, n):
                if u != "D":
                    b, user = pair_of[u, n], user_before[u, n]
                    if user:
                        done = user[1] + 1
                        if user[0] == "A":
                            done = FIRST_OF[user[1]][-1] + 1
                        elif user[0] == "N":
                            done += NG
                        pe.wait_ge(freed[user[0]], done)
                    else:
                        pe.wait_ge(a_taken, (NB - 1) * NG)
                        if b in Y0_PAIR:
                            pe.wait_ge(y0_taken, NT - Y0_PAIR[::-1].index(b))
                if u == "Q":
                    pe.wait_ge(q1_ready, n + 1)
                    for c in range(DC):
                        for j in range(GN):
                            last = nc.tensor.transpose(ps[:, b + c, j * P:(j + 1) * P], qtok[:, j, c * P:(c + 1) * P], ident)
                    last.then_inc(q1T_filled, 1)
                elif u in "GU":
                    pe.wait_ge(q1T_done, n // GN + 1)
                    pe.wait_ge(scales_ready, n // GN + 1)
                    pe.wait_ge(w_ternary, 1 if u == "G" else 2)
                    w = w_gate if u == "G" else w_up
                    for half in range(2):
                        for d in range(DC):
                            last = mm(ps[:, b + half, :], qT[:, n // GN, d, n % GN * P:(n % GN + 1) * P],
                                      w[:, d, half * 512:(half + 1) * 512], start=(d == 0), stop=(d == DC - 1))
                    last.then_inc(gate_filled if u == "G" else up0_filled, 1)
                elif u == "F":
                    pe.wait_ge(fly_done, n + 1)
                    for c in range(IC):
                        last = nc.tensor.transpose(ps[:, b + c // 4, (c % 4) * P:(c % 4 + 1) * P], inner[:, n % 2, c * P:(c + 1) * P], ident)
                    last.then_inc(fT_filled, 1)
                elif u == "H":
                    pe.wait_ge(fT_done, n + 1)
                    pe.wait_ge(had_copied, 1)
                    for k in range(IC // 2):
                        dst = ps[:, b + k // 2, (k % 2) * 2 * P:(k % 2 + 1) * 2 * P]
                        for m, part in enumerate((fT_lo, fT_hi)):
                            for a in range(2):
                                last = mm(dst, part[:, 2 * k + a, :], had[:, a, :], start=(m + a == 0), stop=(m + a == 2))
                    last.then_inc(had_filled, 1)
                elif u == "N":
                    transpose_norm(1, n, b)
                elif u == "A":
                    pe.wait_ge(qk_split, 1)
                    pe.wait_ge(wv_split, 1)
                    if n >= 3:
                        pe.wait_ge(hT_done, NG + n - 2)
                    for m in FIRST_OF[n]:
                        unit(FIRST[m], first_bank[m], 0)
                elif u == "C":
                    pe.wait_ge(q2_clipped, n + 1)
                    for c in range(IC):
                        last = nc.tensor.transpose(ps[:, b + c // 4, (c % 4) * P:(c % 4 + 1) * P], q2[:, c * P:(c + 1) * P], ident)
                    last.then_inc(q2T_filled, 1)
                else:
                    pe.wait_ge(q2T_done, n + 1)
                    pe.wait_ge(w_ternary, 3)
                    for c in range(IC):
                        last = mm(ps[:, pair_of["C", n], 0:D], q2T[:, c, :], w_down[:, c, :], start=(c == 0), stop=(c == IC - 1))
                    last.then_inc(y1_filled, 1)

            pe.wait_ge(ld_const, 16)
            transpose_norm(0, 0, 0)
            pe.wait_ge(ctx_done, 1)
            for g in range(NG):
                pe.wait_ge(hT_done, g + 1)
                for e in range(NB):
                    if e >= 2 or g:
                        before_e = (e - 2) % NB
                        before_g = g if e >= 2 else g - 1
                        if before_e == 0:
                            pe.wait_ge(a_first_copied, before_g + 1)
                        else:
                            pe.wait_ge(a_taken, (NB - 1) * before_g + before_e)
                    for f in range(DC):
                        for c in range(DC):
                            last = product(ps[:, 2 + 2 * (e % 2) + f, :],
                                           both(cT_hi, cT_lo, A, c, slice(e * S + f * P, e * S + (f + 1) * P)),
                                           both(hT_hi, hT_lo, A, c, slice(g * GT, (g + 1) * GT)), c == 0, c == DC - 1)
                    last.then_inc(a_filled, 1)
                    if g == 0 and e == 1:
                        transpose_norm(0, 1, 0)
                    if g == 0 and e == 2:
                        pe.wait_ge(set_up, 2)
                        pe.wait_ge(wsum_done, 1)
                        mm(ps[:, 7, 0:3], ones[:, :], wsum[:, :], start=True, stop=True).then_inc(wtot_filled, 1)
            for g in range(NG):
                pe.wait_ge(z_done, g + 1)
                for n in range(g * GN, (g + 1) * GN):
                    if n == NT - 1:
                        fill("Q", 0)
                    if n == 0:
                        pe.wait_ge(wscale_done, 1)
                    elif n == 2:
                        pe.wait_ge(a_taken, (NB - 1) * NG)
                    elif n >= 3:
                        pe.wait_ge(y0_taken, n - 2)
                    for b in range(2):
                        for c in range(DC):
                            last = product(ps[:, Y0_PAIR[n] + b, :],
                                           both(z_hi, z_lo, A, g, c, slice((n - g * GN) * P, (n - g * GN + 1) * P)),
                                           both(cT_hi, cT_lo, A, c, slice(b * 2 * S, (b + 1) * 2 * S)), c == 0, c == DC - 1)
                    last.then_inc(y0_filled, 1)

            for u, n in FFN[1:]:
                fill(u, n)

            def add_head(half, par, o_split, w_split, final=False):
                pe.wait_ge(wo_split, w_split)
                pe.wait_ge(lo_done, o_split)
                for n in range(half * GN, (half + 1) * GN):
                    last = product(ps[:, 4 + n // 2, (n % 2) * D:(n % 2 + 1) * D],
                                   both(oT_hi, oT_lo, A, slice(n * P, (n + 1) * P)), (wo_hi[par][:, :], wo_lo[par][:, :]),
                                   False, final and n % 2 == 1, check=False)
                    if final and n % 2:
                        last.then_inc(y2_filled, 1)

            def attend(i, j, pair, at=None, later=True):
                units = ring_of(at)
                before_step = ring_of(at - 1 if at else None)
                for u in STEP:
                    if u[0] == "Y":
                        if later:
                            add_head(int(u[1]), 1 - j % 2, split_before(i, "O" + u[1], at), i)
                        continue
                    if u not in units:
                        continue
                    earlier = [v for v in units[:units.index(u)] if BANK[v] == BANK[u]]
                    if not earlier:
                        pe.wait_ge(lo_done, split_before(i, [v for v in before_step if BANK[v] == BANK[u]][-1], at))
                    elif earlier[-1][0] == "S":
                        pe.wait_ge(exp_done, i * NB + int(earlier[-1][1]) + 1)
                    else:
                        pe.wait_ge(lo_done, split(i, earlier[-1], at))
                    if u in ("S0", "S2"):
                        pe.wait_ge(lo_done, split_before(i, "Q" + str(int(u[1]) // 2), at))
                    if u == "K0":
                        pe.wait_ge(qk_split, i + 2)
                    if u == "V0":
                        pe.wait_ge(wv_split, pair + 2)
                    if u[0] == "T":
                        pe.wait_ge(probs_done, i * NB + int(u[1]) + 1)
                    if u[0] == "O":
                        pe.wait_ge(lo_done, split(i, "T" + str(2 * int(u[1]) + 1), at))
                    name, slot = place(u, j)
                    unit(name, BANK[u], slot, j)

            pe.wait_ge(y1_taken, NT)
            pe.wait_ge(hT_done, 2 * NG)
            pe.wait_ge(lo_done, len(FIRST))
            for b in range(4):
                mm(ps[:, 4 + b, :], zeros[:, 0:P], zeros[:, :], start=True, stop=False, skip_group_check=True)
            for j in range(4):
                attend(j, j, j // 2, j, later=j > 0)
            with pe.Fori(1, LOOPED // 4) as i:
                for j in range(4):
                    attend(i * 4 + j, j, i * 2 + j // 2)
            for j in range(4):
                attend(LOOPED + j, j, (LOOPED + j) // 2, LOOPED + j)
            for half in range(2):
                add_head(half, 1, split(NH - 1, "O" + str(half), NH - 1), NH, final=True)

            pe.wait_ge(lo_done, split(NH - 1, "O1", NH - 1))
            pe.wait_ge(small_split, 1)
            transpose_norm(2, 0, 0)
            pe.wait_ge(y2_taken, NT)
            transpose_norm(2, 1, 4)
            for g in range(NG):
                pe.wait_ge(hT_done, 2 * NG + g + 1)
                for n in range(g * GN, (g + 1) * GN):
                    for c in range(DC):
                        last = product(ps[:, 2, n * E:(n + 1) * E], both(hT_hi, hT_lo, A, c, slice(n * P, (n + 1) * P)),
                                       both(gw_hi, gw_lo, A, c, A), c == 0, c == DC - 1)
                last.then_inc(logit_filled, 1)
            for g in range(NG):
                for c in range(DC):
                    last = product(ps[:, XL_BANK[g], :], both(fc1_hi, fc1_lo, A, c, A),
                                   both(hT_hi, hT_lo, A, c, slice(g * GT, (g + 1) * GT)), c == 0, c == DC - 1)
                last.then_inc(xl_filled, 1)
            pe.wait_ge(su_split, 1)
            for n in range(NG * SC):
                g, m = n // SC, n % SC
                if g:
                    pe.wait_ge(su_taken, n - SC + 1)
                for c in range(DC):
                    last = product(ps[:, 4 + m, :], both(su_hi, su_lo, A, c, slice(m * P, (m + 1) * P)),
                                   both(hT_hi, hT_lo, A, c, slice(g * GT, (g + 1) * GT)), c == 0, c == DC - 1)
                last.then_inc(su_filled, 1)
            pe.wait_ge(xl_done, NG)
            for n in range(NT):
                if n % GN == 0:
                    pe.wait_ge(su_taken, SC * (n // GN + 1))
                if n == 6:
                    pe.wait_ge(y3_taken, 2)
                for c in range(SC):
                    last = mm(ps[:, Y3_BANK[n // 2], (n % 2) * D:(n % 2 + 1) * D], s_act[:, c, n * P:(n + 1) * P], sd[:, c, :],
                              start=(c == 0), stop=(c == SC - 1))
                if n % 2:
                    last.then_inc(y3_filled, 1)
                if n == 0:
                    pe.wait_ge(cw_ready, 1)
                    pe.wait_ge(sc_done, 1)
                    for q in range(NG):
                        last = nc.tensor.transpose(ps[:, 2, q * P:(q + 1) * P],
                                                   cw[:, q * GN:(q + 1) * GN, :].rearrange("p n e -> p (n e)"), ident)
                    last.then_inc(cwT_filled, 1)

            def up(e, j, split_count, free):
                pe.wait_ge(w1_split, split_count)
                if free:
                    pe.wait_ge(wa_done, e + (j - 1))
                    pe.wait_ge(relu_done, e + (j - 1))
                w = both(w1_hi[j // 2 % 2], w1_lo[j // 2 % 2], A, j % 2, A)
                for t in range(2):
                    last = product(ps[:, 4 + 2 * (j % 2) + t, :], w, both(xl_hi, xl_lo, A, slice(t * 512, (t + 1) * 512)))
                last.then_inc(up_filled, 1)

            def experts(e, i, final):
                for j in range(4):
                    if not (final and j >= 2):
                        up(e, j + 2, i * 2 + ((j + 2) // 2 + 1), True)
                    pe.wait_ge(e_z_done, e + (j + 1))
                    pe.wait_ge(ld_w2[j // 2], i * 16 + 16)
                    for t in range(2):
                        last = mm(ps[:, t, :], w2[j // 2][:, j % 2, :], e_z[j % 2][:, t * 512:(t + 1) * 512],
                                  start=False, stop=final and j == 3, skip_group_check=True)
                    last.then_inc(down_done, 1)

            up(0, 0, 1, False)
            up(0, 1, 1, False)
            pe.wait_ge(y3_taken, NT)
            for b in range(2):
                mm(ps[:, b, :], zeros[:, 0:P], zeros[:, :], start=True, stop=False, skip_group_check=True)
            with pe.Fori(0, E // 4 - 1) as i:
                experts(i * 4, i, False)
            experts(E - 4, E // 4 - 1, True)
            pe.wait_ge(yl_done, 1)
            for n in range(NT):
                last = mm(ps[:, 4 + n // 2, (n % 2) * D:(n % 2 + 1) * D], yl[:, n * P:(n + 1) * P], fc2[:, :], start=True, stop=True)
                if n % 2:
                    last.then_inc(y4_filled, 1)


def kernel(**inputs):
    import numpy as np
    import concourse.bacc as bacc
    from concourse.bass_utils import run_bass_kernel_spmd

    a = {k: np.asarray(v) for k, v in inputs.items()}
    B, S, D = a["x"].shape
    T, P = B * S, 128
    heads = a["L1_xattn_Wq"].shape[1] // P

    def head_columns(w):
        return w.reshape(D // P, P, heads, P).transpose(2, 1, 0, 3)

    had = np.ones((1, 1), np.float32)
    while had.shape[0] < P:
        had = np.block([[had, had], [had, -had]])
    inner = a["L0_ffn_w_gate"].shape[0]
    arrays = {
        "x": a["x"].reshape(T, D),
        "ids": a["itok_BxS_13_99985"].reshape(T),
        "ctx_t": a["ctx_2048"].transpose(2, 0, 1).reshape(D, T),
        "g_xattn": a["g_xattn"],
        "g_ffn": a["g_ffn"],
        "w_gate_t": a["L0_ffn_w_gate"].T,
        "w_up_t": a["L0_ffn_w_up"].T,
        "w_down_t": a["L0_ffn_w_down"].T,
        "w_qk": np.stack([head_columns(a["L1_xattn_" + n]) for n in ("Wq", "Wk")], axis=2),
        "w_v": a["L1_xattn_Wv"].reshape(D // P, P, heads // 2, 2 * P).transpose(2, 1, 0, 3),
        "w_o": a["L1_xattn_Wo"].reshape(heads, P, D),
        "gate_w_t": a["L1_ffn_gate_w"].T,
        "gate_bias": a["L1_ffn_gate_bias"],
        "fc1_t": a["L1_ffn_fc1_w"].T,
        "fc2_t": a["L1_ffn_fc2_w"].T,
        "w1_t": a["L1_ffn_w1"].transpose(0, 2, 1),
        "w2_t": a["L1_ffn_w2"].transpose(0, 2, 1),
        "shared_up_t": a["L1_ffn_shared_up_w"].T,
        "shared_down_t": a["L1_ffn_shared_down_w"].T,
        "consts": np.stack([np.eye(P, dtype=np.float32)] + [had * np.float32(f / np.sqrt(inner)) for f in (1, 1, 1, -1)], axis=1),
    }
    arrays = {f"in_{k}": np.ascontiguousarray(v) for k, v in arrays.items()}
    nc = bacc.Bacc("TRN2", target_bir_lowering=False, num_devices=1)
    args = [nc.dram_tensor(k, v.shape, mybir.dt.from_np(v.dtype), kind="ExternalInput").ap() for k, v in arrays.items()]
    experts = a["L1_ffn_gate_w"].shape[0]
    scratch = nc.dram_tensor("cw_scratch", (experts, T), mybir.dt.float32, kind="Internal").ap()
    out = nc.dram_tensor("out", (T, D), mybir.dt.float32, kind="ExternalOutput").ap()
    flamingo_two_layer_kernel(nc, *args, scratch, out, B)
    r = run_bass_kernel_spmd(nc, [arrays], core_ids=[0])
    return r.results[0]["out"].reshape(B, S, D)
```

```python
import concourse.bass as bass
from concourse import mybir
from contextlib import ExitStack


def flamingo_two_layer_kernel(nc, x, ids, ctx_t, g_xattn, g_ffn, w_gate_t, w_up_t, w_down_t,
                              w_qk, w_v, w_o, gate_w_t, gate_bias, fc1_t, fc2_t, w1_t, w2_t,
                              shared_up_t, shared_down_t, consts, cw_scratch, out, batches):
    F32, F32R, BF16, I32 = mybir.dt.float32, mybir.dt.float32r, mybir.dt.bfloat16, mybir.dt.int32
    ALU, ACT, AX = mybir.AluOpType, mybir.ActivationFunctionType, mybir.AxisListType

    P = 128
    T, D = x.shape
    NB = batches
    S = T // NB
    NT = T // P
    DC = D // P
    NG = 2
    GN = NT // NG
    GT = T // NG
    INTER = w_gate_t.shape[1]
    IC = INTER // P
    NH = w_qk.shape[0]
    E = gate_w_t.shape[1]
    NGRP, TOPG = 4, 2
    EG = E // NGRP
    SI = shared_up_t.shape[1]
    SC = SI // P
    LN_EPS, Q_EPS = 1e-5, 1e-5
    ROUTED_SCALE = 2.5
    TOK_PER_EXPERT = 12500 // NB
    ROUND = 12582912.0
    RSQRT_GUESS = float(0x5F3759DF - 2**31)
    QK_SCALE = float(P) ** -0.5
    W_COUNT = float(INTER * D)

    ctx = ExitStack()
    with ctx:
        def sb(name, shape, dt=F32, where=None):
            return (where or ctx).enter_context(nc.sbuf_tensor(name, shape, dt))

        def sem(name):
            return ctx.enter_context(nc.semaphore(name))

        xr = sb("xr", [P, NT, D])
        h = sb("h", [P, NT, D])
        hT_hi = sb("hT_hi", [P, DC, T], F32R)
        hT_lo = sb("hT_lo", [P, DC, T], F32R)
        cT_hi = sb("cT_hi", [P, DC, NB * S], F32R)
        cT_lo = sb("cT_lo", [P, DC, NB * S], F32R)
        cst = sb("cst", [P, 5, P])
        ident = cst[:, 0, :]
        ones = sb("ones", [P, P])
        zeros = sb("zeros", [P, 512], F32R)
        gl = sb("gl", [P, 4])
        tg = sb("tg", [P, 4])
        st = sb("st", [P, NT, 6])
        mv = sb("mv", [P, NT, 2])
        ln_v = sb("ln_v", [P, NT])
        ln_y = sb("ln_y", [P, NT])
        ln_t = sb("ln_t", [P, NT])
        ln_i = sb("ln_i", [P, NT], I32)
        wqk_raw = [sb(f"wqk_raw{i}", [P, 2, DC, P]) for i in range(2)]
        wqk_hi = [sb(f"wqk_hi{i}", [P, 2, DC, P], F32R) for i in range(2)]
        wqk_lo = [sb(f"wqk_lo{i}", [P, 2, DC, P], F32R) for i in range(2)]
        wv_raw = [sb(f"wv_raw{i}", [P, DC, 2 * P]) for i in range(2)]
        wv_hi = sb("wv_hi", [P, DC, 2 * P], F32R)
        wv_lo = sb("wv_lo", [P, DC, 2 * P], F32R)
        wo_raw = [sb(f"wo_raw{i}", [P, D]) for i in range(2)]
        wo_hi = [sb(f"wo_hi{i}", [P, D], F32R) for i in range(2)]
        wo_lo = [sb(f"wo_lo{i}", [P, D], F32R) for i in range(2)]
        fc1_raw = sb("fc1_raw", [P, DC, P])
        fc1_hi = sb("fc1_hi", [P, DC, P], F32R)
        fc1_lo = sb("fc1_lo", [P, DC, P], F32R)
        fc2 = sb("fc2", [P, D])
        gw_raw = sb("gw_raw", [P, DC, E])
        gw_hi = sb("gw_hi", [P, DC, E], F32R)
        gw_lo = sb("gw_lo", [P, DC, E], F32R)
        gbias = sb("gbias", [P, E])

        region = ExitStack()
        cT_raw = sb("cT_raw", [P, DC, NB * S], F32, region)
        ids_row = sb("ids_row", [P, T], I32, region)
        ge_row = sb("ge_row", [P, NB - 1, T], I32, region)
        wraw = [sb(f"wraw{i}", [P, 2 * INTER], F32, region) for i in range(3)]
        wq8 = [sb(f"wq8_{i}", [P, 2 * INTER], BF16, region) for i in range(3)]
        ids_col = sb("ids_col", [P, NT], I32, region)
        ge_col = sb("ge_col", [P, NB - 1, NT], F32, region)
        tgm = sb("tgm", [P, NB, NT], F32, region)
        had = sb("had", [P, 2, 2 * P], F32R, region)
        wsum = sb("wsum", [P, 3], F32, region)
        wmean = sb("wmean", [P, 3], F32, region)
        wscale = sb("wscale", [P, 3], F32, region)
        fdown = sb("fdown", [P, 1], F32, region)
        am = sb("am", [P, NT], F32, region)
        am_r = sb("am_r", [P, NT], F32, region)
        am_c = sb("am_c", [P, NT], F32, region)
        c_gate = sb("c_gate", [P, NT], F32, region)
        c_up = sb("c_up", [P, NT], F32, region)
        qtok = sb("qtok", [P, GN, D], F32, region)
        qT = sb("qT", [P, NG, DC, GT], BF16, region)
        am2 = sb("am2", [P, 2, 4], F32, region)
        part = ExitStack()
        a_sel = sb("a_sel", [P, NG, DC, GT], F32, part)
        z_hi = sb("z_hi", [P, NG, DC, GT], F32R, part)
        z_lo = sb("z_lo", [P, NG, DC, GT], F32R, part)
        a_silu = sb("a_silu", [P, DC, GT], F32, part)
        part.close()
        part = ExitStack()
        inner = sb("inner", [P, 2, INTER], F32, part)
        fly = sb("fly", [P, INTER], F32, part)
        fT_hi = sb("fT_hi", [P, IC, P], F32R, part)
        fT_lo = sb("fT_lo", [P, IC, P], F32R, part)
        q2 = sb("q2", [P, INTER], F32, part)
        q2T = sb("q2T", [P, IC, P], BF16, part)
        part.close()
        region.close()

        region = ExitStack()
        kT_hi = [sb(f"kT_hi{i}", [P, T], F32R, region) for i in range(2)]
        kT_lo = [sb(f"kT_lo{i}", [P, T], F32R, region) for i in range(2)]
        v_hi, v_lo = [None, None], [None, None]
        v_hi[0] = sb("v_hi0", [P, NT, 2, P], F32R, region)
        v_lo[0] = sb("v_lo0", [P, NT, 2, P], F32R, region)
        qT_hi = [sb(f"qT_hi{i}", [P, T], F32R, region) for i in range(2)]
        qT_lo = [sb(f"qT_lo{i}", [P, T], F32R, region) for i in range(2)]
        v_hi[1] = sb("v_hi1", [P, NT, 2, P], F32R, region)
        v_lo[1] = sb("v_lo1", [P, NT, 2, P], F32R, region)
        probs = sb("probs", [P, NB, 2, S], F32, region)
        pT_hi = sb("pT_hi", [P, NB, 2, S], F32R, region)
        pT_lo = sb("pT_lo", [P, NB, 2, S], F32R, region)
        oT_hi = sb("oT_hi", [P, T], F32R, region)
        oT_lo = sb("oT_lo", [P, T], F32R, region)
        nmax = sb("nmax", [P, NB, 2], F32, region)
        esum = sb("esum", [P, NB, 2], F32, region)
        rsum = sb("rsum", [P, NB, 2], F32, region)
        region.close()

        region = ExitStack()
        su_raw = sb("su_raw", [P, DC, SI], F32, region)
        su_hi = sb("su_hi", [P, DC, SI], F32R, region)
        su_lo = sb("su_lo", [P, DC, SI], F32R, region)
        sd_raw = sb("sd_raw", [P, SC, D], F32, region)
        sd_hi = sb("sd_hi", [P, SC, D], F32R, region)
        sd_lo = sb("sd_lo", [P, SC, D], F32R, region)
        xl_hi = sb("xl_hi", [P, T], F32R, region)
        xl_lo = sb("xl_lo", [P, T], F32R, region)
        scT = sb("scT", [E, T], F32, region)
        sc = sb("sc", [P, NT, E], F32, region)
        sbias = sb("sbias", [P, NT, E], F32, region)
        gtop = sb("gtop", [P, NT * NGRP, 8], F32, region)
        gscore = sb("gscore", [P, NT, NGRP], F32, region)
        before = sb("before", [P, NGRP, NGRP], F32, region)
        cmp = sb("cmp", [P, NT, NGRP, NGRP], F32, region)
        eqs = sb("eqs", [P, NT, NGRP, NGRP], F32, region)
        grank = sb("grank", [P, NT, NGRP], F32, region)
        gmask = sb("gmask", [P, NT, NGRP], I32, region)
        gmask8 = sb("gmask8", [P, NT, E], I32, region)
        masked = sb("masked", [P, NT, E], F32, region)
        top8 = sb("top8", [P, NT, 8], F32, region)
        left = sb("left", [P, NT, E], F32, region)
        sel = sb("sel", [P, NT, E], F32, region)
        wsel = sb("wsel", [P, NT, E], F32, region)
        wden = sb("wden", [P, NT], F32, region)
        cw = sb("cw", [P, NT, E], F32, region)
        cwT = sb("cwT", [P, NG * P], F32, region)
        cw_row = [sb(f"cw_row{i}", [P, T], F32, region) for i in range(4)]
        w1_raw = [sb(f"w1_raw{i}", [P, 2, P], F32, region) for i in range(2)]
        w1_hi = [sb(f"w1_hi{i}", [P, 2, P], F32R, region) for i in range(2)]
        w1_lo = [sb(f"w1_lo{i}", [P, 2, P], F32R, region) for i in range(2)]
        w2_raw = [sb(f"w2_raw{i}", [P, 2, P], F32, region) for i in range(2)]
        w2_hi = [sb(f"w2_hi{i}", [P, 2, P], F32R, region) for i in range(2)]
        w2_lo = [sb(f"w2_lo{i}", [P, 2, P], F32R, region) for i in range(2)]
        part = ExitStack()
        s_relu = sb("s_relu", [P, 2, GT], F32, part)
        s_sq = sb("s_sq", [P, 2, GT], F32, part)
        s_hi = sb("s_hi", [P, SC, T], F32R, part)
        s_lo = sb("s_lo", [P, SC, T], F32R, part)
        part.close()
        part = ExitStack()
        e_relu = [sb(f"e_relu{i}", [P, T], F32, part) for i in range(2)]
        e_wa = [sb(f"e_wa{i}", [P, T], F32, part) for i in range(2)]
        e_z = [sb(f"e_z{i}", [P, T], F32, part) for i in range(2)]
        z_half_hi = [sb(f"z_half_hi{i}", [P, GT], F32R, part) for i in range(2)]
        z_half_lo = [sb(f"z_half_lo{i}", [P, GT], F32R, part) for i in range(2)]
        yl = sb("yl", [P, T], F32, part)
        part.close()
        region.close()

        ps = ctx.enter_context(nc.psum_tensor("ps", [P, 8, 512], F32))

        ld_const, ld_ids, ld_ctx, ld_gates = sem("ld_const"), sem("ld_ids"), sem("ld_ctx"), sem("ld_gates")
        ld_x = [sem(f"ld_x{g}") for g in range(NG)]
        ld_w = [sem(f"ld_w{i}") for i in range(3)]
        ld_small = sem("ld_small")
        ld_qk = [sem(f"ld_qk{i}") for i in range(2)]
        ld_wv = [sem(f"ld_wv{i}") for i in range(2)]
        ld_wo = [sem(f"ld_wo{i}") for i in range(2)]
        ld_shared = sem("ld_shared")
        ld_w1 = [sem(f"ld_w1_{i}") for i in range(2)]
        ld_w2 = [sem(f"ld_w2_{i}") for i in range(2)]
        ld_cw = [sem(f"ld_cw{i}") for i in range(4)]
        cw_stored, out_stored = sem("cw_stored"), sem("out_stored")
        dve_step, pool_step = sem("dve_step"), sem("pool_step")
        set_up, h_ready, hT_filled, hT_hi_done, hT_done = (
            sem("set_up"), sem("h_ready"), sem("hT_filled"), sem("hT_hi_done"), sem("hT_done"))
        tanh_done, masks_ready = sem("tanh_done"), sem("masks_ready")
        ctx_hi_done, ctx_done = sem("ctx_hi_done"), sem("ctx_done")
        a_filled, a_first_copied, a_taken = sem("a_filled"), sem("a_first_copied"), sem("a_taken")
        a_silu_done, z_ready, z_hi_done, z_done = sem("a_silu_done"), sem("z_ready"), sem("z_hi_done"), sem("z_done")
        y0_filled, y0_taken = sem("y0_filled"), sem("y0_taken")
        wsum_done, wtot_filled, wscale_done, w_ternary = (
            sem("wsum_done"), sem("wtot_filled"), sem("wscale_done"), sem("w_ternary"))
        q1_ready, q1T_filled, q1T_done = sem("q1_ready"), sem("q1T_filled"), sem("q1T_done")
        had_copied = sem("had_copied")
        gate_filled, up_values_filled, silu_done, inner_done = sem("gate_filled"), sem("up_values_filled"), sem("silu_done"), sem("inner_done")
        fly_step, fly_done = sem("fly_step"), sem("fly_done")
        scales_ready = sem("scales_ready")
        fT_filled, fT_hi_done, fT_done = sem("fT_filled"), sem("fT_hi_done"), sem("fT_done")
        had_filled, s2_ready, q2_done, q2_clipped = sem("had_filled"), sem("s2_ready"), sem("q2_done"), sem("q2_clipped")
        q2T_filled, q2T_done, y1_filled, y1_taken = sem("q2T_filled"), sem("q2T_done"), sem("y1_filled"), sem("y1_taken")
        small_split = sem("small_split")
        qk_split, wv_split, wo_split = sem("qk_split"), sem("wv_split"), sem("wo_split")
        unit_filled, hi_done, lo_done = sem("unit_filled"), sem("hi_done"), sem("lo_done")
        max_done, exp_done, rsum_done, probs_done = sem("max_done"), sem("exp_done"), sem("rsum_done"), sem("probs_done")
        y2_filled, y2_taken = sem("y2_filled"), sem("y2_taken")
        su_split = sem("su_split")
        logit_filled, scT_done, scT_back, sc_done = sem("logit_filled"), sem("scT_done"), sem("scT_back"), sem("sc_done")
        xl_filled, xl_hi_done, xl_done = sem("xl_filled"), sem("xl_hi_done"), sem("xl_done")
        su_filled, su_relu, su_square, su_taken = sem("su_filled"), sem("su_relu"), sem("su_square"), sem("su_taken")
        s_done, sd_split = sem("s_done"), sem("sd_split")
        y3_filled, y3_taken = sem("y3_filled"), sem("y3_taken")
        cw_ready, cwT_filled, cwT_done = sem("cw_ready"), sem("cwT_filled"), sem("cwT_done")
        w1_split, w2_split = sem("w1_split"), sem("w2_split")
        half_hi_done, half_lo_done = sem("half_hi_done"), sem("half_lo_done")
        up_filled, relu_done, wa_done, e_z_done, down_done = (
            sem("up_filled"), sem("relu_done"), sem("wa_done"), sem("e_z_done"), sem("down_done"))
        yl_done, y4_filled, y4_taken = sem("yl_done"), sem("y4_filled"), sem("y4_taken")

        block = ctx.enter_context(nc.Block())

        STEP = ["S0", "S1", "Y0", "S2", "K0", "S3", "K1", "T0", "Y1", "T1", "V0", "T2",
                "Q0", "Q1", "T3", "O0", "V1", "O1"]
        RING = [u for u in STEP if u[0] != "Y"]
        BANK = {u: p % 4 for p, u in enumerate(RING)}
        RING0 = ["K0", "K1", "S0", "S1", "V0", "V1", "Z0", "T0", "T1", "S2", "S3", "Q0", "T2", "Q1", "T3", "O0", "O1"]
        BANK0 = {u: p % 4 for p, u in enumerate(RING0)}
        RINGL = ["S0", "S1", "S2", "S3", "T0", "T1", "O0", "T2", "T3", "O1"]
        BANKL = {u: p % 4 for p, u in enumerate(RINGL)}
        FIRST = ["K0", "K1", "V0", "V1", "V2", "V3", "Q0"]
        BEFORE_1 = len(FIRST) + len(RING0) - len(RING)
        LOOPED = NH // 4 * 4 - 4
        SPLITS = sum(u[0] != "S" for u in RING)

        def ring_of(i):
            if i == 0:
                return RING0
            if i == NH - 1:
                return RINGL
            return [u for u in RING if u[0] != "V"] if i == NH - 2 else RING

        def banks_of(i):
            return BANK0 if i == 0 else BANKL if i == NH - 1 else BANK

        def splits_of(i):
            return [u for u in ring_of(i) if u[0] != "S"]

        def filled(i, u, at=None):
            if at == NH - 1:
                return BEFORE_1 + len(RING) * (NH - 2) + len(ring_of(NH - 2)) + ring_of(at).index(u) + 1
            return i * len(RING) + ((BEFORE_1 if at != 0 else len(FIRST)) + ring_of(at).index(u) + 1)

        def split(i, u, at=None):
            if at == NH - 1:
                return BEFORE_1 + SPLITS * (NH - 2) + len(splits_of(NH - 2)) + splits_of(at).index(u) + 1
            return i * SPLITS + ((BEFORE_1 if at != 0 else len(FIRST)) + splits_of(at).index(u) + 1)

        def place(u, j):
            if u == "Z0":
                return "Q1", 0
            if u[0] == "V":
                return "V" + str(2 * (j % 2) + int(u[1])), 1 - j // 2
            return u, 1 - j % 2 if u[0] in "QK" else j % 2

        def split_before(i, u, at=None):
            if at == NH - 1:
                return split(NH - 2, u, NH - 2)
            if at == 1:
                return split(0, u, 0)
            return i * SPLITS + (split(0, u) - SPLITS)

        STAGES = [("G", 0), ("U", 0), ("H", 2), ("C", 3), ("F", 1), ("D", 3)]
        AFTER = {0: [("A", 0)], 1: [("A", 1)], 2: [("A", 2)], NT: [("N", 0)], NT + 1: [("A", 3), ("X", 0)],
                 NT + 2: [("X", 1), ("N", 1)]}
        STARTS = [["K0"], ["K1"], ["S0", "S1", "V0", "V1"]]
        REST = RING0[sum(len(us) for us in STARTS):]
        FFN = [("Q", 0)]
        for i in range(NT + 2):
            if i == GN - 1:
                FFN.append(("Q", 1))
            FFN += [(u, i - behind) for u, behind in STAGES if 0 <= i - behind < NT]
            FFN += AFTER.get(i, [])
        FFN += [("C", NT - 1), ("X", 1), ("D", NT - 1), ("X", 2), ("N", 1)]
        PAIRS = [4, 2, 6, 0]
        pair_of, user_before, last_user = {}, {}, {}
        for k, u in enumerate(u for u in FFN if u[0] not in "DX"):
            pair_of[u] = {("C", NT - 1): 6, ("N", 1): 4}.get(u, PAIRS[k % 4])
            user_before[u] = last_user.get(pair_of[u])
            last_user[pair_of[u]] = u
        FRONT = [("N", 0), ("L", 0), ("X", 0), ("U", 0), ("N", 1), ("U", 1), ("U", 2), ("L", 1), ("U", 3),
                 ("B", 0), ("X", 1)] + [("U", n) for n in range(SC, NG * SC)]
        N_BANK = [0, 6]
        U_BANK = [4, 5, 0, 1]
        Y3_BANK = [6, 7, 3, 2]
        Y0_PAIR = [6, 0, 2, 6, 0, 2, 6, 0]
        FIRST_OF = [(0, 1), (2, 3), (4, 5), (6,)]
        first_bank = {m: pair_of["A", n] + m % 2 for n, ms in enumerate(FIRST_OF) for m in ms}

        @block.sync
        def _(sp):
            sp.dma_start(xr[:, 0:GN, :], x[0:GT, :].rearrange("(n p) d -> p n d", p=P)).then_inc(ld_x[0], 16)
            sp.dma_start(cst[:, :, :], consts).then_inc(ld_const, 16)
            sp.dma_start(cT_raw[:, :, :], ctx_t.rearrange("(c p) n -> p c n", p=P)).then_inc(ld_ctx, 16)
            sp.dma_start(xr[:, GN:NT, :], x[GT:T, :].rearrange("(n p) d -> p n d", p=P)).then_inc(ld_x[1], 16)
            sp.dma_start(ids_row[:, :], ids.rearrange("(a t) -> a t", a=1).broadcast_to([P, T])).then_inc(ld_ids, 16)
            sp.dma_start(ids_col[:, :], ids.rearrange("(n p) -> p n", p=P),
                         allow_slow_non_contiguous=True).then_inc(ld_ids, 16)
            sp.dma_start(gl[:, 0:2], g_xattn.rearrange("(a t) -> a t", a=1).broadcast_to([P, 2])).then_inc(ld_gates, 16)
            sp.dma_start(gl[:, 2:4], g_ffn.rearrange("(a t) -> a t", a=1).broadcast_to([P, 2])).then_inc(ld_gates, 16)
            for i, (w, c) in enumerate(((w_gate_t, DC), (w_up_t, DC), (w_down_t, IC))):
                sp.dma_start(wraw[i][:, :].rearrange("p (c n) -> p c n", c=c),
                             w.rearrange("(c p) n -> p c n", p=P)).then_inc(ld_w[i], 16)
            for i in range(2):
                sp.dma_start(wqk_raw[i][:, :, :, :], w_qk[i]).then_inc(ld_qk[i], 16)
                sp.dma_start(wv_raw[i][:, :, :], w_v[i]).then_inc(ld_wv[i], 16)
                sp.dma_start(wo_raw[i][:, :], w_o[i]).then_inc(ld_wo[i], 16)
            sp.dma_start(fc1_raw[:, :, :], fc1_t.rearrange("(c p) n -> p c n", p=P)).then_inc(ld_small, 16)
            sp.dma_start(gw_raw[:, :, :], gate_w_t.rearrange("(c p) n -> p c n", p=P)).then_inc(ld_small, 16)
            sp.dma_start(fc2[:, :], fc2_t).then_inc(ld_small, 16)
            sp.dma_start(gbias[:, :], gate_bias.rearrange("(a t) -> a t", a=1).broadcast_to([P, E])).then_inc(ld_small, 16)

            def reload(i, j, pair):
                b = j % 2
                sp.wait_ge(qk_split, i + 1)
                sp.dma_start(wqk_raw[b][:, :, :, :], w_qk[i + 2]).then_inc(ld_qk[b], 16)
                if pair is not None:
                    sp.wait_ge(wv_split, pair + 1)
                    sp.dma_start(wv_raw[j // 2][:, :, :], w_v[pair + 2]).then_inc(ld_wv[j // 2], 16)
                sp.wait_ge(wo_split, i + 1)
                sp.dma_start(wo_raw[b][:, :], w_o[i + 2]).then_inc(ld_wo[b], 16)

            with sp.Fori(0, LOOPED // 4) as i:
                for j in range(4):
                    reload(i * 4 + j, j, None if j % 2 else i * 2 + j // 2)
            for j in range(2):
                reload(LOOPED + j, j, None)
            sp.wait_ge(y2_filled, 4)
            sp.dma_start(su_raw[:, :, :], shared_up_t.rearrange("(c p) n -> p c n", p=P)).then_inc(ld_shared, 16)
            sp.dma_start(sd_raw[:, :, :], shared_down_t.rearrange("(c p) n -> p c n", p=P)).then_inc(ld_shared, 16)
            for i in range(2):
                sp.dma_start(w1_raw[i][:, :, :], w1_t[2 * i:2 * i + 2].rearrange("e p n -> p e n")).then_inc(ld_w1[i], 16)
                sp.dma_start(w2_raw[i][:, :, :], w2_t[2 * i:2 * i + 2].rearrange("e p n -> p e n")).then_inc(ld_w2[i], 16)
            sp.wait_ge(cwT_done, 1)
            scratch = cw_scratch.rearrange("e (g j p) -> e g j p", g=NG, j=GN)
            for j in range(GN):
                sp.dma_start(scratch[:, :, j, :], cwT[j * E:(j + 1) * E, :].rearrange("e (g p) -> e g p", g=NG)).then_inc(cw_stored, 16)
            sp.wait_ge(cw_stored, 16 * GN)
            for j in range(4):
                sp.dma_start(cw_row[j][:, :], cw_scratch[j:j + 1, :].broadcast_to([P, T])).then_inc(ld_cw[j], 16)

            def reload_w1(b, e, count):
                sp.wait_ge(w1_split, count)
                sp.dma_start(w1_raw[b][:, :, :], w1_t[bass.ds(e, 2)].rearrange("e p n -> p e n")).then_inc(ld_w1[b], 16)

            def reload_experts(i, final):
                reload_w1(1, i * 4 + 6, i * 2 + 2)
                for b in range(2):
                    for j in (2 * b, 2 * b + 1):
                        sp.wait_ge(wa_done, i * 4 + j + 1)
                        sp.dma_start(cw_row[j][:, :], cw_scratch[bass.ds(i * 4 + (j + 4), 1), :].broadcast_to([P, T])).then_inc(ld_cw[j], 16)
                    sp.wait_ge(down_done, i * 4 + 2 * b + 2)
                    sp.dma_start(w2_raw[b][:, :, :], w2_t[bass.ds(i * 4 + (2 * b + 4), 2)].rearrange("e p n -> p e n")).then_inc(ld_w2[b], 16)
                    if b == 0 and not final:
                        reload_w1(0, i * 4 + 8, i * 2 + 3)

            reload_w1(0, 4, 1)
            with sp.Fori(0, E // 4 - 2) as i:
                reload_experts(i, False)
            reload_experts(E // 4 - 2, True)
            for g in range(NG):
                sp.wait_ge(y4_taken, GN * (g + 1))
                sp.dma_start(out[g * GT:(g + 1) * GT, :].rearrange("(n p) d -> p n d", p=P),
                             xr[:, g * GN:(g + 1) * GN, :]).then_inc(out_stored, 16)
            sp.wait_ge(out_stored, 16 * NG)

        @block.gpsimd
        def _(pool):
            steps = [0]

            def own(ins):
                steps[0] += 1
                ins.then_inc(pool_step, 1)
                pool.wait_ge(pool_step, steps[0])

            nc.gpsimd.memset(ones[:, :], 1.0).then_inc(set_up, 1)
            nc.gpsimd.memset(zeros[:, :].bitcast(F32), 0.0).then_inc(set_up, 1)

            def high(dst, src):
                return nc.gpsimd.tensor_tensor(dst, src, zeros[:, 0:1].bitcast(F32).to_broadcast([P, src.shape[1]]), ALU.add)

            pool.wait_ge(ld_ids, 32)
            for e in range(1, NB):
                nc.gpsimd.tensor_scalar(ge_row[:, e - 1, :], ids_row[:, :], float(e * TOK_PER_EXPERT), None, ALU.is_ge)\
                    .then_inc(masks_ready, 1)

            def first_weights():
                for b in range(2):
                    pool.wait_ge(ld_qk[b], 16)
                    own(high(wqk_hi[b][:, :, :, :].rearrange("p w c n -> p (w c n)"), wqk_raw[b][:, :, :, :].rearrange("p w c n -> p (w c n)")))
                    nc.gpsimd.tensor_tensor(wqk_lo[b][:, :, :, :], wqk_raw[b][:, :, :, :],
                                            wqk_hi[b][:, :, :, :].bitcast(F32), ALU.subtract).then_inc(qk_split, 1)
                pool.wait_ge(ld_wv[0], 16)
                own(high(wv_hi[:, :, :].rearrange("p c n -> p (c n)"), wv_raw[0][:, :, :].rearrange("p c n -> p (c n)")))
                nc.gpsimd.tensor_tensor(wv_lo[:, :, :], wv_raw[0][:, :, :], wv_hi[:, :, :].bitcast(F32), ALU.subtract).then_inc(wv_split, 1)

            for i in range(3):
                if i == 2:
                    first_weights()
                pool.wait_ge(wscale_done, 1)
                own(nc.gpsimd.tensor_scalar(wraw[i][:, :], wraw[i][:, :], wscale[:, i:i + 1], ROUND, ALU.mult, ALU.add))
                own(nc.gpsimd.tensor_scalar(wraw[i][:, :], wraw[i][:, :], ROUND + 1.0, ROUND - 1.0, ALU.min, ALU.max))
                nc.gpsimd.tensor_scalar(wq8[i][:, :], wraw[i][:, :], -ROUND, 1.0, ALU.add, ALU.mult).then_inc(w_ternary, 1)

            pool.wait_ge(ld_small, 64)
            nc.gpsimd.tensor_copy(gw_hi[:, :, :], gw_raw[:, :, :])
            own(nc.gpsimd.tensor_copy(fc1_hi[:, :, :], fc1_raw[:, :, :]))
            nc.gpsimd.tensor_tensor(gw_lo[:, :, :], gw_raw[:, :, :], gw_hi[:, :, :].bitcast(F32), ALU.subtract)
            nc.gpsimd.tensor_tensor(fc1_lo[:, :, :], fc1_raw[:, :, :], fc1_hi[:, :, :].bitcast(F32), ALU.subtract).then_inc(small_split, 1)

            for n in range(NT):
                pool.wait_ge(inner_done, n + 1)
                if n:
                    pool.wait_ge(fly_done, n)
                half = INTER // 2
                src = inner[:, n % 2, :]
                nc.gpsimd.tensor_tensor(fly[:, 0:half], src[:, 0:half], src[:, half:INTER], ALU.add)
                nc.gpsimd.tensor_tensor(fly[:, half:INTER], src[:, 0:half], src[:, half:INTER], ALU.subtract).then_inc(fly_step, 1)
                pool.wait_ge(fly_step, n + 1)
                f = fly[:, :].rearrange("p (a two c) -> p a two c", a=2, two=2)
                d = src.rearrange("p (a two c) -> p a two c", a=2, two=2)
                nc.gpsimd.tensor_tensor(d[:, :, 0], f[:, :, 0], f[:, :, 1], ALU.add)
                nc.gpsimd.tensor_tensor(d[:, :, 1], f[:, :, 0], f[:, :, 1], ALU.subtract).then_inc(fly_done, 1)

            def attend(i):
                for b in range(NB):
                    pool.wait_ge(rsum_done, i * NB + b + 1)
                    nc.gpsimd.tensor_tensor(probs[:, b, :, :], probs[:, b, :, :],
                                            rsum[:, b, :].unsqueeze(2).to_broadcast([P, 2, S]), ALU.mult).then_inc(probs_done, 1)

            def split_weights(par, load, qk, count):
                if qk:
                    pool.wait_ge(ld_qk[par], load + 32)
                    high(wqk_hi[par][:, :, :, :].rearrange("p w c n -> p (w c n)"), wqk_raw[par][:, :, :, :].rearrange("p w c n -> p (w c n)")).then_inc(pool_step, 1)
                pool.wait_ge(ld_wo[par], load + 16)
                high(wo_hi[par][:, :], wo_raw[par][:, :]).then_inc(pool_step, 1)
                pool.wait_ge(pool_step, count)
                if qk:
                    nc.gpsimd.tensor_tensor(wqk_lo[par][:, :, :, :], wqk_raw[par][:, :, :, :],
                                            wqk_hi[par][:, :, :, :].bitcast(F32), ALU.subtract).then_inc(qk_split, 1)
                nc.gpsimd.tensor_tensor(wo_lo[par][:, :], wo_raw[par][:, :], wo_hi[par][:, :].bitcast(F32),
                                        ALU.subtract).then_inc(wo_split, 1)

            def split_values(b, load, read, count):
                pool.wait_ge(ld_wv[b], load)
                pool.wait_ge(unit_filled, read)
                high(wv_hi[:, :, :].rearrange("p c n -> p (c n)"), wv_raw[b][:, :, :].rearrange("p c n -> p (c n)")).then_inc(pool_step, 1)
                pool.wait_ge(pool_step, count)
                nc.gpsimd.tensor_tensor(wv_lo[:, :, :], wv_raw[b][:, :, :], wv_hi[:, :, :].bitcast(F32), ALU.subtract).then_inc(wv_split, 1)

            steps[0] += 1
            split_values(1, 16, FIRST.index("V3") + 1, steps[0])
            base = steps[0]
            with pool.Fori(0, LOOPED // 4) as i:
                for j in range(4):
                    attend(i * 4 + j)
                    split_weights(j % 2, i * 32 + 16 * (j // 2), True, i * 10 + (base + 2 * j + 2 + j // 2))
                    if j % 2:
                        split_values(j // 2, i * 16 + 32, filled(i * 4 + j, "V1"), i * 10 + (base + 2 * j + 3 + j // 2))
            steps[0] = base + 10 * (LOOPED // 4)
            for j in range(4):
                attend(LOOPED + j)
                steps[0] += 2 if j < 2 else 1
                split_weights(j % 2, 8 * LOOPED + 16 * (j // 2), j < 2, steps[0])

            pool.wait_ge(y2_filled, 4)
            nc.gpsimd.memset(before[:, :, :], 0.0).then_inc(set_up, 1)
            pool.wait_ge(set_up, 3)
            for a in range(1, NGRP):
                last = nc.gpsimd.memset(before[:, a, 0:a], 1.0)
            last.then_inc(set_up, 1)
            pool.wait_ge(ld_shared, 32)
            own(high(su_hi[:, :, :].rearrange("p c n -> p (c n)"), su_raw[:, :, :].rearrange("p c n -> p (c n)")))
            nc.gpsimd.tensor_tensor(su_lo[:, :, :], su_raw[:, :, :], su_hi[:, :, :].bitcast(F32), ALU.subtract).then_inc(su_split, 1)
            own(high(sd_hi[:, :, :].rearrange("p c n -> p (c n)"), sd_raw[:, :, :].rearrange("p c n -> p (c n)")))
            nc.gpsimd.tensor_tensor(sd_lo[:, :, :], sd_raw[:, :, :], sd_hi[:, :, :].bitcast(F32), ALU.subtract).then_inc(sd_split, 1)

            def shared_lows(g):
                for n in range(g * SC, (g + 1) * SC):
                    s = slice(g * GT, (g + 1) * GT)
                    pool.wait_ge(su_taken, n + 1)
                    nc.gpsimd.tensor_tensor(s_lo[:, n % SC, s], s_sq[:, n % 2, :], s_hi[:, n % SC, s].bitcast(F32), ALU.subtract)\
                        .then_inc(s_done, 1)

            shared_lows(0)

            def split_w1(b, landed, count):
                pool.wait_ge(ld_w1[b], landed)
                high(w1_hi[b][:, :, :].rearrange("p e n -> p (e n)"), w1_raw[b][:, :, :].rearrange("p e n -> p (e n)")).then_inc(pool_step, 1)
                pool.wait_ge(pool_step, count)
                nc.gpsimd.tensor_tensor(w1_lo[b][:, :, :], w1_raw[b][:, :, :], w1_hi[b][:, :, :].bitcast(F32),
                                        ALU.subtract).then_inc(w1_split, 1)

            base = steps[0]
            for b in range(2):
                split_w1(b, 16, base + b + 1)
            shared_lows(1)

            def split_w2(b, landed, count):
                pool.wait_ge(ld_w2[b], landed)
                high(w2_hi[b][:, :, :].rearrange("p e n -> p (e n)"), w2_raw[b][:, :, :].rearrange("p e n -> p (e n)")).then_inc(pool_step, 1)
                pool.wait_ge(pool_step, count)
                nc.gpsimd.tensor_tensor(w2_lo[b][:, :, :], w2_raw[b][:, :, :], w2_hi[b][:, :, :].bitcast(F32),
                                        ALU.subtract).then_inc(w2_split, 1)

            def half_low(e, j):
                pool.wait_ge(half_hi_done, e + (j + 1))
                nc.gpsimd.tensor_tensor(z_half_lo[j % 2][:, :], e_z[j % 2][:, 0:GT], z_half_hi[j % 2][:, :].bitcast(F32),
                                        ALU.subtract).then_inc(half_lo_done, 1)

            base += 2
            with pool.Fori(0, E // 4 - 1) as i:
                for b in range(2):
                    split_w2(b, i * 16 + 16, i * 4 + (base + 2 * b + 1))
                    half_low(i * 4, 2 * b)
                    pool.wait_ge(up_filled, i * 4 + 2 * b + 2)
                    split_w1(b, i * 16 + 32, i * 4 + (base + 2 * b + 2))
                    half_low(i * 4, 2 * b + 1)
            for b in range(2):
                split_w2(b, E // 4 * 16, base + 4 * (E // 4 - 1) + b + 1)
                for j in range(2):
                    half_low(E - 4, 2 * b + j)

        @block.scalar
        def _(act):
            def norm_hi(k, g, bank):
                act.wait_ge(hT_filled, k * NG + g + 1)
                nc.scalar.activation(hT_hi[:, :, g * GT:(g + 1) * GT], ps[:, bank:bank + 2, :], ACT.Copy).then_inc(hT_hi_done, 1)

            act.wait_ge(ld_ctx, 16)
            nc.scalar.activation(cT_hi[:, :, :], cT_raw[:, :, :], ACT.Copy).then_inc(ctx_hi_done, 1)
            norm_hi(0, 0, 0)

            def sum_weight(i):
                act.wait_ge(ld_w[i], 16)
                return nc.scalar.activation(wq8[i][:, :], wraw[i][:, :], ACT.Abs, accum_out=wsum[:, i:i + 1])

            def first_expert(g):
                act.wait_ge(a_filled, NB * g + 1)
                nc.scalar.activation(a_sel[:, g, :, :], ps[:, 2:4, :], ACT.Copy).then_inc(a_first_copied, 1)

            sum_weight(0)
            sum_weight(1)
            first_expert(0)
            act.wait_ge(ld_gates, 32)
            nc.scalar.activation(tg[:, :], gl[:, :], ACT.Tanh).then_inc(tanh_done, 1)
            norm_hi(0, 1, 0)
            sum_weight(2).then_inc(wsum_done, 1)
            act.wait_ge(ld_const, 16)
            nc.scalar.activation(had[:, :, :].rearrange("p a n -> p (a n)"), cst[:, 1:5, :].rearrange("p a n -> p (a n)"), ACT.Copy)\
                .then_inc(had_copied, 1)
            for g in range(NG):
                if g:
                    first_expert(g)
                act.wait_ge(a_taken, (NB - 1) * (g + 1))
                nc.scalar.activation(a_silu[:, :, :], a_sel[:, g, :, :], ACT.Silu).then_inc(a_silu_done, 1)
                act.wait_ge(z_ready, g + 1)
                nc.scalar.activation(z_hi[:, g, :, :], a_sel[:, g, :, :], ACT.Copy).then_inc(z_hi_done, 1)

            def tokens_back(g):
                act.wait_ge(q1T_filled, g + 1)
                b = pair_of["Q", g]
                nc.scalar.activation(qT[:, g, :, :], ps[:, b:b + 2, :], ACT.Copy, bias=-ROUND).then_inc(q1T_done, 1)

            def unit_dst(kind, half, par):
                if kind == "Q":
                    return qT_hi[par][:, half * GT:(half + 1) * GT], QK_SCALE
                if kind == "K":
                    return kT_hi[par][:, half * GT:(half + 1) * GT], 1.0
                if kind == "V":
                    return v_hi[par][:, 2 * half:2 * half + 2, :, :].rearrange("p n a d -> p (n a d)"), 1.0
                if kind == "T":
                    return pT_hi[:, half, :, :], 1.0
                return oT_hi[:, half * GT:(half + 1) * GT], 1.0

            def high_part(u, bank, par, at):
                act.wait_ge(unit_filled, at)
                dst, scale = unit_dst(u[0], int(u[1]), par)
                nc.scalar.activation(dst, ps[:, bank, :], ACT.Copy, scale=scale).then_inc(hi_done, 1)

            def attend(i, j, at=None, units=None):
                bank = banks_of(at)
                for u in units or ring_of(at):
                    if u[0] == "S":
                        b = int(u[1])
                        act.wait_ge(max_done, i * NB + b + 1)
                        for t in range(2):
                            last = nc.scalar.activation(probs[:, b, t, :], ps[:, bank[u], t * S:(t + 1) * S], ACT.Exp,
                                                        bias=nmax[:, b, t:t + 1], accum_out=esum[:, b, t:t + 1])
                        last.then_inc(exp_done, 1)
                    else:
                        name, slot = place(u, j)
                        high_part(name, bank[u], slot, filled(i, u, at))

            tokens_back(0)
            for i in range(NT + 3):
                if i < NT:
                    act.wait_ge(gate_filled, i + 1)
                    b = pair_of["G", i]
                    nc.scalar.activation(inner[:, i % 2, :], ps[:, b:b + 2, :], ACT.Silu, scale=c_gate[:, i:i + 1])\
                        .then_inc(silu_done, 1)
                if i == GN - 1:
                    tokens_back(1)
                if 0 <= i - 3 < NT:
                    act.wait_ge(q2T_filled, i - 2)
                    b = pair_of["C", i - 3]
                    nc.scalar.activation(q2T[:, :, :], ps[:, b:b + 2, :], ACT.Copy, bias=-ROUND).then_inc(q2T_done, 1)
                if 0 <= i - 1 < NT:
                    act.wait_ge(fT_filled, i)
                    b = pair_of["F", i - 1]
                    nc.scalar.activation(fT_hi[:, :, :], ps[:, b:b + 2, :], ACT.Copy).then_inc(fT_hi_done, 1)
                if 0 <= i - 2 < NT:
                    act.wait_ge(s2_ready, i - 1)
                    b = pair_of["H", i - 2]
                    nc.scalar.activation(q2[:, :], ps[:, b:b + 2, :], ACT.Copy,
                                         scale=am2[:, i % 2, 2:3], bias=ROUND).then_inc(q2_done, 1)
                for u, n in AFTER.get(i, []):
                    if u == "N":
                        if n == 1:
                            attend(0, 0, 0, ["V0", "V1"])
                        norm_hi(1, n, pair_of["N", n])
                    elif u == "X":
                        attend(0, 0, 0, STARTS[n])
                    else:
                        for m in FIRST_OF[n]:
                            high_part(FIRST[m], first_bank[m], 0, m + 1)

            attend(0, 0, 0, ["S0", "S1"] + REST)
            for j in range(1, 4):
                attend(j, j)
            with act.Fori(1, LOOPED // 4) as i:
                for j in range(4):
                    attend(i * 4 + j, j)
            for j in range(4):
                attend(LOOPED + j, j, LOOPED + j)

            for u, n in FRONT:
                if u == "N":
                    norm_hi(2, n, N_BANK[n])
                elif u == "L":
                    act.wait_ge(logit_filled, n + 1)
                    nc.scalar.activation(scT[:, n * GT:(n + 1) * GT], ps[0:E, 2, :], ACT.Sigmoid).then_inc(scT_done, 1)
                elif u == "X":
                    act.wait_ge(xl_filled, n + 1)
                    nc.scalar.activation(xl_hi[:, n * GT:(n + 1) * GT], ps[:, 3, :], ACT.Copy).then_inc(xl_hi_done, 1)
                elif u == "B":
                    act.wait_ge(scT_back, 1)
                    nc.scalar.activation(sc[:, :, :], ps[:, 2, 0:NT * E].rearrange("p (n e) -> p n e", e=E), ACT.Copy).then_inc(sc_done, 1)
                else:
                    act.wait_ge(su_filled, n + 1)
                    nc.scalar.activation(s_relu[:, n % 2, :], ps[:, U_BANK[n % SC], :], ACT.Relu).then_inc(su_relu, 1)
                    act.wait_ge(su_relu, n + 1)
                    if n >= 2:
                        act.wait_ge(s_done, n - 1)
                    nc.scalar.activation(s_sq[:, n % 2, :], s_relu[:, n % 2, :], ACT.Square).then_inc(su_square, 1)
                    act.wait_ge(su_square, n + 1)
                    nc.scalar.activation(s_hi[:, n % SC, n // SC * GT:(n // SC + 1) * GT], s_sq[:, n % 2, :], ACT.Copy)\
                        .then_inc(su_taken, 1)

            act.wait_ge(cwT_filled, 1)
            nc.scalar.activation(cwT[:, :], ps[:, 2, 0:NG * P], ACT.Copy).then_inc(cwT_done, 1)

            def expert(e, j, first):
                act.wait_ge(up_filled, e + (j + 1))
                if not (first and j < 2):
                    act.wait_ge(e_z_done, e + (j - 1))
                nc.scalar.activation(e_relu[j % 2][:, :], ps[:, 4 + 2 * (j % 2):6 + 2 * (j % 2), :], ACT.Relu).then_inc(relu_done, 1)
                if not (first and j == 0):
                    half_high(e, j - 1)

            def half_high(e, j):
                act.wait_ge(e_z_done, e + (j + 1))
                nc.scalar.activation(z_half_hi[j % 2][:, :], e_z[j % 2][:, 0:GT], ACT.Copy).then_inc(half_hi_done, 1)

            for j in range(4):
                expert(0, j, True)
            with act.Fori(1, E // 4) as i:
                for j in range(4):
                    expert(i * 4, j, False)
            half_high(E - 4, 3)
            act.wait_ge(down_done, E)
            nc.scalar.activation(yl[:, :], ps[:, 0:2, :], ACT.Copy).then_inc(yl_done, 1)

        @block.vector
        def _(dve):
            steps = [0]
            V = nc.vector

            def own(ins):
                steps[0] += 1
                ins.then_inc(dve_step, 1)
                dve.wait_ge(dve_step, steps[0])

            def stats(n):
                return V.bn_stats(st[:, n, :], xr[:, n, :])

            def factors(t0, t1):
                for n in range(t0, t1):
                    last = V.bn_aggr(mv[:, n, :], st[:, n, :])
                own(last)
                v, y, t = ln_v[:, t0:t1], ln_y[:, t0:t1], ln_t[:, t0:t1]
                own(V.tensor_scalar(v, mv[:, t0:t1, 1], LN_EPS, None, ALU.add))
                own(V.tensor_scalar(ln_i[:, t0:t1], v.bitcast(I32), 1, None, ALU.logical_shift_right))
                own(V.tensor_scalar(y.bitcast(I32), ln_i[:, t0:t1], -1.0, RSQRT_GUESS, ALU.mult, ALU.add))
                for _ in range(3):
                    own(V.scalar_tensor_tensor(t, y, 0.5, y, ALU.mult, ALU.mult))
                    own(V.tensor_tensor(t, t, v, ALU.mult))
                    own(V.scalar_tensor_tensor(y, t, 1.5, y, ALU.subtract, ALU.mult))

            def scaled(g):
                for n in range(g * GN, (g + 1) * GN):
                    last = V.tensor_scalar(h[:, n, :], xr[:, n, :], mv[:, n, 0:1], ln_y[:, n:n + 1], ALU.subtract, ALU.mult)
                return last

            def norm(g, counted=0):
                for n in range(g * GN + counted, (g + 1) * GN):
                    last = stats(n)
                own(last)
                factors(g * GN, (g + 1) * GN)
                return scaled(g)

            def norm_lo(k, g, bank):
                dve.wait_ge(hT_hi_done, k * NG + g + 1)
                s = slice(g * GT, (g + 1) * GT)
                V.tensor_tensor(hT_lo[:, :, s], ps[:, bank:bank + 2, :], hT_hi[:, :, s].bitcast(F32), ALU.subtract).then_inc(hT_done, 1)

            dve.wait_ge(ld_x[0], 16)
            norm(0).then_inc(h_ready, 1)
            dve.wait_ge(ctx_hi_done, 1)
            V.tensor_tensor(cT_lo[:, :, :], cT_raw[:, :, :], cT_hi[:, :, :].bitcast(F32), ALU.subtract).then_inc(ctx_done, 1)
            norm_lo(0, 0, 0)
            dve.wait_ge(ld_x[1], 16)
            norm(1).then_inc(h_ready, 1)

            dve.wait_ge(ld_ids, 32)
            for e in range(1, NB):
                last = V.tensor_scalar(ge_col[:, e - 1, :], ids_col[:, :], float(e * TOK_PER_EXPERT), None, ALU.is_ge)
            own(last)
            V.tensor_scalar(tgm[:, 0, :], ge_col[:, 0, :], -1.0, 1.0, ALU.mult, ALU.add)
            for e in range(1, NB - 1):
                V.tensor_tensor(tgm[:, e, :], ge_col[:, e - 1, :], ge_col[:, e, :], ALU.subtract)
            own(V.tensor_copy(tgm[:, NB - 1, :], ge_col[:, NB - 2, :]))

            def gates_and_means():
                dve.wait_ge(tanh_done, 1)
                own(V.tensor_scalar(tgm[:, :, :], tgm[:, :, :], tg[:, 0:1], None, ALU.mult))
                dve.wait_ge(wtot_filled, 1)
                own(V.tensor_scalar(wmean[:, :], ps[:, 7, 0:3], 1.0 / W_COUNT, Q_EPS, ALU.mult, ALU.max))
                V.tensor_scalar(fdown[:, :], wmean[:, 2:3], tg[:, 2:3], 1.0 / 128.0, ALU.mult, ALU.mult)
                V.reciprocal(wscale[:, :], wmean[:, :]).then_inc(wscale_done, 1)

            for g in range(NG):
                s = slice(g * GT, (g + 1) * GT)
                for e in range(1, NB):
                    dve.wait_ge(a_filled, NB * g + e + 1)
                    if e == 1:
                        dve.wait_ge(a_first_copied, g + 1)
                        dve.wait_ge(masks_ready, NB - 1)
                    b = 2 + 2 * (e % 2)
                    for c in range(DC):
                        last = V.copy_predicated(a_sel[:, g, c, :], ge_row[:, e - 1, s], ps[:, b + c, :])
                    last.then_inc(a_taken, 1)
                    if g == 0 and e == 1:
                        norm_lo(0, 1, 0)
                    if g == 0 and e == 3:
                        gates_and_means()
                    dve.wait_ge(a_taken, (NB - 1) * g + e)
                dve.wait_ge(a_silu_done, g + 1)
                V.tensor_tensor(a_sel[:, g, :, :], a_sel[:, g, :, :], a_silu[:, :, :], ALU.mult).then_inc(z_ready, 1)
                dve.wait_ge(z_hi_done, g + 1)
                V.tensor_tensor(z_lo[:, g, :, :], a_sel[:, g, :, :], z_hi[:, g, :, :].bitcast(F32), ALU.subtract).then_inc(z_done, 1)

            def add_experts(tiles, counted=None):
                before = {}
                for e in range(NB):
                    for n in tiles:
                        if e == 0:
                            dve.wait_ge(y0_filled, n + 1)
                        else:
                            dve.wait_ge(dve_step, before[n])
                        ins = V.scalar_tensor_tensor(xr[:, n, :], ps[:, Y0_PAIR[n] + e // 2, (e % 2) * D:(e % 2 + 1) * D],
                                                     tgm[:, e, n:n + 1], xr[:, n, :], ALU.mult, ALU.add)
                        if e < NB - 1:
                            steps[0] += 1
                            before[n] = steps[0]
                            ins.then_inc(dve_step, 1)
                        else:
                            ins.then_inc(y0_taken, 1)
                    if e == 0 and counted is not None:
                        dve.wait_ge(y0_taken, counted + 1)
                        stats(counted)

            def quantise(g):
                s = slice(g * GN, (g + 1) * GN)
                own(V.tensor_reduce(am[:, s], h[:, s, :], AX.X, ALU.max, apply_absolute_value=True))
                own(V.tensor_scalar(am[:, s], am[:, s], Q_EPS, None, ALU.max))
                own(V.reciprocal(am_r[:, s], am[:, s]))
                own(V.tensor_scalar(am_r[:, s], am_r[:, s], 128.0, None, ALU.mult))
                if g:
                    dve.wait_ge(q1T_filled, g)
                for n in range(GN):
                    last = V.tensor_scalar(qtok[:, n, :], h[:, g * GN + n, :], am_r[:, g * GN + n:g * GN + n + 1], ROUND,
                                           ALU.mult, ALU.add)
                own(last)
                V.tensor_scalar(qtok[:, :, :], qtok[:, :, :], ROUND + 127.0, ROUND - 128.0, ALU.min, ALU.max).then_inc(q1_ready, 1)
                own(V.tensor_scalar(am_c[:, s], am[:, s], 1.0 / 128.0, None, ALU.mult))
                V.tensor_scalar(c_up[:, s], am_c[:, s], wmean[:, 1:2], None, ALU.mult)
                V.tensor_scalar(c_gate[:, s], am_c[:, s], wmean[:, 0:1], None, ALU.mult).then_inc(scales_ready, 1)

            def low_part(u, bank, par, at):
                dve.wait_ge(hi_done, at)
                kind, half = u[0], int(u[1])
                s, n = slice(half * GT, (half + 1) * GT), slice(2 * half, 2 * half + 2)
                src = ps[:, bank, :]
                if kind == "Q":
                    ins = V.scalar_tensor_tensor(qT_lo[par][:, s], src, QK_SCALE, qT_hi[par][:, s].bitcast(F32),
                                                 ALU.mult, ALU.subtract)
                elif kind == "K":
                    ins = V.tensor_tensor(kT_lo[par][:, s], src, kT_hi[par][:, s].bitcast(F32), ALU.subtract)
                elif kind == "V":
                    ins = V.tensor_tensor(v_lo[par][:, n, :, :].rearrange("p n a d -> p (n a d)"), src,
                                          v_hi[par][:, n, :, :].rearrange("p n a d -> p (n a d)").bitcast(F32), ALU.subtract)
                elif kind == "T":
                    ins = V.tensor_tensor(pT_lo[:, half, :, :].rearrange("p c q -> p (c q)"), src,
                                          pT_hi[:, half, :, :].rearrange("p c q -> p (c q)").bitcast(F32), ALU.subtract)
                else:
                    ins = V.tensor_tensor(oT_lo[:, s], src, oT_hi[:, s].bitcast(F32), ALU.subtract)
                ins.then_inc(lo_done, 1)

            def add_attention(g):
                for n in range(g * GN, (g + 1) * GN):
                    dve.wait_ge(y2_filled, n // 2 + 1)
                    V.scalar_tensor_tensor(xr[:, n, :], ps[:, 4 + n // 2, (n % 2) * D:(n % 2 + 1) * D], tg[:, 1:2],
                                           xr[:, n, :], ALU.mult, ALU.add).then_inc(y2_taken, 1)
                    if n % GN:
                        dve.wait_ge(y2_taken, n)
                        stats(n - 1)
                dve.wait_ge(y2_taken, (g + 1) * GN)
                return stats((g + 1) * GN - 1)

            def take_max(i, u, bank, at=None):
                dve.wait_ge(unit_filled, filled(i, u, at))
                V.tensor_reduce(nmax[:, int(u[1]), :], ps[:, bank, :].rearrange("p (t k) -> p t k", t=2), AX.X, ALU.max,
                                negate=True).then_inc(max_done, 1)

            def invert_sum(i, b):
                dve.wait_ge(exp_done, i * NB + b + 1)
                V.reciprocal(rsum[:, b, :], esum[:, b, :]).then_inc(rsum_done, 1)

            def attend(i, j, at=None):
                units, bank = ring_of(at), banks_of(at)
                for u in [v for v in units if v[0] == "S"] + [v for v in units if v[0] != "S"]:
                    if u[0] == "S":
                        take_max(i, u, bank[u], at)
                    else:
                        if (u, at) == ("O1", NH - 1):
                            add_attention(0)
                        name, slot = place(u, j)
                        low_part(name, bank[u], slot, split(i, u, at))
                    for b in {"S1": [0], "S2": [1, 2], "K0": [3], "T0": [] if "K0" in units else [3]}.get(u, []):
                        invert_sum(i, b)

            def attend_first(units):
                for u in units:
                    if u[0] == "r":
                        invert_sum(0, int(u[1]))
                    elif u[0] == "S":
                        take_max(0, u, BANK0[u], 0)
                    else:
                        name, slot = place(u, 0)
                        low_part(name, BANK0[u], slot, split(0, u, 0))

            for n in range(GN):
                add_experts([n], n - 1 if n else None)
            dve.wait_ge(y0_taken, GN)
            own(norm(0, GN - 1))
            quantise(0)
            add_experts([GN])
            add_experts([GN + 1, GN + 2], GN)
            add_experts([GN + 3], GN + 1)
            dve.wait_ge(y0_taken, NT)
            for i in range(NT + 3):
                if i == NT:
                    factors(0, GN)
                    scaled(0).then_inc(h_ready, 1)
                if i == NT + 2:
                    attend_first(["K1"])
                if i < NT:
                    b = pair_of["U", i]
                    dve.wait_ge(silu_done, i + 1)
                    dve.wait_ge(up_values_filled, i + 1)
                    V.tensor_tensor(inner[:, i % 2, :], inner[:, i % 2, :], ps[:, b:b + 2, :].rearrange("p a n -> p (a n)"),
                                    ALU.mult).then_inc(inner_done, 1)
                if i == 0:
                    own(norm(1, 2))
                if i == 1:
                    quantise(1)
                if 0 <= i - 2 < NT:
                    n = i - 2
                    b, a = pair_of["H", n], am2[:, n % 2, :]
                    dve.wait_ge(had_filled, n + 1)
                    own(V.tensor_reduce(a[:, 0:1], ps[:, b:b + 2, :], AX.XY, ALU.max, apply_absolute_value=True))
                    own(V.tensor_scalar(a[:, 1:2], a[:, 0:1], c_up[:, n:n + 1], Q_EPS, ALU.mult, ALU.max))
                    own(V.reciprocal(a[:, 0:1], a[:, 1:2]))
                    V.tensor_scalar(a[:, 2:3], a[:, 0:1], 128.0, c_up[:, n:n + 1], ALU.mult, ALU.mult).then_inc(s2_ready, 1)
                    V.tensor_scalar(a[:, 3:4], a[:, 1:2], fdown[:, 0:1], None, ALU.mult)
                if 0 <= i - 1 < NT:
                    n = i - 1
                    b = pair_of["F", n]
                    dve.wait_ge(fT_hi_done, n + 1)
                    V.tensor_tensor(fT_lo[:, :, :].rearrange("p c t -> p (c t)"), ps[:, b:b + 2, :].rearrange("p a n -> p (a n)"),
                                    fT_hi[:, :, :].rearrange("p c t -> p (c t)").bitcast(F32), ALU.subtract).then_inc(fT_done, 1)
                if 0 <= i - 3 < NT:
                    n = i - 3
                    dve.wait_ge(y1_filled, n + 1)
                    dve.wait_ge(dve_step, steps[0])
                    V.scalar_tensor_tensor(xr[:, n, :], ps[:, pair_of["C", n], 0:D], am2[:, n % 2, 3:4], xr[:, n, :],
                                           ALU.mult, ALU.add).then_inc(y1_taken, 1)
                if 0 <= i - 2 < NT:
                    dve.wait_ge(q2_done, i - 1)
                    V.tensor_scalar(q2[:, :], q2[:, :], ROUND + 127.0, ROUND - 128.0, ALU.min, ALU.max).then_inc(q2_clipped, 1)
                if 0 <= i - 3 < NT:
                    dve.wait_ge(y1_taken, i - 2)
                    last = stats(i - 3)
                if i == NT + 2:
                    own(last)
                    factors(GN, NT)
                    scaled(1).then_inc(h_ready, 1)
                for u, n in AFTER.get(i, []):
                    if u == "N":
                        if n == 1:
                            attend_first(["S0", "V0", "V1"])
                        norm_lo(1, n, pair_of["N", n])
                    elif u == "X":
                        if n == 0:
                            attend_first(["K0"])
                    else:
                        for m in FIRST_OF[n]:
                            low_part(FIRST[m], first_bank[m], 0, m + 1)

            attend_first(["S1", "r0", "r1", "Z0", "T0", "T1", "S2", "S3", "r2", "Q0", "r3"] + REST[REST.index("T2"):])
            for j in range(1, 4):
                attend(j, j)
            with dve.Fori(1, LOOPED // 4) as i:
                for j in range(4):
                    attend(i * 4 + j, j)
            for j in range(4):
                attend(LOOPED + j, j, LOOPED + j)

            def split_latent(g):
                dve.wait_ge(xl_hi_done, g + 1)
                V.tensor_tensor(xl_lo[:, g * GT:(g + 1) * GT], ps[:, 3, :], xl_hi[:, g * GT:(g + 1) * GT].bitcast(F32),
                                ALU.subtract).then_inc(xl_done, 1)

            dve.wait_ge(lo_done, split(NH - 1, "O1", NH - 1))
            factors(0, GN)
            scaled(0).then_inc(h_ready, 1)
            add_attention(1)
            norm_lo(2, 0, 0)
            dve.wait_ge(hT_done, 2 * NG + 1)
            factors(GN, NT)
            scaled(1).then_inc(h_ready, 1)
            split_latent(0)
            norm_lo(2, 1, 6)

            dve.wait_ge(sc_done, 1)
            dve.wait_ge(ld_small, 64)
            own(V.tensor_tensor(sbias[:, :, :], sc[:, :, :],
                                gbias[:, :].unsqueeze(1).to_broadcast([P, NT, E]), ALU.add))
            for n in range(NT):
                for q in range(NGRP):
                    last = V.max(gtop[:, n * NGRP + q, :], sbias[:, n, q * EG:(q + 1) * EG])
            own(last)
            own(V.tensor_tensor(gscore[:, :, :].rearrange("p n q -> p (n q)"), gtop[:, :, 0], gtop[:, :, 1], ALU.add))
            other = gscore[:, :, :].unsqueeze(2).to_broadcast([P, NT, NGRP, NGRP])
            own_score = gscore[:, :, :].unsqueeze(3).to_broadcast([P, NT, NGRP, NGRP])
            dve.wait_ge(set_up, 4)
            V.tensor_tensor(cmp[:, :, :, :], other, own_score, ALU.is_gt)
            own(V.tensor_tensor(eqs[:, :, :, :], other, own_score, ALU.is_equal))
            own(V.tensor_tensor(eqs[:, :, :, :], eqs[:, :, :, :],
                                before[:, :, :].unsqueeze(1).to_broadcast([P, NT, NGRP, NGRP]), ALU.mult))
            own(V.tensor_tensor(cmp[:, :, :, :], cmp[:, :, :, :], eqs[:, :, :, :], ALU.add))
            own(V.tensor_reduce(grank[:, :, :], cmp[:, :, :, :], AX.X, ALU.add))
            split_latent(1)
            V.memset(masked[:, :, :], -3.0e38)
            own(V.tensor_scalar(gmask[:, :, :], grank[:, :, :], float(TOPG), None, ALU.is_lt))
            own(V.tensor_copy(gmask8[:, :, :].rearrange("p n (q k) -> p (n q) k", k=EG),
                              gmask[:, :, :].rearrange("p n q -> p (n q)").unsqueeze(2).to_broadcast([P, NT * NGRP, EG])))
            own(V.copy_predicated(masked[:, :, :], gmask8[:, :, :], sbias[:, :, :]))
            for n in range(NT):
                last = V.max(top8[:, n, :], masked[:, n, :])
            own(last)
            for n in range(NT):
                last = V.match_replace(left[:, n, :], top8[:, n, :], masked[:, n, :], -3.4e38)
            own(last)
            own(V.tensor_tensor(sel[:, :, :], masked[:, :, :], left[:, :, :], ALU.not_equal))
            own(V.tensor_tensor(wsel[:, :, :], sel[:, :, :], sc[:, :, :], ALU.mult))
            own(V.tensor_reduce(wden[:, :], wsel[:, :, :], AX.X, ALU.add))
            own(V.reciprocal(wden[:, :], wden[:, :]))
            own(V.tensor_scalar(wden[:, :], wden[:, :], ROUTED_SCALE, None, ALU.mult))
            V.tensor_tensor(cw[:, :, :], wsel[:, :, :], wden[:, :].unsqueeze(2).to_broadcast([P, NT, E]), ALU.mult)\
                .then_inc(cw_ready, 1)

            for n in range(NT):
                dve.wait_ge(y3_filled, n // 2 + 1)
                V.scalar_tensor_tensor(xr[:, n, :], ps[:, Y3_BANK[n // 2], (n % 2) * D:(n % 2 + 1) * D], tg[:, 3:4], xr[:, n, :],
                                       ALU.mult, ALU.add).then_inc(y3_taken, 1)

            def expert(e, j, landed, first):
                up = ps[:, 4 + 2 * (j % 2):6 + 2 * (j % 2), :].rearrange("p b t -> p (b t)")
                dve.wait_ge(relu_done, e + (j + 1))
                dve.wait_ge(ld_cw[j], landed)
                V.scalar_tensor_tensor(e_wa[j % 2][:, :], up, 0.0, cw_row[j][:, :], ALU.max, ALU.mult).then_inc(wa_done, 1)
                dve.wait_ge(wa_done, e + (j + 1))
                if not (first and j < 2):
                    dve.wait_ge(down_done, e + (j - 1))
                V.tensor_tensor(e_z[j % 2][:, :], e_wa[j % 2][:, :], e_relu[j % 2][:, :], ALU.mult).then_inc(e_z_done, 1)

            for j in range(4):
                expert(0, j, 16, True)
            with dve.Fori(1, E // 4) as i:
                for j in range(4):
                    expert(i * 4, j, i * 16 + 16, False)
            dve.wait_ge(y3_taken, NT)
            for n in range(NT):
                dve.wait_ge(y4_filled, n // 2 + 1)
                V.scalar_tensor_tensor(xr[:, n, :], ps[:, 4 + n // 2, (n % 2) * D:(n % 2 + 1) * D], tg[:, 3:4], xr[:, n, :],
                                       ALU.mult, ALU.add).then_inc(y4_taken, 1)

        @block.tensor
        def _(pe):
            mm = nc.tensor.matmul

            def product(dst, lhs, rhs, first=True, last=True, check=True):
                (l_hi, l_lo), (r_hi, r_lo) = lhs, rhs
                kw = {} if check else {"skip_group_check": True}
                mm(dst, l_lo, r_hi, start=first, stop=False, **kw)
                mm(dst, l_hi, r_lo, start=False, stop=False, **kw)
                return mm(dst, l_hi, r_hi, start=False, stop=last, **kw)

            def both(hi, lo, *at):
                return hi[at], lo[at]

            A = slice(None)

            def transpose_norm(k, g, bank):
                pe.wait_ge(h_ready, k * NG + g + 1)
                for c in range(DC):
                    for j in range(GN):
                        last = nc.tensor.transpose(ps[:, bank + c, j * P:(j + 1) * P], h[:, g * GN + j, c * P:(c + 1) * P], ident)
                last.then_inc(hT_filled, 1)

            def unit(u, bank, par, j=0):
                kind, half = u[0], int(u[1])
                dst = ps[:, bank, :]
                s = slice(half * GT, (half + 1) * GT)
                if kind in "QK":
                    w = "QK".index(kind)
                    src = (hT_hi, hT_lo) if kind == "Q" else (cT_hi, cT_lo)
                    for c in range(DC):
                        last = product(dst, both(wqk_hi[par], wqk_lo[par], A, w, c, A), both(*src, A, c, s), c == 0, c == DC - 1)
                elif kind == "V":
                    for n in range(2):
                        t = half * 2 + n
                        for c in range(DC):
                            last = product(dst[:, n * 2 * P:(n + 1) * 2 * P], both(cT_hi, cT_lo, A, c, slice(t * P, (t + 1) * P)),
                                           both(wv_hi, wv_lo, A, c, A), c == 0, c == DC - 1)
                elif kind == "S":
                    for t in range(2):
                        q0 = half * S + t * P
                        last = product(dst[:, t * S:(t + 1) * S], both(qT_hi[par], qT_lo[par], A, slice(q0, q0 + P)),
                                       both(kT_hi[par], kT_lo[par], A, slice(half * S, (half + 1) * S)))
                elif kind == "T":
                    for k in range(2):
                        for t in range(2):
                            last = nc.tensor.transpose(dst[:, k * S + t * P:k * S + (t + 1) * P],
                                                       probs[:, half, t, k * P:(k + 1) * P], ident)
                else:
                    pair = j // 2
                    for b in (2 * half, 2 * half + 1):
                        for k in range(2):
                            last = product(dst[:, (b % 2) * S:(b % 2 + 1) * S], both(v_hi[pair], v_lo[pair], A, 2 * b + k, par, A),
                                           both(pT_hi, pT_lo, A, b, k, A), k == 0, k == 1)
                last.then_inc(unit_filled, 1)

            w_gate = wq8[0][:, :].rearrange("p (c n) -> p c n", c=DC)
            w_up = wq8[1][:, :].rearrange("p (c n) -> p c n", c=DC)
            w_down = wq8[2][:, :].rearrange("p (c n) -> p c n", c=IC)

            freed = {"Q": q1T_done, "G": silu_done, "U": inner_done, "C": y1_taken, "H": q2_done, "F": fT_done,
                     "A": lo_done, "N": hT_done}

            def wait_freed(user):
                done = user[1] + 1
                if user[0] == "A":
                    done = FIRST_OF[user[1]][-1] + 1
                elif user[0] == "N":
                    done += NG
                pe.wait_ge(freed[user[0]], done)

            def fill(u, n):
                if u != "D":
                    b, user = pair_of[u, n], user_before[u, n]
                    if user:
                        wait_freed(user)
                    else:
                        pe.wait_ge(a_taken, (NB - 1) * NG)
                        if b in Y0_PAIR:
                            pe.wait_ge(y0_taken, NT - Y0_PAIR[::-1].index(b))
                if u == "Q":
                    pe.wait_ge(q1_ready, n + 1)
                    for c in range(DC):
                        for j in range(GN):
                            last = nc.tensor.transpose(ps[:, b + c, j * P:(j + 1) * P], qtok[:, j, c * P:(c + 1) * P], ident)
                    last.then_inc(q1T_filled, 1)
                elif u in "GU":
                    pe.wait_ge(q1T_done, n // GN + 1)
                    pe.wait_ge(scales_ready, n // GN + 1)
                    pe.wait_ge(w_ternary, 1 if u == "G" else 2)
                    w = w_gate if u == "G" else w_up
                    for half in range(2):
                        for d in range(DC):
                            last = mm(ps[:, b + half, :], qT[:, n // GN, d, n % GN * P:(n % GN + 1) * P],
                                      w[:, d, half * 512:(half + 1) * 512], start=(d == 0), stop=(d == DC - 1))
                    last.then_inc(gate_filled if u == "G" else up_values_filled, 1)
                elif u == "F":
                    pe.wait_ge(fly_done, n + 1)
                    for c in range(IC):
                        last = nc.tensor.transpose(ps[:, b + c // 4, (c % 4) * P:(c % 4 + 1) * P], inner[:, n % 2, c * P:(c + 1) * P], ident)
                    last.then_inc(fT_filled, 1)
                elif u == "H":
                    pe.wait_ge(fT_done, n + 1)
                    pe.wait_ge(had_copied, 1)
                    for k in range(IC // 2):
                        dst = ps[:, b + k // 2, (k % 2) * 2 * P:(k % 2 + 1) * 2 * P]
                        for m, part in enumerate((fT_lo, fT_hi)):
                            for a in range(2):
                                last = mm(dst, part[:, 2 * k + a, :], had[:, a, :], start=(m + a == 0), stop=(m + a == 2))
                    last.then_inc(had_filled, 1)
                elif u == "N":
                    transpose_norm(1, n, b)
                elif u == "A":
                    pe.wait_ge(qk_split, 1)
                    pe.wait_ge(wv_split, 1)
                    if n >= 3:
                        pe.wait_ge(hT_done, NG + n - 2)
                    for m in FIRST_OF[n]:
                        unit(FIRST[m], first_bank[m], 0)
                elif u == "C":
                    pe.wait_ge(q2_clipped, n + 1)
                    for c in range(IC):
                        last = nc.tensor.transpose(ps[:, b + c // 4, (c % 4) * P:(c % 4 + 1) * P], q2[:, c * P:(c + 1) * P], ident)
                    last.then_inc(q2T_filled, 1)
                else:
                    pe.wait_ge(q2T_done, n + 1)
                    pe.wait_ge(w_ternary, 3)
                    for c in range(IC):
                        last = mm(ps[:, pair_of["C", n], 0:D], q2T[:, c, :], w_down[:, c, :], start=(c == 0), stop=(c == IC - 1))
                    last.then_inc(y1_filled, 1)

            pe.wait_ge(ld_const, 16)
            transpose_norm(0, 0, 0)
            pe.wait_ge(ctx_done, 1)
            for g in range(NG):
                pe.wait_ge(hT_done, g + 1)
                for e in range(NB):
                    if e >= 2 or g:
                        before_e = (e - 2) % NB
                        before_g = g if e >= 2 else g - 1
                        if before_e == 0:
                            pe.wait_ge(a_first_copied, before_g + 1)
                        else:
                            pe.wait_ge(a_taken, (NB - 1) * before_g + before_e)
                    for f in range(DC):
                        for c in range(DC):
                            last = product(ps[:, 2 + 2 * (e % 2) + f, :],
                                           both(cT_hi, cT_lo, A, c, slice(e * S + f * P, e * S + (f + 1) * P)),
                                           both(hT_hi, hT_lo, A, c, slice(g * GT, (g + 1) * GT)), c == 0, c == DC - 1)
                    last.then_inc(a_filled, 1)
                    if g == 0 and e == 1:
                        transpose_norm(0, 1, 0)
                    if g == 0 and e == 2:
                        pe.wait_ge(set_up, 2)
                        pe.wait_ge(wsum_done, 1)
                        mm(ps[:, 7, 0:3], ones[:, :], wsum[:, :], start=True, stop=True).then_inc(wtot_filled, 1)
            for g in range(NG):
                pe.wait_ge(z_done, g + 1)
                for n in range(g * GN, (g + 1) * GN):
                    if n == NT - 1:
                        fill("Q", 0)
                    if n == 0:
                        pe.wait_ge(wscale_done, 1)
                    elif n == 2:
                        pe.wait_ge(a_taken, (NB - 1) * NG)
                    elif n >= 3:
                        pe.wait_ge(y0_taken, n - 2)
                    for b in range(2):
                        for c in range(DC):
                            last = product(ps[:, Y0_PAIR[n] + b, :],
                                           both(z_hi, z_lo, A, g, c, slice((n - g * GN) * P, (n - g * GN + 1) * P)),
                                           both(cT_hi, cT_lo, A, c, slice(b * 2 * S, (b + 1) * 2 * S)), c == 0, c == DC - 1)
                    last.then_inc(y0_filled, 1)

            def add_head(half, par, o_split, w_split, final=False):
                pe.wait_ge(wo_split, w_split)
                pe.wait_ge(lo_done, o_split)
                for n in range(half * GN, (half + 1) * GN):
                    last = product(ps[:, 4 + n // 2, (n % 2) * D:(n % 2 + 1) * D],
                                   both(oT_hi, oT_lo, A, slice(n * P, (n + 1) * P)), (wo_hi[par][:, :], wo_lo[par][:, :]),
                                   False, final and n % 2 == 1, check=False)
                    if final and n % 2:
                        last.then_inc(y2_filled, 1)

            def attend(i, j, pair, at=None, order=None):
                units = ring_of(at)
                before_step = ring_of(at - 1 if at else None)
                bank, bank_before = banks_of(at), banks_of(at - 1 if at else None)
                for u in order or STEP:
                    if u[0] == "Y":
                        add_head(int(u[1]), 1 - j % 2, split_before(i, "O" + u[1], at), i)
                        continue
                    if u not in units:
                        continue
                    earlier = [v for v in units[:units.index(u)] if bank[v] == bank[u]]
                    if not earlier and at == 0:
                        wait_freed(last_user[bank[u] // 2 * 2])
                    elif not earlier:
                        pe.wait_ge(lo_done, split_before(i, [v for v in before_step if bank_before[v] == bank[u]][-1], at))
                    elif earlier[-1][0] == "S":
                        pe.wait_ge(exp_done, i * NB + int(earlier[-1][1]) + 1)
                    else:
                        pe.wait_ge(lo_done, split(i, earlier[-1], at))
                    if u in ("S0", "S2"):
                        if at == 0:
                            pe.wait_ge(lo_done, len(FIRST) if u == "S0" else split(0, "Z0", 0))
                        else:
                            pe.wait_ge(lo_done, split_before(i, "Q" + str(int(u[1]) // 2), at))
                    if u == "Z0":
                        pe.wait_ge(hT_done, 2 * NG)
                    if u == "K0":
                        pe.wait_ge(qk_split, i + 2)
                    if u == "V0":
                        pe.wait_ge(wv_split, pair + 2)
                    if u[0] == "T":
                        pe.wait_ge(probs_done, i * NB + int(u[1]) + 1)
                    if u[0] == "O":
                        pe.wait_ge(lo_done, split(i, "T" + str(2 * int(u[1]) + 1), at))
                    name, slot = place(u, j)
                    unit(name, bank[u], slot, j)

            for u, n in FFN[1:]:
                if u == "X":
                    attend(0, 0, 0, 0, STARTS[n])
                else:
                    fill(u, n)

            attend(0, 0, 0, 0, REST)
            pe.wait_ge(y1_taken, NT)
            pe.wait_ge(hT_done, 2 * NG)
            for b in range(4):
                mm(ps[:, 4 + b, :], zeros[:, 0:P], zeros[:, :], start=True, stop=False, skip_group_check=True)
            for j in range(1, 4):
                attend(j, j, j // 2, j)
            with pe.Fori(1, LOOPED // 4) as i:
                for j in range(4):
                    attend(i * 4 + j, j, i * 2 + j // 2)
            for j in range(3):
                attend(LOOPED + j, j, (LOOPED + j) // 2, LOOPED + j)
            last_step = (NH - 1, 3, NH // 2 - 1, NH - 1)
            attend(*last_step, ["S0", "S1", "Y0", "S2", "S3", "T0", "T1", "Y1", "O0", "T2", "T3"])
            add_head(0, 1, split(NH - 1, "O0", NH - 1), NH, final=True)
            attend(*last_step, ["O1"])
            add_head(1, 1, split(NH - 1, "O1", NH - 1), NH, final=True)

            pe.wait_ge(lo_done, split(NH - 1, "O1", NH - 1))
            pe.wait_ge(small_split, 1)
            for u, n in FRONT:
                s = slice(n * GT, (n + 1) * GT)
                if u == "N":
                    if n:
                        pe.wait_ge(y2_taken, NT)
                    transpose_norm(2, n, N_BANK[n])
                elif u == "L":
                    pe.wait_ge(hT_done, 2 * NG + n + 1)
                    if n:
                        pe.wait_ge(scT_done, n)
                    for c in range(DC):
                        last = product(ps[0:E, 2, :], both(gw_hi, gw_lo, A, c, A), both(hT_hi, hT_lo, A, c, s), c == 0, c == DC - 1)
                    last.then_inc(logit_filled, 1)
                elif u == "X":
                    if n:
                        pe.wait_ge(xl_done, n)
                    for c in range(DC):
                        last = product(ps[:, 3, :], both(fc1_hi, fc1_lo, A, c, A), both(hT_hi, hT_lo, A, c, s), c == 0, c == DC - 1)
                    last.then_inc(xl_filled, 1)
                elif u == "B":
                    pe.wait_ge(scT_done, NG)
                    for t in range(NT):
                        last = nc.tensor.transpose(ps[:, 2, t * E:(t + 1) * E], scT[:, t * P:(t + 1) * P], ident[0:E, 0:E])
                    last.then_inc(scT_back, 1)
                else:
                    g, m = n // SC, n % SC
                    if g:
                        pe.wait_ge(su_taken, n - SC + 1)
                    elif m < 2:
                        pe.wait_ge(y2_taken, GN)
                    pe.wait_ge(su_split, 1)
                    for c in range(DC):
                        last = product(ps[:, U_BANK[m], :], both(su_hi, su_lo, A, c, slice(m * P, (m + 1) * P)),
                                       both(hT_hi, hT_lo, A, c, slice(g * GT, (g + 1) * GT)), c == 0, c == DC - 1)
                    last.then_inc(su_filled, 1)
            pe.wait_ge(hT_done, 3 * NG)
            for n in range(NT):
                if n % GN == 0:
                    pe.wait_ge(sd_split, 1)
                    pe.wait_ge(s_done, SC * (n // GN + 1))
                if n == 4:
                    pe.wait_ge(xl_done, NG)
                if n == 6:
                    pe.wait_ge(cwT_done, 1)
                for c in range(SC):
                    last = product(ps[:, Y3_BANK[n // 2], (n % 2) * D:(n % 2 + 1) * D],
                                   both(s_hi, s_lo, A, c, slice(n * P, (n + 1) * P)), both(sd_hi, sd_lo, A, c, A), c == 0, c == SC - 1)
                if n % 2:
                    last.then_inc(y3_filled, 1)
                if n == 3:
                    pe.wait_ge(cw_ready, 1)
                    pe.wait_ge(sc_done, 1)
                    for q in range(NG):
                        last = nc.tensor.transpose(ps[:, 2, q * P:(q + 1) * P],
                                                   cw[:, q * GN:(q + 1) * GN, :].rearrange("p n e -> p (n e)"), ident)
                    last.then_inc(cwT_filled, 1)

            def up(e, j, split_count, free):
                pe.wait_ge(w1_split, split_count)
                if free:
                    pe.wait_ge(wa_done, e + (j - 1))
                    pe.wait_ge(relu_done, e + (j - 1))
                w = both(w1_hi[j // 2 % 2], w1_lo[j // 2 % 2], A, j % 2, A)
                for t in range(2):
                    last = product(ps[:, 4 + 2 * (j % 2) + t, :], w, both(xl_hi, xl_lo, A, slice(t * 512, (t + 1) * 512)))
                last.then_inc(up_filled, 1)

            def experts(e, i, final):
                for j in range(4):
                    if not (final and j >= 2):
                        up(e, j + 2, i * 2 + ((j + 2) // 2 + 1), True)
                    pe.wait_ge(e_z_done, e + (j + 1))
                    pe.wait_ge(ld_w2[j // 2], i * 16 + 16)
                    mm(ps[:, 1, :], w2_raw[j // 2][:, j % 2, :], e_z[j % 2][:, GT:T],
                       start=False, stop=final and j == 3, skip_group_check=True)
                    pe.wait_ge(w2_split, i * 2 + (j // 2 + 1))
                    pe.wait_ge(half_lo_done, e + (j + 1))
                    last = product(ps[:, 0, :], both(w2_hi[j // 2], w2_lo[j // 2], A, j % 2, A),
                                   (z_half_hi[j % 2][:, :], z_half_lo[j % 2][:, :]), False, final and j == 3, check=False)
                    last.then_inc(down_done, 1)

            pe.wait_ge(su_taken, NG * SC)
            up(0, 0, 1, False)
            pe.wait_ge(y3_taken, 4)
            up(0, 1, 1, False)
            for b in range(2):
                mm(ps[:, b, :], zeros[:, 0:P], zeros[:, :], start=True, stop=False, skip_group_check=True)
            with pe.Fori(0, E // 4 - 1) as i:
                experts(i * 4, i, False)
            experts(E - 4, E // 4 - 1, True)
            pe.wait_ge(yl_done, 1)
            for n in range(NT):
                last = mm(ps[:, 4 + n // 2, (n % 2) * D:(n % 2 + 1) * D], yl[:, n * P:(n + 1) * P], fc2[:, :], start=True, stop=True)
                if n % 2:
                    last.then_inc(y4_filled, 1)


def kernel(**inputs):
    import numpy as np
    import concourse.bacc as bacc
    from concourse.bass_utils import run_bass_kernel_spmd

    a = {k: np.asarray(v) for k, v in inputs.items()}
    B, S, D = a["x"].shape
    T, P = B * S, 128
    heads = a["L1_xattn_Wq"].shape[1] // P

    def head_columns(w):
        return w.reshape(D // P, P, heads, P).transpose(2, 1, 0, 3)

    had = np.ones((1, 1), np.float32)
    while had.shape[0] < P:
        had = np.block([[had, had], [had, -had]])
    inner = a["L0_ffn_w_gate"].shape[0]
    arrays = {
        "x": a["x"].reshape(T, D),
        "ids": a["itok_BxS_13_99985"].reshape(T),
        "ctx_t": a["ctx_2048"].transpose(2, 0, 1).reshape(D, T),
        "g_xattn": a["g_xattn"],
        "g_ffn": a["g_ffn"],
        "w_gate_t": a["L0_ffn_w_gate"].T,
        "w_up_t": a["L0_ffn_w_up"].T,
        "w_down_t": a["L0_ffn_w_down"].T,
        "w_qk": np.stack([head_columns(a["L1_xattn_" + n]) for n in ("Wq", "Wk")], axis=2),
        "w_v": a["L1_xattn_Wv"].reshape(D // P, P, heads // 2, 2 * P).transpose(2, 1, 0, 3),
        "w_o": a["L1_xattn_Wo"].reshape(heads, P, D),
        "gate_w_t": a["L1_ffn_gate_w"].T,
        "gate_bias": a["L1_ffn_gate_bias"],
        "fc1_t": a["L1_ffn_fc1_w"].T,
        "fc2_t": a["L1_ffn_fc2_w"].T,
        "w1_t": a["L1_ffn_w1"].transpose(0, 2, 1),
        "w2_t": a["L1_ffn_w2"].transpose(0, 2, 1),
        "shared_up_t": a["L1_ffn_shared_up_w"].T,
        "shared_down_t": a["L1_ffn_shared_down_w"].T,
        "consts": np.stack([np.eye(P, dtype=np.float32)] + [had * np.float32(f / np.sqrt(inner)) for f in (1, 1, 1, -1)], axis=1),
    }
    arrays = {f"in_{k}": np.ascontiguousarray(v) for k, v in arrays.items()}
    nc = bacc.Bacc("TRN2", target_bir_lowering=False, num_devices=1)
    args = [nc.dram_tensor(k, v.shape, mybir.dt.from_np(v.dtype), kind="ExternalInput").ap() for k, v in arrays.items()]
    experts = a["L1_ffn_gate_w"].shape[0]
    scratch = nc.dram_tensor("cw_scratch", (experts, T), mybir.dt.float32, kind="Internal").ap()
    out = nc.dram_tensor("out", (T, D), mybir.dt.float32, kind="ExternalOutput").ap()
    flamingo_two_layer_kernel(nc, *args, scratch, out, B)
    r = run_bass_kernel_spmd(nc, [arrays], core_ids=[0])
    return r.results[0]["out"].reshape(B, S, D)
```
